# Optimizing a Trainium2 kernel written in Bass

```python
import numpy as np
import jax
import jax.numpy as jnp

def _softmax(x, axis=-1):
    return jax.nn.softmax(x, axis=axis)

def _gelu(x):
    return jax.nn.gelu(x, approximate=True)

def _silu(x):
    return jax.nn.silu(x)

def _sigmoid(x):
    return jax.nn.sigmoid(x)

def _layernorm(x, axis=-1, eps=1e-05):
    m = jnp.mean(x, axis=axis, keepdims=True)
    v = jnp.var(x, axis=axis, keepdims=True)
    return (x - m) / jnp.sqrt(v + eps)

def _scatter_add(tgt, idx, src, axis=0):
    return tgt.at[idx].add(src)

def _segment_sum(src, seg, n):
    return jax.ops.segment_sum(src, seg, n)
kernel_name = 'mk_early_fusion_d2_tok_img256_r4_d39236'

def setup_inputs(seed: int=0):
    np.random.seed(seed)
    _w = jnp.asarray

    def _rec_inputs():
        import jax
        import jax.numpy as jnp
        _rk = jax.random.key(seed)
        x = -0.000596345 + 1.00056 * jax.random.normal(jax.random.fold_in(_rk, 1), (64, 64, 64, 3), jnp.float32)
        txt = -0.093804 + 0.29155 * jax.random.normal(jax.random.fold_in(_rk, 2), (64, 77, 64), jnp.float32)
        return (x, txt)
    x, txt = _rec_inputs()

    def _L0_tok_setup():
        import jax, jax.numpy as jnp
        import numpy as np
        B, H, W = (16, 64, 64)
        WIDTH, LAYERS, M1, M2 = (32, 4, 12, 12)
        EPS = 1e-05

        def layer_norm(x, g, b):
            mu = jnp.mean(x, axis=-1, keepdims=True)
            var = jnp.mean((x - mu) ** 2, axis=-1, keepdims=True)
            return (x - mu) * jax.lax.rsqrt(var + EPS) * g + b

        def gelu(x):
            return jax.nn.gelu(x, approximate=False)

        def spectral_conv(x, w1, w2):
            b, c, h, w = x.shape
            x_ft = jnp.fft.rfft2(x)
            out_ft = jnp.zeros((b, w1.shape[1], h, w // 2 + 1), dtype=x_ft.dtype)
            out_ft = out_ft.at[:, :, :M1, :M2].set(jnp.einsum('bixy,ioxy->boxy', x_ft[:, :, :M1, :M2], w1))
            out_ft = out_ft.at[:, :, -M1:, :M2].set(jnp.einsum('bixy,ioxy->boxy', x_ft[:, :, -M1:, :M2], w2))
            return jnp.fft.irfft2(out_ft, s=(h, w))
        key = jax.random.key(seed)
        ks = jax.random.split(key, 16)
        scale = 1.0 / (WIDTH * WIDTH)
        d = {'x': jax.random.normal(ks[0], (B, H, W, 3), jnp.float32), 'fc0_w': jax.random.normal(ks[1], (3, WIDTH), jnp.float32) * 0.5, 'fc0_b': jnp.zeros((WIDTH,), jnp.float32), 'ln0_g': jnp.ones((WIDTH,), jnp.float32), 'ln0_b': jnp.zeros((WIDTH,), jnp.float32), 'w1r': jax.random.uniform(ks[2], (LAYERS, WIDTH, WIDTH, M1, M2), jnp.float32) * scale, 'w1i': jax.random.uniform(ks[3], (LAYERS, WIDTH, WIDTH, M1, M2), jnp.float32) * scale, 'w2r': jax.random.uniform(ks[4], (LAYERS, WIDTH, WIDTH, M1, M2), jnp.float32) * scale, 'w2i': jax.random.uniform(ks[5], (LAYERS, WIDTH, WIDTH, M1, M2), jnp.float32) * scale, 'conv_w': jax.random.normal(ks[6], (LAYERS, WIDTH, WIDTH), jnp.float32) * (1.0 / np.sqrt(WIDTH)), 'conv_b': jnp.zeros((LAYERS, WIDTH), jnp.float32), 'ln_g': jnp.ones((LAYERS, WIDTH), jnp.float32), 'ln_b': jnp.zeros((LAYERS, WIDTH), jnp.float32), 'fc1_w': jax.random.normal(ks[7], (WIDTH, 128), jnp.float32) * (1.0 / np.sqrt(WIDTH)), 'fc1_b': jnp.zeros((128,), jnp.float32), 'fc2_w': jax.random.normal(ks[8], (128, 64), jnp.float32) * (1.0 / np.sqrt(128)), 'fc2_b': jnp.zeros((64,), jnp.float32), 'fc3_w': jax.random.normal(ks[9], (64, 1), jnp.float32) * (1.0 / np.sqrt(64)), 'fc3_b': jnp.zeros((1,), jnp.float32)}
        return d
    _L0_tok_all = _L0_tok_setup()
    _L0_tok_in = {k: v for k, v in _L0_tok_all.items() if k in ('fc0_w', 'fc0_b', 'ln0_g', 'ln0_b', 'w1r', 'w1i', 'w2r', 'w2i', 'conv_w', 'conv_b', 'ln_g', 'ln_b', 'fc1_w', 'fc1_b', 'fc2_w', 'fc2_b', 'fc3_w', 'fc3_b')}
    del _L0_tok_all

    def _L0_attn_setup():
        import jax, jax.numpy as jnp
        import numpy as np
        TEMPERATURE = 1.0
        W_BLEND = 0.8
        EPS = 1e-12

        def _l2norm(x):
            n = jnp.sqrt(jnp.sum(x * x, axis=-1, keepdims=True))
            return x / jnp.maximum(n, EPS)
        key = jax.random.key(seed)
        feats = jax.random.normal(key, (4, 512, 64), dtype=jnp.float32)
        return {'feats': feats}
    _L0_attn_all = _L0_attn_setup()
    _L0_attn_in = {k: v for k, v in _L0_attn_all.items() if k in ()}
    del _L0_attn_all

    def _L0_ffn_setup():
        import jax, jax.numpy as jnp
        import numpy as np
        NUM_EXPERTS = 8
        TOP_K = 2
        B, S, D = (8, 2048, 64)

        def _moe(tokens, router_w, w1, b1, w2, b2):
            N = tokens.shape[0]
            E = router_w.shape[0]
            logits = tokens.astype(jnp.float32) @ router_w.astype(jnp.float32).T
            probs = jax.nn.softmax(logits, axis=-1)
            rw, re = jax.lax.top_k(probs, TOP_K)
            if TOP_K > 1:
                rw = rw / jnp.maximum(rw.sum(-1, keepdims=True), 1e-12)
            rw = rw.astype(tokens.dtype)
            combine = jnp.zeros((N, E), tokens.dtype).at[jnp.arange(N)[:, None], re].set(rw)
            out = tokens
            for e in range(E):
                h = jax.nn.gelu(tokens @ w1[e] + b1[e], approximate=False)
                y = h @ w2[e] + b2[e]
                out = out + combine[:, e:e + 1] * y
            return out
        key = jax.random.key(seed)
        ks = jax.random.split(key, 4)
        scale = 1.0 / np.sqrt(D).astype(np.float32)
        return {'input_embeddings': jax.random.normal(ks[0], (B, S, D), jnp.float32), 'router_w': jax.random.normal(ks[1], (NUM_EXPERTS, D), jnp.float32) * scale, 'w1': jax.random.normal(ks[2], (NUM_EXPERTS, D, D), jnp.float32) * scale, 'b1': jnp.zeros((NUM_EXPERTS, D), jnp.float32), 'w2': jax.random.normal(ks[3], (NUM_EXPERTS, D, D), jnp.float32) * scale, 'b2': jnp.zeros((NUM_EXPERTS, D), jnp.float32)}
    _L0_ffn_all = _L0_ffn_setup()
    _L0_ffn_in = {k: v for k, v in _L0_ffn_all.items() if k in ('router_w', 'w1', 'b1', 'w2', 'b2')}
    del _L0_ffn_all

    def _L1_attn_setup():
        import jax, jax.numpy as jnp
        import numpy as np
        DIM = 64
        HEADS = 4
        HEAD_DIM = DIM // HEADS
        SCALE = HEAD_DIM ** (-0.5)
        key = jax.random.key(seed)
        ks = jax.random.split(key, 9)
        B, N, C = (2, 1024, DIM)
        x = jax.random.normal(ks[0], (B, N, C), dtype=jnp.float32)
        lim = np.sqrt(6.0 / (C + C)).astype(np.float32)

        def w(k):
            return jax.random.uniform(k, (C, C), dtype=jnp.float32, minval=-lim, maxval=lim)
        return {'x': x, 'Wq': w(ks[1]), 'bq': jnp.zeros((C,), jnp.float32), 'Wk': w(ks[2]), 'bk': jnp.zeros((C,), jnp.float32), 'Wv': w(ks[3]), 'bv': jnp.zeros((C,), jnp.float32), 'Wo': w(ks[4]), 'bo': jnp.zeros((C,), jnp.float32)}
    _L1_attn_all = _L1_attn_setup()
    _L1_attn_in = {k: v for k, v in _L1_attn_all.items() if k in ('Wq', 'bq', 'Wk', 'bk', 'Wv', 'bv', 'Wo', 'bo')}
    del _L1_attn_all

    def _L1_ffn_setup():
        import math
        import jax, jax.numpy as jnp
        import numpy as np
        CAPACITY_FACTOR = 1.25
        key = jax.random.key(seed)
        ks = jax.random.split(key, 5)
        B, L, D, F, E = (8, 2048, 64, 256, 8)
        h = jax.random.normal(ks[0], (B, L, D), dtype=jnp.float32)
        gate_w = jax.random.normal(ks[1], (D, E), dtype=jnp.float32) * 0.02
        gate_b = jnp.zeros((E,), dtype=jnp.float32)
        w1 = jax.random.normal(ks[2], (E, D, F), dtype=jnp.float32) * (1.0 / math.sqrt(D))
        b1 = jnp.zeros((E, F), dtype=jnp.float32)
        w2 = jax.random.normal(ks[3], (E, F, D), dtype=jnp.float32) * (1.0 / math.sqrt(F))
        b2 = jnp.zeros((E, D), dtype=jnp.float32)
        return {'h': h, 'gate_w': gate_w, 'gate_b': gate_b, 'w1': w1, 'b1': b1, 'w2': w2, 'b2': b2}
    _L1_ffn_all = _L1_ffn_setup()
    _L1_ffn_in = {k: v for k, v in _L1_ffn_all.items() if k in ('gate_w', 'gate_b', 'w1', 'b1', 'w2', 'b2')}
    del _L1_ffn_all
    return {'x': x, 'txt': txt, 'L0_tok_fc0_w': _L0_tok_in['fc0_w'], 'L0_tok_fc0_b': _L0_tok_in['fc0_b'], 'L0_tok_ln0_g': _L0_tok_in['ln0_g'], 'L0_tok_ln0_b': _L0_tok_in['ln0_b'], 'L0_tok_w1r': _L0_tok_in['w1r'], 'L0_tok_w1i': _L0_tok_in['w1i'], 'L0_tok_w2r': _L0_tok_in['w2r'], 'L0_tok_w2i': _L0_tok_in['w2i'], 'L0_tok_conv_w': _L0_tok_in['conv_w'], 'L0_tok_conv_b': _L0_tok_in['conv_b'], 'L0_tok_ln_g': _L0_tok_in['ln_g'], 'L0_tok_ln_b': _L0_tok_in['ln_b'], 'L0_tok_fc1_w': _L0_tok_in['fc1_w'], 'L0_tok_fc1_b': _L0_tok_in['fc1_b'], 'L0_tok_fc2_w': _L0_tok_in['fc2_w'], 'L0_tok_fc2_b': _L0_tok_in['fc2_b'], 'L0_tok_fc3_w': _L0_tok_in['fc3_w'], 'L0_tok_fc3_b': _L0_tok_in['fc3_b'], 'L0_ffn_router_w': _L0_ffn_in['router_w'], 'L0_ffn_w1': _L0_ffn_in['w1'], 'L0_ffn_b1': _L0_ffn_in['b1'], 'L0_ffn_w2': _L0_ffn_in['w2'], 'L0_ffn_b2': _L0_ffn_in['b2'], 'L1_attn_Wq': _L1_attn_in['Wq'], 'L1_attn_bq': _L1_attn_in['bq'], 'L1_attn_Wk': _L1_attn_in['Wk'], 'L1_attn_bk': _L1_attn_in['bk'], 'L1_attn_Wv': _L1_attn_in['Wv'], 'L1_attn_bv': _L1_attn_in['bv'], 'L1_attn_Wo': _L1_attn_in['Wo'], 'L1_attn_bo': _L1_attn_in['bo'], 'L1_ffn_gate_w': _L1_ffn_in['gate_w'], 'L1_ffn_gate_b': _L1_ffn_in['gate_b'], 'L1_ffn_w1': _L1_ffn_in['w1'], 'L1_ffn_b1': _L1_ffn_in['b1'], 'L1_ffn_w2': _L1_ffn_in['w2'], 'L1_ffn_b2': _L1_ffn_in['b2']}

def reference(x, txt, L0_tok_fc0_w, L0_tok_fc0_b, L0_tok_ln0_g, L0_tok_ln0_b, L0_tok_w1r, L0_tok_w1i, L0_tok_w2r, L0_tok_w2i, L0_tok_conv_w, L0_tok_conv_b, L0_tok_ln_g, L0_tok_ln_b, L0_tok_fc1_w, L0_tok_fc1_b, L0_tok_fc2_w, L0_tok_fc2_b, L0_tok_fc3_w, L0_tok_fc3_b, L0_ffn_router_w, L0_ffn_w1, L0_ffn_b1, L0_ffn_w2, L0_ffn_b2, L1_attn_Wq, L1_attn_bq, L1_attn_Wk, L1_attn_bk, L1_attn_Wv, L1_attn_bv, L1_attn_Wo, L1_attn_bo, L1_ffn_gate_w, L1_ffn_gate_b, L1_ffn_w1, L1_ffn_b1, L1_ffn_w2, L1_ffn_b2):
    import jax
    import jax.numpy as jnp

    def _L0_tok_ref(x, fc0_w, fc0_b, ln0_g, ln0_b, w1r, w1i, w2r, w2i, conv_w, conv_b, ln_g, ln_b, fc1_w, fc1_b, fc2_w, fc2_b, fc3_w, fc3_b):
        import jax, jax.numpy as jnp
        import numpy as np
        B, H, W = (16, 64, 64)
        WIDTH, LAYERS, M1, M2 = (32, 4, 12, 12)
        EPS = 1e-05

        def layer_norm(x, g, b):
            mu = jnp.mean(x, axis=-1, keepdims=True)
            var = jnp.mean((x - mu) ** 2, axis=-1, keepdims=True)
            return (x - mu) * jax.lax.rsqrt(var + EPS) * g + b

        def gelu(x):
            return jax.nn.gelu(x, approximate=False)

        def spectral_conv(x, w1, w2):
            b, c, h, w = x.shape
            x_ft = jnp.fft.rfft2(x)
            out_ft = jnp.zeros((b, w1.shape[1], h, w // 2 + 1), dtype=x_ft.dtype)
            out_ft = out_ft.at[:, :, :M1, :M2].set(jnp.einsum('bixy,ioxy->boxy', x_ft[:, :, :M1, :M2], w1))
            out_ft = out_ft.at[:, :, -M1:, :M2].set(jnp.einsum('bixy,ioxy->boxy', x_ft[:, :, -M1:, :M2], w2))
            return jnp.fft.irfft2(out_ft, s=(h, w))
        h = layer_norm(x @ fc0_w + fc0_b, ln0_g, ln0_b)
        h = jnp.transpose(h, (0, 3, 1, 2))
        for i in range(LAYERS):
            w1 = w1r[i] + 1j * w1i[i]
            w2 = w2r[i] + 1j * w2i[i]
            x1 = spectral_conv(h, w1, w2)
            x2 = jnp.einsum('bchw,oc->bohw', h, conv_w[i]) + conv_b[i][None, :, None, None]
            h = x1 + x2
            h = jnp.transpose(h, (0, 2, 3, 1))
            h = layer_norm(h, ln_g[i], ln_b[i])
            if i < LAYERS - 1:
                h = gelu(h)
            h = jnp.transpose(h, (0, 3, 1, 2))
        h = jnp.transpose(h, (0, 2, 3, 1))
        h = gelu(h @ fc1_w + fc1_b)
        h = gelu(h @ fc2_w + fc2_b)
        h = h @ fc3_w + fc3_b
        return h[..., 0]

    def _L0_attn_ref(feats):
        import jax, jax.numpy as jnp
        import numpy as np
        TEMPERATURE = 1.0
        W_BLEND = 0.8
        EPS = 1e-12

        def _l2norm(x):
            n = jnp.sqrt(jnp.sum(x * x, axis=-1, keepdims=True))
            return x / jnp.maximum(n, EPS)
        B, N, C = feats.shape
        f = _l2norm(feats.reshape(B * N, C))
        scores = jnp.matmul(f, f.T) / TEMPERATURE
        attn = jax.nn.softmax(scores, axis=-1)
        feats_att = jnp.matmul(attn, f)
        feats_fcm = f * W_BLEND + feats_att * (1.0 - W_BLEND)
        return _l2norm(feats_fcm.reshape(B, N, C))

    def _L0_ffn_ref(input_embeddings, router_w, w1, b1, w2, b2):
        import jax, jax.numpy as jnp
        import numpy as np
        NUM_EXPERTS = 8
        TOP_K = 2
        B, S, D = (8, 2048, 64)

        def _moe(tokens, router_w, w1, b1, w2, b2):
            N = tokens.shape[0]
            E = router_w.shape[0]
            logits = tokens.astype(jnp.float32) @ router_w.astype(jnp.float32).T
            probs = jax.nn.softmax(logits, axis=-1)
            rw, re = jax.lax.top_k(probs, TOP_K)
            if TOP_K > 1:
                rw = rw / jnp.maximum(rw.sum(-1, keepdims=True), 1e-12)
            rw = rw.astype(tokens.dtype)
            combine = jnp.zeros((N, E), tokens.dtype).at[jnp.arange(N)[:, None], re].set(rw)
            out = tokens
            for e in range(E):
                h = jax.nn.gelu(tokens @ w1[e] + b1[e], approximate=False)
                y = h @ w2[e] + b2[e]
                out = out + combine[:, e:e + 1] * y
            return out
        b, s, d = input_embeddings.shape
        tokens = input_embeddings.reshape(b * s, d)
        return _moe(tokens, router_w, w1, b1, w2, b2).reshape(b, s, d)

    def _L1_attn_ref(x, Wq, bq, Wk, bk, Wv, bv, Wo, bo):
        import jax, jax.numpy as jnp
        import numpy as np
        DIM = 64
        HEADS = 4
        HEAD_DIM = DIM // HEADS
        SCALE = HEAD_DIM ** (-0.5)
        B, N, C = x.shape
        x = jnp.clip(x, -10000.0, 10000.0)

        def heads(t):
            return t.reshape(B, N, HEADS, HEAD_DIM).transpose(0, 2, 1, 3)
        q = heads((x @ Wq.T + bq).astype(jnp.float32))
        k = heads((x @ Wk.T + bk).astype(jnp.float32))
        v = heads((x @ Wv.T + bv).astype(jnp.float32))
        attn = jnp.einsum('bhnd,bhmd->bhnm', q, k) * SCALE
        attn = jax.nn.softmax(attn, axis=-1)
        out = jnp.einsum('bhnm,bhmd->bhnd', attn, v)
        out = out.transpose(0, 2, 1, 3).reshape(B, N, C)
        out = out.astype(jnp.bfloat16).astype(jnp.float32)
        return out @ Wo.T + bo

    def _L1_ffn_ref(h, gate_w, gate_b, w1, b1, w2, b2):
        import math
        import jax, jax.numpy as jnp
        import numpy as np
        CAPACITY_FACTOR = 1.25
        B, L, D = h.shape
        E = gate_w.shape[1]
        T = B * L
        C = max(1, math.ceil(CAPACITY_FACTOR * T / E))
        x = h.reshape(T, D)
        logits = x @ gate_w + gate_b
        probs = jax.nn.softmax(logits, axis=-1)
        idx = jnp.argmax(probs, axis=-1)
        prb = jnp.take_along_axis(probs, idx[:, None], axis=1)[:, 0]
        one_hot = jax.nn.one_hot(idx, E, dtype=jnp.float32)
        pos = (jnp.cumsum(one_hot, axis=0) * one_hot).sum(-1).astype(jnp.int32) - 1
        kept = pos < C
        pos_safe = jnp.where(kept, pos, C)
        buf = jnp.zeros((E, C, D), dtype=h.dtype).at[idx, pos_safe].set(x, mode='drop')
        hmid = jax.nn.relu(jnp.einsum('ecd,edf->ecf', buf, w1) + b1[:, None, :])
        ybuf = jnp.einsum('ecf,efd->ecd', hmid, w2) + b2[:, None, :]
        pos_g = jnp.minimum(pos, C - 1)
        y_tok = ybuf[idx, pos_g] * (prb * kept)[:, None]
        y = y_tok.reshape(B, L, D)
        y = jnp.nan_to_num(y, nan=0.0, posinf=10000.0, neginf=-10000.0)
        return y
    h = _L0_tok_ref(x, L0_tok_fc0_w, L0_tok_fc0_b, L0_tok_ln0_g, L0_tok_ln0_b, L0_tok_w1r, L0_tok_w1i, L0_tok_w2r, L0_tok_w2i, L0_tok_conv_w, L0_tok_conv_b, L0_tok_ln_g, L0_tok_ln_b, L0_tok_fc1_w, L0_tok_fc1_b, L0_tok_fc2_w, L0_tok_fc2_b, L0_tok_fc3_w, L0_tok_fc3_b)
    h = jnp.concatenate([h, txt], axis=1)
    h = h + _L0_attn_ref(_layernorm(h, axis=-1))
    h = h + _L0_ffn_ref(_layernorm(h, axis=-1), L0_ffn_router_w, L0_ffn_w1, L0_ffn_b1, L0_ffn_w2, L0_ffn_b2)
    h = h + _L1_attn_ref(_layernorm(h, axis=-1), L1_attn_Wq, L1_attn_bq, L1_attn_Wk, L1_attn_bk, L1_attn_Wv, L1_attn_bv, L1_attn_Wo, L1_attn_bo)
    h = h + _L1_ffn_ref(_layernorm(h, axis=-1), L1_ffn_gate_w, L1_ffn_gate_b, L1_ffn_w1, L1_ffn_b1, L1_ffn_w2, L1_ffn_b2)
    return h

_drawn_inputs = setup_inputs


def setup_inputs(seed=0):
    import zlib

    import numpy as np

    out = dict(_drawn_inputs(seed))
    spreads = {'L0_tok_fc0_b': (0.0, 0.1),
     'L0_tok_ln0_g': (1.0, 0.2),
     'L0_tok_ln0_b': (0.0, 0.1),
     'L0_tok_conv_b': (0.0, 0.1),
     'L0_tok_ln_g': (1.0, 0.2),
     'L0_tok_ln_b': (0.0, 0.1),
     'L0_tok_fc1_b': (0.0, 0.1),
     'L0_tok_fc2_b': (0.0, 0.1),
     'L0_ffn_b1': (0.0, 0.1),
     'L0_ffn_b2': (0.0, 0.1),
     'L1_attn_bq': (0.0, 0.555),
     'L1_attn_bk': (0.0, 2.0),
     'L1_attn_bv': (0.0, 0.1),
     'L1_attn_bo': (0.0, 0.1),
     'L1_ffn_gate_b': (0.0, 0.1),
     'L1_ffn_b1': (0.0, 0.8),
     'L1_ffn_b2': (0.0, 0.798)}
    factors = {'L0_tok_w1r': 8.0, 'L0_tok_w1i': 32.823, 'L0_tok_w2r': 29.415, 'L0_tok_w2i': 29.282}
    for name, (base, spread) in spreads.items():
        noise = np.random.default_rng([zlib.crc32(name.encode()), seed]).standard_normal(out[name].shape)
        drawn = base * np.exp(spread * noise) if base else spread * noise
        out[name] = jnp.asarray(drawn.astype(out[name].dtype))
    for name, factor in factors.items():
        out[name] = (out[name] * factor).astype(out[name].dtype)
    return out
```

```python
from contextlib import ExitStack

import numpy as np

import concourse.bass as bass
from concourse import mybir

F32 = mybir.dt.float32
BF16 = mybir.dt.bfloat16
ALU = mybir.AluOpType
ACT = mybir.ActivationFunctionType
AX = mybir.AxisListType

P = 128
BATCH, SIDE, CH = 64, 64, 32
LAYERS, MODES = 4, 12
PIX = SIDE * SIDE
OCT = 8
TILE_IMG = P // CH
TILES = OCT // TILE_IMG
N_OCT = BATCH // OCT
NORMS = LAYERS + 1
CHUNK = 512
CHUNKS = PIX // CHUNK
KRI = 2 * MODES
HBLK = 4
N_HBLK = SIDE // HBLK
TXT = 77
SEQ = SIDE + TXT
D = 64
TOK = BATCH * SEQ
NT = 72
FULL_T = TOK // P
REST = TOK - FULL_T * P
LN_EPS = 1e-5


def fourier_tables():
    n = np.arange(SIDE)
    ky = np.arange(MODES)
    kx = np.concatenate([np.arange(MODES), np.arange(SIDE - MODES, SIDE)])
    aw = 2 * np.pi * np.outer(n, ky) / SIDE
    ah = 2 * np.pi * np.outer(n, kx) / SIDE
    fw = np.zeros((2, TILE_IMG, 32, MODES, 2, TILE_IMG))
    for half in range(2):
        a = aw[32 * half:32 * half + 32]
        for b in range(TILE_IMG):
            fw[half, b, :, :, 0, b] = np.cos(a)
            fw[half, b, :, :, 1, b] = -np.sin(a)
    fh = np.zeros((2, TILES, SIDE, TILES, 2, 2, MODES))
    c, s = np.cos(ah).reshape(SIDE, 2, MODES), np.sin(ah).reshape(SIDE, 2, MODES)
    for g in range(TILES):
        fh[0, g, :, g, :, 0], fh[0, g, :, g, :, 1] = c, -s
        fh[1, g, :, g, :, 0], fh[1, g, :, g, :, 1] = s, c
    ih = np.zeros((2, 2, 32, SIDE, 2))
    for st in range(2):
        ih[st, 0, :MODES, :, 0], ih[st, 0, :MODES, :, 1] = c[:, st].T, s[:, st].T
        ih[st, 1, :MODES, :, 0], ih[st, 1, :MODES, :, 1] = -s[:, st].T, c[:, st].T
    iw = np.zeros((HBLK, MODES, 2, HBLK, SIDE))
    weight = np.where(ky == 0, 1.0, 2.0)[:, None] / PIX
    for h in range(HBLK):
        iw[h, :, 0, h] = weight * np.cos(aw).T
        iw[h, :, 1, h] = -weight * np.sin(aw).T
    eye = np.eye(P)
    mean = np.kron(np.eye(TILE_IMG), np.full((CH, CH), 1.0 / CH))
    sign = np.ones((P, 1))
    sign[32:64], sign[96:128] = -1.0, -1.0
    parts = {
        "fw0": fw[0].reshape(P, -1), "fw1": fw[1].reshape(P, -1),
        "fh0": fh[0].reshape(P, -1), "fh1": fh[1].reshape(P, -1),
        "ih": ih.reshape(P, -1), "iw": np.pad(iw.reshape(HBLK * KRI, -1), ((0, P - HBLK * KRI), (0, 0))),
        "eye": eye, "mean": mean, "center": eye - mean, "sign": sign,
    }
    at, n = {}, 0
    for name, a in parts.items():
        at[name] = (n, a.shape[1])
        n += a.shape[1]
    return np.concatenate(list(parts.values()), axis=1).astype(np.float32), at


TABLES, TABLE_AT = fourier_tables()
PRM = {}
_n = 0
for _name, _w in (("bias", NORMS), ("gain", NORMS), ("shift", NORMS), ("fc1b", 1), ("fc2b", 1), ("fc3b", 1),
                  ("fc0", 3 * TILE_IMG), ("conv", LAYERS * P), ("fc1", 128), ("fc2", 64), ("fc3", 2)):
    PRM[_name] = (_n, _w)
    _n += _w
PRM_W = _n


def layout_operator(i):
    p = np.zeros((P, PRM_W), np.float32)

    def put(name, a):
        n, w = PRM[name]
        p[:, n:n + w] = a

    def four(v):
        return np.tile(v, TILE_IMG)

    put("bias", np.stack([four(i["L0_tok_fc0_b"])] + [four(v) for v in i["L0_tok_conv_b"]], 1))
    put("gain", np.stack([four(i["L0_tok_ln0_g"])] + [four(v) for v in i["L0_tok_ln_g"]], 1))
    put("shift", np.stack([four(i["L0_tok_ln0_b"])] + [four(v) for v in i["L0_tok_ln_b"]], 1))
    put("fc1b", i["L0_tok_fc1_b"][:, None])
    put("fc2b", np.tile(i["L0_tok_fc2_b"], 2)[:, None])
    put("fc3b", np.broadcast_to(i["L0_tok_fc3_b"][None, :], (P, 1)))
    fc0 = np.zeros((TILE_IMG, CH, TILE_IMG, 3), np.float32)
    conv = np.zeros((TILE_IMG, CH, LAYERS, TILE_IMG, CH), np.float32)
    for b in range(TILE_IMG):
        fc0[b, :, b, :] = i["L0_tok_fc0_w"].T
        conv[b, :, :, b, :] = i["L0_tok_conv_w"].transpose(1, 0, 2)
    put("fc0", fc0.reshape(P, -1))
    put("conv", conv.reshape(P, -1))
    put("fc1", np.tile(i["L0_tok_fc1_w"], (TILE_IMG, 1)))
    put("fc2", i["L0_tok_fc2_w"])
    fc3 = np.zeros((2, 64, 2), np.float32)
    for s in range(2):
        fc3[s, :, s] = i["L0_tok_fc3_w"][:, 0]
    put("fc3", fc3.reshape(P, 2))
    w = np.empty((LAYERS, 2, 2, CH, MODES, MODES, 2, CH), np.float32)
    for st, (re, im) in enumerate((("L0_tok_w1r", "L0_tok_w1i"), ("L0_tok_w2r", "L0_tok_w2i"))):
        r = i[re].transpose(0, 1, 4, 3, 2)
        m = i[im].transpose(0, 1, 4, 3, 2)
        w[:, st, 0, :, :, :, 0], w[:, st, 0, :, :, :, 1] = r, m
        w[:, st, 1, :, :, :, 0], w[:, st, 1, :, :, :, 1] = m, r
    x = i["x"].transpose(0, 3, 1, 2).reshape(N_OCT, TILES, TILE_IMG * 3, PIX)
    return {"tables": TABLES, "prm": p, "spec": w.reshape(LAYERS, P, MODES * MODES * 2 * CH), "pix": x}


def operator_setup(nc, din, spec_ready, prm, tab, fc0c):
    SPEC_W = MODES * MODES * 2 * CH
    t = lambda name: tab[:, TABLE_AT[name][0]:sum(TABLE_AT[name])]
    q = lambda name: prm[:, PRM[name][0]:sum(PRM[name])]
    with ExitStack() as ctx:
        sb = lambda name, shape: ctx.enter_context(nc.sbuf_tensor(name, shape, F32))
        sem = lambda name: ctx.enter_context(nc.semaphore(name))
        raw = sb("spec_raw", [P, SPEC_W])
        done = sb("spec_done", [P, SPEC_W])
        mean = sb("spec_mean", [P, SPEC_W // CH])
        ps = ctx.enter_context(nc.psum_tensor("setup_ps", [P, 2, CHUNK], F32))
        tables_in, spec_in = sem("tables_in"), sem("spec_in")
        centered, center_kept = sem("centered"), sem("center_kept")
        signed, summed, scaled, finished, stored = (sem(n) for n in ("signed", "summed", "scaled", "finished", "stored"))
        block = ctx.enter_context(nc.Block())

        @block.sync
        def _(sp):
            sp.dma_start(prm[:, :], din["prm"]).then_inc(tables_in, 16)
            sp.dma_start(tab[:, :], din["tables"]).then_inc(tables_in, 16)
            with sp.Fori(0, LAYERS) as layer:
                sp.wait_ge(finished, layer)
                sp.dma_start(raw[:, :], din["spec"][bass.ds(layer, 1), :, :].rearrange("a p n -> (a p) n")).then_inc(spec_in, 16)
            sp.wait_ge(stored, 16 * LAYERS)

        @block.scalar
        def _(act):
            with act.Fori(0, LAYERS) as layer:
                act.wait_ge(finished, layer + 1)
                act.dma_start(spec_ready[bass.ds(layer, 1), :, :].rearrange("a p n -> (a p) n"), done[:, :]).then_inc(stored, 16)

        @block.vector
        def _(dve):
            dve.wait_ge(centered, 1)
            dve.tensor_copy(q("conv"), ps[:, 0, :]).then_inc(center_kept, 1)
            dve.tensor_copy(q("bias"), ps[:, 1, 0:NORMS]).then_inc(center_kept, 1)
            dve.tensor_copy(fc0c[:, :], ps[0:3 * TILE_IMG, 1, P:2 * P]).then_inc(center_kept, 1)
            with dve.Fori(0, LAYERS) as layer:
                dve.wait_ge(spec_in, layer * 16 + 16)
                re_out = raw[:, :].rearrange("p (m r o) -> p m r o", r=2, o=CH)[:, :, 0, :]
                dve.tensor_scalar(re_out, re_out, t("sign"), None, ALU.mult).then_inc(signed, 1)
                dve.wait_ge(signed, layer + 1)
                rows = raw[:, :].rearrange("p (m o) -> p m o", o=CH)
                dve.tensor_reduce(mean[:, :], rows, AX.X, ALU.add).then_inc(summed, 1)
                dve.wait_ge(summed, layer + 1)
                dve.tensor_scalar(mean[:, :], mean[:, :], 1.0 / CH, None, ALU.mult).then_inc(scaled, 1)
                dve.wait_ge(scaled, layer + 1)
                dve.wait_ge(stored, layer * 16)
                dve.tensor_tensor(done[:, :].rearrange("p (m o) -> p m o", o=CH), rows,
                                  mean[:, :].unsqueeze(2).broadcast_to([P, SPEC_W // CH, CH]), ALU.subtract).then_inc(finished, 1)

        @block.tensor
        def _(pe):
            pe.wait_ge(tables_in, 32)
            for layer in range(LAYERS):
                pe.matmul(ps[:, 0, P * layer:P * layer + P], q("conv")[:, P * layer:P * layer + P], t("center"), start=True, stop=True)
            pe.matmul(ps[:, 1, 0:NORMS], t("center"), q("bias"), start=True, stop=True)
            pe.matmul(ps[0:3 * TILE_IMG, 1, P:2 * P], q("fc0"), t("center"), start=True, stop=True).then_inc(centered, 1)


def operator(nc, din, spec_ready, hid, prm, tab, fc0c, n_oct=N_OCT):
    t = lambda name: tab[:, TABLE_AT[name][0]:sum(TABLE_AT[name])]
    q = lambda name, rows=P: prm[0:rows, PRM[name][0]:sum(PRM[name])]
    tok = hid.rearrange("(b s) d -> b (s d)", s=SEQ)
    with ExitStack() as ctx:
        sb = lambda name, shape: ctx.enter_context(nc.sbuf_tensor(name, shape, F32))
        sem = lambda name: ctx.enter_context(nc.semaphore(name))
        Z = sb("Z", [P, TILES, PIX])
        ZW = sb("ZW", [P, TILES, PIX])
        WS = sb("WS", [P, MODES * MODES, 2 * CH])
        MB = sb("MB", [P, MODES * MODES, 2, OCT])
        Y = sb("Y", [P, MODES, OCT, 32])
        YT = sb("YT", [P, MODES, OCT, 32])
        U = sb("U", [P, KRI, TILE_IMG, CH])
        T = sb("T", [P, TILES, SIDE, MODES, 2])
        TT = sb("TT", [HBLK * KRI, TILES, N_HBLK, P])
        SQ = sb("SQ", [P, 4, CHUNK])
        RS = sb("RS", [P, 4, CHUNK])
        conv = sb("conv_now", [P, P])
        vecs = sb("vecs_now", [P, 4])
        epsb = sb("epsb", [P, 1])
        OUT = TT[0:2, :, :, :].rearrange("p t a n -> p (t a n)")
        PS = ctx.enter_context(nc.psum_tensor("PS", [P, 8, CHUNK], F32))
        psf = PS[:, :, :].rearrange("p a n -> p (a n)")
        (pix_in, weights_in, prepared, vecs_ready, conv_ready, y_done, sq_done, var_done, std_done, inv_done, norm_done,
         z_done, turned, u_mm, u_kept, v_mm, v_kept, mix_mm, mix_kept, y_turned, t_mm, t_kept, tt_mm, tt_kept,
         fc1_mm, fc1_act, fc2_mm, fc2_act, fc3_mm, fc3_kept, out_sent, text_sent) = (sem(n) for n in (
             "pix_in weights_in prepared vecs_ready conv_ready y_done sq_done var_done std_done inv_done norm_done z_done "
             "turned u_mm u_kept v_mm v_kept mix_mm mix_kept y_turned t_mm t_kept tt_mm tt_kept fc1_mm fc1_act fc2_mm "
             "fc2_act fc3_mm fc3_kept out_sent text_sent").split())
        NCH = TILES * CHUNKS
        PAIRS = OCT // 2
        NM = PAIRS * CHUNKS
        cols = lambda c: slice((c % CHUNKS) * CHUNK, (c % CHUNKS + 1) * CHUNK)
        H1 = [SQ[:, 0:2, :], SQ[:, 2:4, :]]
        H2 = [RS[:, 0, :], RS[:, 1, :]]

        def keep_modes(copy, y0, y1):
            for img in range(TILE_IMG):
                for st in range(2):
                    for ri in range(2):
                        src = psf[32 * img:32 * img + 32, P * y0:P * y1].rearrange("p (y n) -> p y n", n=P)[:, :, 0:96]
                        src = src.rearrange("p y (g s r x) -> p y g s r x", g=2, s=2, r=2)[:, :, :, st, ri, :]
                        at = 64 * st + 32 * ri
                        dst = MB[at:at + 32, MODES * y0:MODES * y1, st, :].rearrange("p (y x) (g i) -> p y g i x", x=MODES, i=TILE_IMG)[:, :, :, img, :]
                        last = copy(dst, src)
            return last

        def keep_mix(copy, part, st):
            src = psf[0:2 * CH, (3 - 3 * part) * CHUNK:(6 - 3 * part) * CHUNK].rearrange("p (y n) -> p y n", n=256)[:, :, 0:192]
            src = src.rearrange("p y (x s b) -> p y x s b", x=MODES, s=2)[:, :, :, st, :]
            dst = Y[64 * st:64 * st + 64, 6 * part:6 * part + 6, :, 0:MODES].rearrange("p y b x -> p y x b")
            return copy(dst, src)

        def keep_t(copy, g):
            src = psf[:, (3 - 3 * g) * CHUNK:(6 - 3 * g) * CHUNK].rearrange("p (y h r) -> p y h r", h=SIDE, r=2)
            return copy(T[:, g, :, :, :].rearrange("p h y r -> p y h r"), src)

        block = ctx.enter_context(nc.Block())

        @block.sync
        def _(sp):
            for b in range(4):
                sp.dma_start(tok[16 * b:16 * b + 16, SIDE * D:], din["txt"][16 * b:16 * b + 16, :]).then_inc(text_sent, 16)
            with sp.Fori(0, n_oct) as octet:
                sp.wait_ge(fc3_kept, octet * NM)
                sp.dma_start(ZW[0:3 * TILE_IMG, :, :], din["pix"][bass.ds(octet, 1), :, :, :].rearrange("a t p n -> p (a t) n")).then_inc(pix_in, 16)
                with sp.Fori(0, LAYERS) as layer:
                    sp.wait_ge(mix_mm, (octet * LAYERS + layer) * 2)
                    sp.dma_start(WS[:, :, :], spec_ready[bass.ds(layer, 1), :, :].rearrange("a p (m n) -> p (a m) n", n=2 * CH)).then_inc(weights_in, 16)
                for pair in range(PAIRS):
                    sp.wait_ge(fc3_kept, octet * NM + (pair + 1) * CHUNKS)
                    sp.dma_start(tok[bass.ds(octet * OCT + 2 * pair, 2), 0:PIX], OUT).then_inc(out_sent, 16)
            sp.wait_ge(out_sent, 16 * PAIRS * n_oct)
            sp.wait_ge(text_sent, 64)

        @block.tensor
        def _(pe):
            def norm(n, make):
                for c in range(NCH + 1):
                    if c < NCH:
                        if c >= 4:
                            pe.wait_ge(norm_done, n * NCH + c - 3)
                        make(c).then_inc(y_done, 1)
                    if c >= 1:
                        v = c - 1
                        if v >= 4:
                            pe.wait_ge(std_done, n * NCH + v - 3)
                        pe.wait_ge(sq_done, n * NCH + v + 1)
                        pe.matmul(PS[:, 4 + v % 4, :], t("mean"), SQ[:, v % 4, :], start=True, stop=True).then_inc(var_done, 1)

            def first(c):
                return pe.matmul(PS[:, c % 4, :], fc0c[:, :], ZW[0:3 * TILE_IMG, c // CHUNKS, cols(c)], start=True, stop=True)

            def layer_step(it, n):
                pe.wait_ge(turned, (it + 1) * TILES)
                for c in range(CH):
                    for half in range(2):
                        z = ZW[:, :, :].rearrange("p t (h v c) -> p t h v c", v=2, c=CH)[:, :, :, half, c]
                        mm = pe.matmul(PS[:, c // 4, 96 * (c % 4):96 * (c % 4) + 96], z, t(f"fw{half}"), start=(half == 0), stop=(half == 1))
                    if c % 4 == 3:
                        mm.then_inc(u_mm, 1)
                pe.wait_ge(u_kept, (it + 1) * 8)
                for ky in range(MODES):
                    for ri in range(2):
                        mm = pe.matmul(psf[:, P * ky:P * ky + 96], U[:, 2 * ky + ri, :, :], t(f"fh{ri}"), start=(ri == 0), stop=(ri == 1))
                    if ky % 4 == 3:
                        mm.then_inc(v_mm, 1)
                pe.wait_ge(weights_in, it * 16 + 16)
                pe.wait_ge(v_kept, (it + 1) * 2)
                for part in range(2):
                    for m in range(72 * part, 72 * part + 72):
                        at = (3 - 3 * part) * CHUNK + 256 * (m // 12 - 6 * part) + 16 * (m % 12)
                        mm = pe.matmul(psf[0:2 * CH, at:at + 16], WS[:, m, :], MB[:, m, :, :], start=True, stop=True)
                    mm.then_inc(mix_mm, 1)
                pe.wait_ge(y_turned, it + 1)
                for g in range(TILES):
                    for ky in range(MODES):
                        at = (3 - 3 * g) * CHUNK + P * ky
                        mm = pe.matmul(psf[:, at:at + P], YT[:, ky, TILE_IMG * g:TILE_IMG * (g + 1), :], t("ih"), start=True, stop=True)
                    mm.then_inc(t_mm, 1)
                pe.wait_ge(t_kept, (it + 1) * 2)
                for u in range(TILES * N_HBLK // 4):
                    g = u // 4
                    for k in range(4):
                        hb = 4 * (u % 4) + k
                        src = T[:, g, HBLK * hb:HBLK * (hb + 1), :, :].rearrange("p h k r -> p (h k r)")
                        mm = pe.transpose(PS[0:HBLK * KRI, u, P * k:P * k + P], src, t("eye"))
                    mm.then_inc(tt_mm, 1)
                pe.wait_ge(tt_kept, (it + 1) * 8)
                pe.wait_ge(conv_ready, it + 1)

                def both(c):
                    g, j = c // CHUNKS, c % CHUNKS
                    for k in range(2):
                        half = PS[:, c % 4, 256 * k:256 * k + 256]
                        pe.matmul(half, conv[:, :], Z[:, g, CHUNK * j + 256 * k:CHUNK * j + 256 * k + 256], start=True, stop=False)
                        mm = pe.matmul(half, TT[:, g, 2 * j + k, :], t("iw")[0:HBLK * KRI, :], start=False, stop=True)
                    return mm

                norm(n, both)

            def mlp(octet):
                b = octet * NM
                for i in range(NM + 2):
                    pair, j = i // CHUNKS, i % CHUNKS
                    if i < NM:
                        if i >= 2:
                            pe.wait_ge(fc1_act, b + i - 1)
                        for s in range(2):
                            im = 2 * pair + s
                            k = 32 * (im % TILE_IMG)
                            mm = pe.matmul(PS[:, 2 * (i % 2) + s, :], q("fc1")[k:k + 32, :], Z[k:k + 32, im // TILE_IMG, CHUNK * j:CHUNK * (j + 1)],
                                           start=True, stop=True)
                        mm.then_inc(fc1_mm, 1)
                    if 1 <= i <= NM:
                        pe.wait_ge(fc1_act, b + i)
                        if i >= 3:
                            pe.wait_ge(fc2_act, b + i - 2)
                        for s in range(2):
                            mm = pe.matmul(PS[64 * s:64 * s + 64, 4 + (i - 1) % 2, :], q("fc2"), H1[(i - 1) % 2][:, s, :], start=True, stop=True)
                        mm.then_inc(fc2_mm, 1)
                    if i >= 2:
                        pe.wait_ge(fc2_act, b + i - 1)
                        if i >= 4:
                            pe.wait_ge(fc3_kept, b + i - 3)
                        pe.matmul(PS[0:2, 6 + i % 2, :], q("fc3"), H2[i % 2], start=True, stop=True).then_inc(fc3_mm, 1)

            pe.wait_ge(prepared, 1)
            with pe.Fori(0, n_oct) as octet:
                pe.wait_ge(pix_in, octet * 16 + 16)
                pe.wait_ge(fc3_kept, octet * NM)
                norm(octet * NORMS, first)
                with pe.Fori(0, LAYERS) as layer:
                    layer_step(octet * LAYERS + layer, octet * NORMS + 1 + layer)
                pe.wait_ge(z_done, (octet + 1) * NORMS * TILES)
                mlp(octet)

        @block.scalar
        def _(act):
            def norm(n, last, gelu):
                act.wait_ge(vecs_ready, n + 1)
                for c in range(NCH + 1):
                    if c < NCH:
                        act.wait_ge(y_done, n * NCH + c + 1)
                        act.activation(SQ[:, c % 4, :], PS[:, c % 4, :], ACT.Square, bias=vecs[:, 0:1]).then_inc(sq_done, 1)
                    if c >= 1:
                        v = c - 1
                        act.wait_ge(var_done, n * NCH + v + 1)
                        if v >= 4:
                            act.wait_ge(norm_done, n * NCH + v - 3)
                        act.activation(RS[:, v % 4, :], PS[:, 4 + v % 4, :], ACT.Sqrt, bias=epsb[:, :]).then_inc(std_done, 1)
                for g in range(TILES):
                    act.wait_ge(norm_done, n * NCH + (g + 1) * CHUNKS)
                    act.activation(Z[:, g, :], Z[:, g, :], ACT.Gelu if gelu else ACT.Identity,
                                   bias=vecs[:, 2:3], scale=vecs[:, 1:2]).then_inc(z_done, 1)

            def layer_step(it, n, gelu):
                for u in range(1, 8, 2):
                    act.wait_ge(u_mm, it * 8 + u + 1)
                    act.copy(U[:, :, :, 4 * u:4 * u + 4].rearrange("p k b c -> p c (k b)"),
                             PS[:, u, 0:384].rearrange("p (c k) -> p c k", c=4)).then_inc(u_kept, 1)
                act.wait_ge(v_mm, it * 3 + 1)
                keep_modes(act.copy, 0, 4).then_inc(v_kept, 1)
                act.wait_ge(mix_mm, it * 2 + 1)
                for st in range(2):
                    last = keep_mix(act.copy, 0, st)
                last.then_inc(mix_kept, 1)
                act.wait_ge(t_mm, it * 2 + 2)
                keep_t(act.copy, 1).then_inc(t_kept, 1)
                for u in range(1, 8, 2):
                    act.wait_ge(tt_mm, it * 8 + u + 1)
                    act.copy(TT[:, u // 4, 4 * (u % 4):4 * (u % 4) + 4, :], PS[0:HBLK * KRI, u, :].rearrange("p (a n) -> p a n", a=4)).then_inc(tt_kept, 1)
                norm(n, None, gelu)

            def mlp(octet):
                b = octet * NM
                for i in range(NM + 1):
                    if i < NM:
                        act.wait_ge(fc1_mm, b + i + 1)
                        if i >= 2:
                            act.wait_ge(fc2_mm, b + i - 1)
                        act.activation(H1[i % 2], PS[:, 2 * (i % 2):2 * (i % 2) + 2, :], ACT.Gelu, bias=q("fc1b")).then_inc(fc1_act, 1)
                    if i >= 1:
                        act.wait_ge(fc2_mm, b + i)
                        if i >= 3:
                            act.wait_ge(fc3_mm, b + i - 2)
                        act.activation(H2[(i - 1) % 2], PS[:, 4 + (i - 1) % 2, :], ACT.Gelu, bias=q("fc2b")).then_inc(fc2_act, 1)

            act.wait_ge(prepared, 1)
            with act.Fori(0, n_oct) as octet:
                act.wait_ge(out_sent, octet * (16 * PAIRS))
                norm(octet * NORMS, None, False)
                with act.Fori(0, LAYERS - 1) as layer:
                    layer_step(octet * LAYERS + layer, octet * NORMS + 1 + layer, True)
                layer_step(octet * LAYERS + LAYERS - 1, octet * NORMS + LAYERS, False)
                mlp(octet)

        @block.vector
        def _(dve):
            def norm(n):
                for c in range(NCH):
                    dve.wait_ge(std_done, n * NCH + c + 1)
                    dve.reciprocal(RS[:, c % 4, :], RS[:, c % 4, :]).then_inc(inv_done, 1)
                    dve.wait_ge(inv_done, n * NCH + c + 1)
                    dve.scalar_tensor_tensor(out=Z[:, c // CHUNKS, cols(c)], in0=PS[:, c % 4, :], scalar=vecs[:, 0:1],
                                             in1=RS[:, c % 4, :], op0=ALU.add, op1=ALU.mult).then_inc(norm_done, 1)

            def take_vecs(n, layer1):
                if layer1 is not None:
                    dve.wait_ge(z_done, n * TILES)
                v = prm[:, 0:3 * NORMS].rearrange("p (k n) -> p k n", n=NORMS)
                v = v[:, :, 0:1] if layer1 is None else v[:, :, bass.ds(layer1, 1)]
                dve.tensor_copy(vecs[:, 0:3].unsqueeze(2), v).then_inc(vecs_ready, 1)

            def layer_step(it, n, layer):
                for g in range(TILES):
                    dve.wait_ge(z_done, n * TILES - TILES + g + 1)
                    dve.transpose(ZW[:, g, :], Z[:, g, :]).then_inc(turned, 1)
                take_vecs(n, layer + 1)
                dve.tensor_copy(conv[:, :].unsqueeze(1), q("conv").rearrange("p (l n) -> p l n", n=P)[:, bass.ds(layer, 1), :]).then_inc(conv_ready, 1)
                for u in range(0, 8, 2):
                    dve.wait_ge(u_mm, it * 8 + u + 1)
                    dve.tensor_copy(U[:, :, :, 4 * u:4 * u + 4].rearrange("p k b c -> p c (k b)"),
                                    PS[:, u, 0:384].rearrange("p (c k) -> p c k", c=4)).then_inc(u_kept, 1)
                dve.wait_ge(v_mm, it * 3 + 3)
                keep_modes(dve.tensor_copy, 4, 12).then_inc(v_kept, 1)
                dve.wait_ge(mix_mm, it * 2 + 2)
                for st in range(2):
                    last = keep_mix(dve.tensor_copy, 1, st)
                last.then_inc(mix_kept, 1)
                dve.wait_ge(mix_kept, (it + 1) * 2)
                dve.transpose(YT[:, :, :, :].rearrange("p y b x -> p (y b x)"), Y[:, :, :, :].rearrange("p y b x -> p (y b x)")).then_inc(y_turned, 1)
                dve.wait_ge(t_mm, it * 2 + 1)
                keep_t(dve.tensor_copy, 0).then_inc(t_kept, 1)
                for u in range(0, 8, 2):
                    dve.wait_ge(tt_mm, it * 8 + u + 1)
                    dve.tensor_copy(TT[:, u // 4, 4 * (u % 4):4 * (u % 4) + 4, :], PS[0:HBLK * KRI, u, :].rearrange("p (a n) -> p a n", a=4)).then_inc(tt_kept, 1)
                norm(n)

            dve.memset(epsb[:, :], LN_EPS)
            dve.memset(MB[:, :, :, :], 0.0)
            dve.memset(Y[:, :, :, :], 0.0).then_inc(prepared, 1)
            dve.wait_ge(prepared, 1)
            with dve.Fori(0, n_oct) as octet:
                dve.wait_ge(out_sent, octet * (16 * PAIRS))
                dve.wait_ge(z_done, octet * NORMS * TILES)
                take_vecs(octet * NORMS, None)
                dve.wait_ge(fc1_mm, octet * NM)
                norm(octet * NORMS)
                with dve.Fori(0, LAYERS) as layer:
                    layer_step(octet * LAYERS + layer, octet * NORMS + 1 + layer, layer)
                for i in range(NM):
                    dve.wait_ge(fc3_mm, octet * NM + i + 1)
                    if i % CHUNKS == 0:
                        dve.wait_ge(out_sent, octet * (16 * PAIRS) + 16 * (i // CHUNKS))
                    dve.tensor_scalar(OUT[:, CHUNK * (i % CHUNKS):CHUNK * (i % CHUNKS + 1)], PS[0:2, 6 + i % 2, :], q("fc3b", 2), None, ALU.add).then_inc(fc3_kept, 1)


HEADS, HD = 4, 16
EXPERTS = 8
CAP = int(np.ceil(1.25 * TOK / EXPERTS))
Q_ROWS = (SEQ + 1) // 2
M_ROWS = (Q_ROWS, SEQ - Q_ROWS)
TC = NT // 4

TPR = {}
_n = 0
for _name, _w in (("eye", P), ("tri", P), ("ones", P), ("rank", EXPERTS), ("router", EXPERTS), ("gate", EXPERTS), ("wo", D),
                  ("wq", P), ("wk", P), ("wv", D), ("m_w1", 4 * P), ("m_b1", 4), ("m_w2", 4 * P), ("m_b2", EXPERTS * D),
                  ("f_w1", 16 * P), ("f_b1", 16), ("f_w2", 16 * D), ("f_b2", EXPERTS * D)):
    TPR[_name] = (_n, _w)
    _n += _w
TPR_W = _n


def layout_tokens(i):
    p = np.zeros((P, TPR_W), np.float32)

    def put(name, a, rows=0):
        n, w = TPR[name]
        a = np.asarray(a).reshape(-1, w)
        p[rows:rows + a.shape[0], n:n + w] = a

    put("eye", np.eye(P))
    put("tri", np.triu(np.ones((P, P))))
    put("ones", np.ones((P, P)))
    put("rank", np.broadcast_to(np.arange(EXPERTS, 0, -1.0), (P, EXPERTS)))
    put("router", i["L0_ffn_router_w"].T)
    put("gate", i["L1_ffn_gate_w"])
    put("gate", i["L1_ffn_gate_b"], D)
    put("wo", i["L1_attn_Wo"].T)
    put("wo", i["L1_attn_bo"], D)
    for name, w, b in (("wq", "L1_attn_Wq", "L1_attn_bq"), ("wk", "L1_attn_Wk", "L1_attn_bk")):
        a = np.zeros((D + 1, HEADS, 32), np.float32)
        a[:D, :, :HD] = i[w].T.reshape(D, HEADS, HD)
        a[D, :, :HD] = i[b].reshape(HEADS, HD)
        put(name, a)
    put("wv", i["L1_attn_Wv"].T)
    put("wv", i["L1_attn_bv"], D)
    put("m_w1", i["L0_ffn_w1"].transpose(1, 0, 2))
    put("m_b1", i["L0_ffn_b1"].reshape(4, P).T)
    w2 = np.zeros((2, D, 4, 2, D), np.float32)
    for e in range(2):
        w2[e, :, :, e] = i["L0_ffn_w2"][e::2].transpose(1, 0, 2)
    put("m_w2", w2)
    put("m_b2", i["L0_ffn_b2"])
    put("f_w1", i["L1_ffn_w1"].transpose(1, 0, 2))
    put("f_b1", i["L1_ffn_b1"].reshape(16, P).T)
    put("f_w2", i["L1_ffn_w2"].reshape(16, P, D).transpose(1, 0, 2))
    put("f_b2", i["L1_ffn_b2"])
    return {"tokprm": p}


def bc(ap, n):
    return ap.unsqueeze(2).broadcast_to([ap.shape[0], ap.shape[1], n])


def chain_of(eng, step):
    count = [0]

    def link(ins):
        count[0] += 1
        ins.then_inc(step, 1)
        eng.wait_ge(step, count[0])
        return count[0]
    return link


def load_tokens(nc, name, src, X, tpr_dma=None):
    with nc.semaphore(name + "_loaded") as loaded, nc.Block() as block:
        @block.sync
        def _(sp):
            sp.dma_start(X[:, 0:FULL_T, :], src[0:FULL_T * P, :].rearrange("(t p) d -> p t d", p=P)).then_inc(loaded, 16)
            sp.dma_start(X[0:REST, FULL_T, :], src[FULL_T * P:TOK, :]).then_inc(loaded, 16)
            n = 32
            if tpr_dma is not None:
                sp.dma_start(tpr_dma[0], tpr_dma[1]).then_inc(loaded, 16)
                n += 16
            sp.wait_ge(loaded, n)

        @block.vector
        def _(dve):
            dve.memset(X[REST:P, FULL_T, :], 0.0)
            dve.memset(X[:, FULL_T + 1:NT, :], 0.0)


def token_norm(nc, name, H, X, SQ, clip=None, unit=None):
    with ExitStack() as ctx:
        sb = lambda n, shape: ctx.enter_context(nc.sbuf_tensor(name + n, shape, F32))
        sem = lambda n: ctx.enter_context(nc.semaphore(name + n))
        st = sb("_stat", [P, 4, NT])
        cst = sb("_const", [P, 2])
        step, rooted, squared = sem("_step"), sem("_rooted"), sem("_squared")
        block = ctx.enter_context(nc.Block())
        sq = SQ[:, 0:NT * D].rearrange("p (t d) -> p t d", d=D)
        marks = {}

        @block.vector
        def _(dve):
            link = chain_of(dve, step)
            dve.memset(cst[:, 0:1], LN_EPS)
            dve.memset(cst[:, 1:2], 0.0)
            link(dve.tensor_reduce(st[:, 0, :], H[:, :, :], AX.X, ALU.add))
            link(dve.tensor_scalar(st[:, 0, :], st[:, 0, :], 1.0 / D, None, ALU.mult))
            marks["centered"] = link(dve.tensor_tensor(X[:, :, :], H[:, :, :], bc(st[:, 0, :], D), ALU.subtract))
            dve.wait_ge(squared, 1)
            marks["variance"] = link(dve.tensor_reduce(st[:, 1, :], sq, AX.X, ALU.add))
            dve.wait_ge(rooted, 1)
            link(dve.reciprocal(st[:, 2, :], st[:, 1, :]))
            marks["normed"] = link(dve.tensor_tensor(X[:, :, :], X[:, :, :], bc(st[:, 2, :], D), ALU.mult))
            if clip is not None:
                link(dve.tensor_scalar(X[:, :, :], X[:, :, :], clip, -clip, ALU.min, ALU.max))
            if unit is not None:
                dve.wait_ge(squared, 2)
                marks["length"] = link(dve.tensor_reduce(st[:, 1, :], sq, AX.X, ALU.add))
                dve.wait_ge(rooted, 2)
                link(dve.tensor_scalar(st[:, 1, :], st[:, 1, :], 1e-12, None, ALU.max))
                link(dve.reciprocal(st[:, 2, :], st[:, 1, :]))
                link(dve.tensor_tensor(unit[:, :, 0:D], X[:, :, :], bc(st[:, 2, :], D), ALU.mult))
                link(dve.memset(unit[:, :, D:D + 1], 0.0))
                dve.memset(unit[:, 0:FULL_T, D:D + 1], 1.0)
                dve.memset(unit[0:REST, FULL_T, D:D + 1], 1.0)

        @block.scalar
        def _(act):
            act.wait_ge(step, marks["centered"])
            act.activation(sq, X[:, :, :], ACT.Square).then_inc(squared, 1)
            act.wait_ge(step, marks["variance"])
            act.activation(st[:, 1, :], st[:, 1, :], ACT.Sqrt, bias=cst[:, 0:1], scale=1.0 / D).then_inc(rooted, 1)
            if unit is not None:
                act.wait_ge(step, marks["normed"])
                act.activation(sq, X[:, :, :], ACT.Square).then_inc(squared, 1)
                act.wait_ge(step, marks["length"])
                act.activation(st[:, 1, :], st[:, 1, :], ACT.Sqrt, bias=cst[:, 1:2]).then_inc(rooted, 1)


def turn_tokens(nc, name, X, tpr, XT=None, weight=None, out=None):
    t = lambda n: tpr[:, TPR[n][0]:sum(TPR[n])]
    w = TPR[weight][1] if weight else 0
    kept_of = 1 if XT is not None else 0
    with ExitStack() as ctx:
        sb = lambda n, shape: ctx.enter_context(nc.sbuf_tensor(name + n, shape, F32))
        sem = lambda n: ctx.enter_context(nc.semaphore(name + n))
        stage = sb("_stage", [P, 2, 4, D])
        xs = sb("_xs", [D + 1, 2, CHUNK])
        ps = ctx.enter_context(nc.psum_tensor(name + "_ps", [P, 4, CHUNK], F32))
        ones_set, staged, turned, slotted, spread, formed, kept = (sem("_" + n) for n in (
            "ones_set", "staged", "turned", "slotted", "spread", "formed", "kept"))
        block = ctx.enter_context(nc.Block())

        @block.gpsimd
        def _(pool):
            if XT is not None:
                with pool.Fori(0, TC // 2) as i:
                    for s in range(2):
                        pool.wait_ge(slotted, 2 * i + s + 1)
                        pool.tensor_copy(XT[0:D + 1, bass.ds((2 * i + s) * CHUNK, CHUNK)], xs[:, s, :]).then_inc(spread, 1)

        @block.vector
        def _(dve):
            dve.memset(xs[D:D + 1, :, :], 1.0).then_inc(ones_set, 1)

            def stage_chunk(c, s):
                dve.tensor_copy(stage[:, s, :, :], X[:, bass.ds(c * 4, 4), 0:D]).then_inc(staged, 1)

            def keep_out(c, s):
                dve.wait_ge(formed, c + 1)
                dve.tensor_copy(out[:, bass.ds(c * 4, 4), 0:w], ps[:, 2 + s, 0:4 * w].rearrange("p (a n) -> p a n", a=4)).then_inc(kept, 1)

            with dve.Fori(0, TC // 2) as i:
                for s in range(2):
                    c = 2 * i + s
                    dve.wait_ge(turned, c - s)
                    stage_chunk(c, s)
                if out is not None:
                    for s in range(2):
                        keep_out(2 * i + s, s)

        @block.scalar
        def _(act):
            act.wait_ge(ones_set, 1)
            with act.Fori(0, TC // 2) as i:
                for s in range(2):
                    c = 2 * i + s
                    if XT is not None:
                        act.wait_ge(spread, c - s)
                    if out is not None:
                        act.wait_ge(formed, c - s)
                    act.wait_ge(turned, c + 1)
                    for k in range(2):
                        last = act.copy(xs[0:D, s, :].rearrange("p (a k n) -> p a k n", k=2, n=P)[:, :, k, :],
                                        ps[D * k:D * k + D, s, 0:2 * P].rearrange("p (a n) -> p a n", n=P))
                    last.then_inc(slotted, 1)

        @block.tensor
        def _(pe):
            with pe.Fori(0, TC // 2) as i:
                for s in range(2):
                    c = 2 * i + s
                    pe.wait_ge(slotted, c - s)
                    pe.wait_ge(staged, c + 1)
                    for k in range(2):
                        mm = pe.transpose(ps[:, s, P * k:P * k + P], stage[:, s, 2 * k:2 * k + 2, :], t("eye"))
                    mm.then_inc(turned, 1)
                if out is not None:
                    for s in range(2):
                        c = 2 * i + s
                        pe.wait_ge(kept, c - s)
                        pe.wait_ge(slotted, c + 1)
                        for k in range(4):
                            mm = pe.matmul(ps[:, 2 + s, w * k:w * k + w], xs[:, s, P * k:P * k + P], t(weight)[0:D + 1, :], start=True, stop=True)
                        mm.then_inc(formed, 1)


def global_attention(nc, FA, FT, OA):
    PAIRS = (FULL_T + 2) // 2
    with ExitStack() as ctx:
        sem = lambda n: ctx.enter_context(nc.semaphore(n))
        E = ctx.enter_context(nc.sbuf_tensor("E", [P, 2, 2, CHUNK], F32))
        Q = ctx.enter_context(nc.sbuf_tensor("queries", [D, 2, CHUNK], F32))
        q_ready = sem("q_ready")
        ps = ctx.enter_context(nc.psum_tensor("att_ps", [P, 8, CHUNK], F32))
        scored, weighed, used, summed, sums_kept = (sem(n) for n in ("scored", "weighed", "used", "summed", "sums_kept"))
        tiles = lambda pr: [j for j in (2 * pr, 2 * pr + 1) if j <= FULL_T]
        block = ctx.enter_context(nc.Block())

        @block.tensor
        def _(pe):
            def chunk(i, half):
                n = 2 * i + half
                pe.wait_ge(q_ready, n + 1)
                for pr in range(PAIRS + 1):
                    if pr < PAIRS:
                        if pr >= 2:
                            pe.wait_ge(weighed, n * PAIRS + pr - 1)
                        for j in tiles(pr):
                            mm = pe.matmul(ps[:, 2 * (pr % 2) + j % 2, :], FT[0:D, P * j:P * j + P], Q[:, half, :], start=True, stop=True)
                        mm.then_inc(scored, 1)
                    if pr >= 1:
                        pe.wait_ge(weighed, n * PAIRS + pr)
                        if pr == 1:
                            pe.wait_ge(sums_kept, n)
                        for j in tiles(pr - 1):
                            for k in range(4):
                                mm = pe.matmul(ps[:, 4 + k, 0:D + 1], E[:, (pr - 1) % 2, j % 2, P * k:P * k + P], FA[:, j, 0:D + 1],
                                               start=(j == 0), stop=(j == FULL_T))
                        mm.then_inc(used, 1)

            with pe.Fori(0, TC // 2) as i:
                for half in range(2):
                    chunk(i, half)

        @block.gpsimd
        def _(pool):
            with pool.Fori(0, TC // 2) as i:
                for half in range(2):
                    pool.wait_ge(used, i * (2 * PAIRS))
                    pool.tensor_copy(Q[:, half, :], FT[0:D, bass.ds((2 * i + half) * CHUNK, CHUNK)]).then_inc(q_ready, 1)

        @block.scalar
        def _(act):
            with act.Fori(0, TC) as i:
                for pr in range(PAIRS):
                    act.wait_ge(scored, i * PAIRS + pr + 1)
                    if pr >= 2:
                        act.wait_ge(used, i * PAIRS + pr - 1)
                    n = len(tiles(pr))
                    act.activation(E[:, pr % 2, 0:n, :], ps[:, 2 * (pr % 2):2 * (pr % 2) + n, :], ACT.Exp).then_inc(weighed, 1)

        @block.vector
        def _(dve):
            with dve.Fori(0, TC) as i:
                dve.wait_ge(used, (i + 1) * PAIRS)
                dve.tensor_copy(OA[:, bass.ds(i * 4, 4), :], ps[:, 4:8, 0:D + 1]).then_inc(sums_kept, 1)


def blend(nc, H, FA, OA, SQ):
    with ExitStack() as ctx:
        st = ctx.enter_context(nc.sbuf_tensor("blend_stat", [P, 2, NT], F32))
        zero = ctx.enter_context(nc.sbuf_tensor("blend_zero", [P, 1], F32))
        step, squared, rooted = (ctx.enter_context(nc.semaphore("blend_" + n)) for n in ("step", "squared", "rooted"))
        sq = SQ[:, 0:NT * D].rearrange("p (t d) -> p t d", d=D)
        block = ctx.enter_context(nc.Block())
        marks = {}

        @block.vector
        def _(dve):
            link = chain_of(dve, step)
            att = OA[:, :, 0:D]
            dve.memset(zero[:, :], 0.0)
            link(dve.reciprocal(st[:, 0:1, :].rearrange("p a t -> p t a"), OA[:, :, D:D + 1]))
            link(dve.tensor_scalar(st[:, 0, :], st[:, 0, :], 1.0 - 0.8, None, ALU.mult))
            link(dve.tensor_tensor(att, att, bc(st[:, 0, :], D), ALU.mult))
            marks["mixed"] = link(dve.scalar_tensor_tensor(out=att, in0=FA[:, :, 0:D], scalar=0.8, in1=att, op0=ALU.mult, op1=ALU.add))
            dve.wait_ge(squared, 1)
            marks["length"] = link(dve.tensor_reduce(st[:, 0, :], sq, AX.X, ALU.add))
            dve.wait_ge(rooted, 1)
            link(dve.tensor_scalar(st[:, 1, :], st[:, 0, :], 1e-12, None, ALU.max))
            link(dve.reciprocal(st[:, 0, :], st[:, 1, :]))
            link(dve.tensor_tensor(att, att, bc(st[:, 0, :], D), ALU.mult))
            link(dve.tensor_tensor(H[:, :, :], H[:, :, :], att, ALU.add))

        @block.scalar
        def _(act):
            act.wait_ge(step, marks["mixed"])
            act.activation(sq, OA[:, :, 0:D], ACT.Square).then_inc(squared, 1)
            act.wait_ge(step, marks["length"])
            act.activation(st[:, 0, :], st[:, 0, :], ACT.Sqrt, bias=zero[:, :]).then_inc(rooted, 1)


def route(nc, name, LG, tpr, coef, top):
    t = lambda n: tpr[:, TPR[n][0]:sum(TPR[n])]
    with ExitStack() as ctx:
        sb = lambda n, shape: ctx.enter_context(nc.sbuf_tensor(name + n, shape, F32))
        sem = lambda n: ctx.enter_context(nc.semaphore(name + n))
        PR, A, S1, S2 = (sb(n, [P, NT, EXPERTS]) for n in ("_prob", "_a", "_first", "_second"))
        st = sb("_stat", [P, NT])
        step, powered, counted = sem("_step"), sem("_powered"), sem("_counted")
        ps = ctx.enter_context(nc.psum_tensor(name + "_ps", [P, 4, CHUNK], F32))
        block = ctx.enter_context(nc.Block())
        marks = {}
        HALF = NT // 2 * EXPERTS
        rank = t("rank").unsqueeze(1).broadcast_to([P, NT, EXPERTS])

        @block.vector
        def _(dve):
            link = chain_of(dve, step)
            tt = lambda out, a, b, op: link(dve.tensor_tensor(out, a, b, op))
            lg = LG[:, :, 0:EXPERTS]
            pr, a, s1, s2 = (x[:, :, :] for x in (PR, A, S1, S2))
            link(dve.tensor_reduce(st[:, :], lg, AX.X, ALU.max))
            marks["shifted"] = tt(pr, lg, bc(st[:, :], EXPERTS), ALU.subtract)
            dve.wait_ge(powered, 1)
            link(dve.tensor_reduce(st[:, :], pr, AX.X, ALU.add))
            link(dve.reciprocal(st[:, :], st[:, :]))
            tt(pr, pr, bc(st[:, :], EXPERTS), ALU.mult)

            def pick(src, one_hot):
                link(dve.tensor_reduce(st[:, :], src, AX.X, ALU.max))
                tt(a, src, bc(st[:, :], EXPERTS), ALU.is_equal)
                tt(a, a, rank, ALU.mult)
                link(dve.tensor_reduce(st[:, :], a, AX.X, ALU.max))
                tt(one_hot, a, bc(st[:, :], EXPERTS), ALU.is_equal)

            pick(pr, s1)
            c = coef[:, :, :]
            if top == 2:
                link(dve.scalar_tensor_tensor(out=s2, in0=s1, scalar=-2.0, in1=pr, op0=ALU.mult, op1=ALU.add))
                pick(s2, c)
                tt(s1, s1, c, ALU.add)
                tt(c, s1, pr, ALU.mult)
                link(dve.tensor_reduce(st[:, :], c, AX.X, ALU.add))
                link(dve.tensor_scalar(st[:, :], st[:, :], 1e-12, None, ALU.max))
                link(dve.reciprocal(st[:, :], st[:, :]))
                tt(c, c, bc(st[:, :], EXPERTS), ALU.mult)
            else:
                marks["picked"] = step_now = tt(c, s1, pr, ALU.mult)
                dve.wait_ge(counted, 1)
                halves = lambda x: x.rearrange("p (h t) e -> p h (t e)", h=2)
                link(dve.tensor_copy(halves(s2), ps[:, 2:4, 0:HALF]))
                for e in range(EXPERTS):
                    last = dve.tensor_tensor_scan(a[:, :, e], s2[:, :, e], s2[:, :, e], 0.0, ALU.add, ALU.bypass)
                link(last)
                tt(a, a, s2, ALU.subtract)
                link(dve.tensor_tensor(halves(s2), ps[:, 0:2, 0:HALF], halves(a), ALU.add))
                link(dve.tensor_scalar(s2, s2, CAP + 0.5, None, ALU.is_lt))
                tt(c, c, s2, ALU.mult)

        @block.scalar
        def _(act):
            act.wait_ge(step, marks["shifted"])
            act.activation(PR[:, :, :], PR[:, :, :], ACT.Exp).then_inc(powered, 1)

        @block.tensor
        def _(pe):
            if top == 1:
                pe.wait_ge(step, marks["picked"])
                for h in range(2):
                    rows = S1[:, NT // 2 * h:NT // 2 * (h + 1), :].rearrange("p t e -> p (t e)")
                    pe.matmul(ps[:, h, 0:HALF], t("tri"), rows, start=True, stop=True)
                    mm = pe.matmul(ps[:, 2 + h, 0:HALF], t("ones"), rows, start=True, stop=True)
                mm.then_inc(counted, 1)


def experts(nc, name, XT, tpr, coef, YO, kt, func):
    t = lambda n: tpr[:, TPR[n][0]:sum(TPR[n])]
    pre = name[0]
    w1, b1, b2 = t(pre + "_w1"), t(pre + "_b1"), t(pre + "_b2")
    wide = TPR[pre + "_w2"][1] // kt
    w2 = t(pre + "_w2").rearrange("p (k n) -> p k n", k=kt)
    per = max(1, kt * wide // (EXPERTS * D))
    ones = t("ones")[0:1, :]
    with ExitStack() as ctx:
        sb = lambda n, shape: ctx.enter_context(nc.sbuf_tensor(name + n, shape, F32))
        sem = lambda n: ctx.enter_context(nc.semaphore(name + n))
        HH = sb("_hidden", [P, 2, kt, CHUNK])
        prod = sb("_prod", [P, 2, EXPERTS * D])
        XC = sb("_tokens", [D, 2, CHUNK])
        x_ready = sem("_x_ready")
        ps = ctx.enter_context(nc.psum_tensor(name + "_ps", [P, 8, CHUNK], F32))
        hidden_mm, hidden, y_mm, scaled, reduced = (sem("_" + n) for n in ("hidden_mm", "hidden", "y_mm", "scaled", "reduced"))
        block = ctx.enter_context(nc.Block())

        @block.tensor
        def _(pe):
            with pe.Fori(0, TC // 2) as i:
                for s in range(2):
                    c = 2 * i + s
                    pe.wait_ge(x_ready, c + 1)
                    for k in range(kt):
                        if k >= 4:
                            pe.wait_ge(hidden, c * kt + k - 3)
                        pe.matmul(ps[:, k % 4, :], w1[0:D, P * k:P * k + P], XC[:, s, :], start=True, stop=True).then_inc(hidden_mm, 1)
                    pe.wait_ge(hidden, c * kt + kt)
                    for j in range(4):
                        if s > 0 or j >= 4:
                            pe.wait_ge(scaled, c * 4 + j - 3)
                        else:
                            pe.wait_ge(scaled, i * 8)
                        for k in range(kt):
                            out = ps[:, 4 + j, wide * (k // per):wide * (k // per) + wide]
                            if k % per == 0:
                                pe.matmul(out, ones, b2[0:1, wide * (k // per):wide * (k // per) + wide], start=True, stop=False)
                            mm = pe.matmul(out, HH[:, s, k, P * j:P * j + P], w2[:, k, :], start=False, stop=(k % per == per - 1))
                        mm.then_inc(y_mm, 1)

        @block.gpsimd
        def _(pool):
            with pool.Fori(0, TC // 2) as i:
                for s in range(2):
                    pool.wait_ge(hidden_mm, i * (2 * kt))
                    pool.tensor_copy(XC[:, s, :], XT[0:D, bass.ds((2 * i + s) * CHUNK, CHUNK)]).then_inc(x_ready, 1)

        @block.scalar
        def _(act):
            with act.Fori(0, TC // 2) as i:
                for s in range(2):
                    c = 2 * i + s
                    act.wait_ge(y_mm, i * 8)
                    for k in range(kt):
                        act.wait_ge(hidden_mm, c * kt + k + 1)
                        act.activation(HH[:, s, k, :], ps[:, k % 4, :], func, bias=b1[:, k:k + 1]).then_inc(hidden, 1)

        @block.vector
        def _(dve):
            with dve.Fori(0, TC // 2) as i:
                for s in range(2):
                    for j in range(4):
                        n = (2 * i + s) * 4 + j
                        dve.wait_ge(y_mm, n + 1)
                        dve.tensor_tensor(prod[:, j % 2, :].rearrange("p (e d) -> p e d", d=D), ps[:, 4 + j, :].rearrange("p (e d) -> p e d", d=D),
                                          coef[:, bass.ds(n, 1), :].rearrange("p a e -> p (a e)").unsqueeze(2).broadcast_to([P, EXPERTS, D]), ALU.mult).then_inc(scaled, 1)
                        dve.wait_ge(scaled, n + 1)
                        dve.tensor_reduce(YO[:, bass.ds(n, 1), 0:D].rearrange("p a d -> p (a d)"),
                                          prod[:, j % 2, :].rearrange("p (e d) -> p d e", d=D), AX.X, ALU.add).then_inc(reduced, 1)


def add_to(nc, name, H, parts, guard=False):
    with ExitStack() as ctx:
        step = ctx.enter_context(nc.semaphore(name + "_step"))
        mask = ctx.enter_context(nc.sbuf_tensor(name + "_mask", [P, NT, D], mybir.dt.uint8)) if guard else None
        fill = ctx.enter_context(nc.sbuf_tensor(name + "_fill", [P, 3], F32)) if guard else None
        block = ctx.enter_context(nc.Block())

        @block.vector
        def _(dve):
            link = chain_of(dve, step)
            if guard:
                y = parts[0]
                top = float(np.finfo(np.float32).max)
                for n, (value, test) in enumerate(((0.0, None), (10000.0, ALU.is_gt), (-10000.0, ALU.is_lt))):
                    link(dve.memset(fill[:, n:n + 1], value))
                    if test is None:
                        link(dve.tensor_tensor(mask[:, :, :], y, y, ALU.not_equal))
                    else:
                        link(dve.tensor_scalar(mask[:, :, :], y, top if value > 0 else -top, None, test))
                    link(dve.copy_predicated(y, mask[:, :, :], fill[:, n:n + 1].unsqueeze(2).broadcast_to([P, NT, D])))
            for part in parts:
                link(dve.tensor_tensor(H[:, :, :], H[:, :, :], part, ALU.add))


def head_attention(nc, XT, tpr, att):
    t = lambda n: tpr[:, TPR[n][0]:sum(TPR[n])]
    with ExitStack() as ctx:
        sb = lambda n, shape, dt=F32: ctx.enter_context(nc.sbuf_tensor("mha_" + n, shape, dt))
        sem = lambda n: ctx.enter_context(nc.semaphore("mha_" + n))
        xb = sb("xb", [D + 1, 2, SEQ])
        QK = sb("qk", [P, 2, SEQ])
        V = sb("v", [Q_ROWS, 2, HEADS, HD + 1])
        S = sb("s", [Q_ROWS, 2 * HEADS, SEQ])
        PT = sb("pt", [Q_ROWS, 2, 2, HEADS * Q_ROWS])
        mx = sb("mx", [Q_ROWS, 2 * HEADS])
        rc = sb("rc", [Q_ROWS, 2 * HEADS])
        OB = sb("ob", [Q_ROWS, 2 * HEADS, HD], BF16)
        OF = sb("of", [Q_ROWS, 2, 2, D])
        ps = ctx.enter_context(nc.psum_tensor("mha_ps", [P, 8, CHUNK], F32))
        (ones_set, x_ready, qkv, qk_kept, v_kept, scored, maxed, shifted, weighed, turned, pt_kept, mixed, inverted,
         rounded, widened, sent) = (sem(n) for n in (
             "ones_set x_ready qkv qk_kept v_kept scored maxed shifted weighed turned pt_kept mixed inverted rounded widened sent").split())
        block = ctx.enter_context(nc.Block())
        PAIRS = BATCH // 2
        rows = att.rearrange("(b s) d -> b s d", s=SEQ)
        sv = ps[0:Q_ROWS, 0:4, 0:2 * SEQ].rearrange("p h (n m) -> p h n m", n=2)
        ov = ps[0:Q_ROWS, 0, 0:2 * HEADS * (HD + 1)].rearrange("p (n f) -> p n f", f=HD + 1)

        @block.gpsimd
        def _(pool):
            with pool.Fori(0, PAIRS) as i:
                for s in range(2):
                    b = 2 * i + s
                    pool.wait_ge(qkv, i * 2)
                    pool.tensor_copy(xb[:, s, :], XT[0:D + 1, bass.ds(b * SEQ, SEQ)]).then_inc(x_ready, 1)

        @block.tensor
        def _(pe):
            pe.wait_ge(ones_set, 1)
            with pe.Fori(0, PAIRS) as i:
                for s in range(2):
                    b = 2 * i + s
                    pe.wait_ge(x_ready, b + 1)
                    pe.wait_ge(pt_kept, b * 2)
                    x = xb[:, s, :]
                    pe.matmul(ps[:, 4, 0:SEQ], t("wq")[0:D + 1, :], x, start=True, stop=True)
                    pe.matmul(ps[:, 4, 256:256 + SEQ], t("wk")[0:D + 1, :], x, start=True, stop=True)
                    for m in range(2):
                        mm = pe.matmul(ps[0:M_ROWS[m], 5, D * m:D * m + D], x[:, Q_ROWS * m:Q_ROWS * m + M_ROWS[m]], t("wv")[0:D + 1, :], start=True, stop=True)
                    mm.then_inc(qkv, 1)
                    pe.wait_ge(qk_kept, b + 1)
                    pe.wait_ge(inverted, b)
                    pe.wait_ge(rounded, b)
                    for n in range(2):
                        q0 = (SEQ - Q_ROWS) * n
                        for h in range(HEADS):
                            mm = pe.matmul(ps[0:Q_ROWS, h, SEQ * n:SEQ * n + SEQ],
                                           QK[32 * h:32 * h + 32, 0, q0:q0 + Q_ROWS], QK[32 * h:32 * h + 32, 1, :], start=True, stop=True)
                    mm.then_inc(scored, 1)
                    pe.wait_ge(weighed, b + 1)
                    pe.wait_ge(v_kept, b + 1)
                    for m in range(2):
                        for n in range(2):
                            for h in range(HEADS):
                                mm = pe.transpose(ps[0:M_ROWS[m], 4 + 2 * m + n, Q_ROWS * h:Q_ROWS * h + Q_ROWS],
                                                  S[:, 2 * h + n, Q_ROWS * m:Q_ROWS * m + M_ROWS[m]], t("eye")[0:Q_ROWS, 0:Q_ROWS])
                        mm.then_inc(turned, 1)
                    pe.wait_ge(pt_kept, b * 2 + 2)
                    for n in range(2):
                        for h in range(HEADS):
                            for m in range(2):
                                mm = pe.matmul(ov[:, HEADS * n + h, :], PT[0:M_ROWS[m], m, n, Q_ROWS * h:Q_ROWS * h + Q_ROWS], V[0:M_ROWS[m], m, h, :],
                                               start=(m == 0), stop=(m == 1))
                    mm.then_inc(mixed, 1)

        @block.scalar
        def _(act):
            with act.Fori(0, PAIRS) as i:
                for s in range(2):
                    b = 2 * i + s
                    act.wait_ge(qkv, b + 1)
                    act.wait_ge(scored, b)
                    act.copy(QK[:, :, :], ps[:, 4, :].rearrange("p (a n) -> p a n", a=2)[:, :, 0:SEQ]).then_inc(qk_kept, 1)
                    act.wait_ge(shifted, b + 1)
                    act.activation(S[:, :, :], S[:, :, :], ACT.Exp, scale=HD ** -0.5).then_inc(weighed, 1)
                    act.wait_ge(turned, b * 2 + 1)
                    act.copy(PT[0:M_ROWS[0], 0, :, :], ps[0:M_ROWS[0], 4:6, 0:HEADS * Q_ROWS]).then_inc(pt_kept, 1)

        @block.vector
        def _(dve):
            dve.memset(V[:, :, :, :], 1.0).then_inc(ones_set, 1)
            dve.wait_ge(ones_set, 1)
            with dve.Fori(0, PAIRS) as i:
                for s in range(2):
                    b = 2 * i + s
                    dve.wait_ge(qkv, b + 1)
                    for m in range(2):
                        last = dve.tensor_copy(V[0:M_ROWS[m], m, :, 0:HD], ps[0:M_ROWS[m], 5, D * m:D * m + D].rearrange("p (h f) -> p h f", f=HD))
                    last.then_inc(v_kept, 1)
                    dve.wait_ge(scored, b + 1)
                    dve.tensor_reduce(mx[:, :].rearrange("p (h n) -> p h n", n=2), sv, AX.X, ALU.max).then_inc(maxed, 1)
                    dve.wait_ge(maxed, b + 1)
                    dve.tensor_tensor(S[:, :, :].rearrange("p (h n) m -> p h n m", n=2), sv,
                                      mx[:, :].rearrange("p (h n) -> p h n", n=2).unsqueeze(3).broadcast_to([Q_ROWS, 4, 2, SEQ]), ALU.subtract).then_inc(shifted, 1)
                    dve.wait_ge(turned, b * 2 + 2)
                    dve.tensor_copy(PT[0:M_ROWS[1], 1, :, :], ps[0:M_ROWS[1], 6:8, 0:HEADS * Q_ROWS]).then_inc(pt_kept, 1)
                    dve.wait_ge(mixed, b + 1)
                    dve.reciprocal(rc[:, :].unsqueeze(2), ov[:, :, HD:HD + 1]).then_inc(inverted, 1)
                    dve.wait_ge(inverted, b + 1)
                    dve.tensor_tensor(OB[:, :, :], ov[:, :, 0:HD], bc(rc[:, :], HD), ALU.mult).then_inc(rounded, 1)
                    dve.wait_ge(rounded, b + 1)
                    dve.wait_ge(sent, i * 64)
                    dve.tensor_copy(OF[:, s, :, :].rearrange("p n d -> p (n d)"), OB[:, :, :].rearrange("p n f -> p (n f)")).then_inc(widened, 1)

        @block.sync
        def _(sp):
            with sp.Fori(0, PAIRS) as i:
                for s in range(2):
                    b = 2 * i + s
                    sp.wait_ge(widened, b + 1)
                    row = rows[bass.ds(b, 1), :, :].rearrange("a s d -> (a s) d")
                    sp.dma_start(row[0:Q_ROWS, :], OF[:, s, 0, :]).then_inc(sent, 16)
                    sp.dma_start(row[Q_ROWS:SEQ, :], OF[1:Q_ROWS, s, 1, :]).then_inc(sent, 16)
            sp.wait_ge(sent, 32 * BATCH)


def token_stages(nc, din, hid, att, result, upto=9):
    with ExitStack() as ctx:
        sb = lambda n, shape: ctx.enter_context(nc.sbuf_tensor(n, shape, F32))
        tpr = sb("tpr", [P, TPR_W])
        H = sb("H", [P, NT, D])
        X = sb("X", [P, NT, D])
        A = sb("A", [P, NT, D + 1])
        B = sb("B", [P, NT, D + 1])
        XT = sb("XT", [D + 1, NT * P])
        coef = sb("coef", [P, NT, EXPERTS])
        SQ = B[:, :, :].rearrange("p t d -> p (t d)")
        load_tokens(nc, "first", hid, H, (tpr[:, :], din["tokprm"]))
        if upto >= 1:
            token_norm(nc, "n0", H, X, SQ, unit=A)
            turn_tokens(nc, "t0", A, tpr, XT=XT)
            global_attention(nc, A, XT, B)
            blend(nc, H, A, B, X[:, :, :].rearrange("p t d -> p (t d)"))
        if upto >= 2:
            token_norm(nc, "n1", H, X, SQ)
            turn_tokens(nc, "t1", X, tpr, XT=XT, weight="router", out=A)
            route(nc, "r1", A, tpr, coef, 2)
            experts(nc, "moe", XT, tpr, coef, B, 4, ACT.Gelu)
            add_to(nc, "a1", H, [X[:, :, :], B[:, :, 0:D]])
        if upto >= 3:
            token_norm(nc, "n2", H, X, SQ, clip=10000.0)
            turn_tokens(nc, "t2", X, tpr, XT=XT)
            head_attention(nc, XT, tpr, att)
            load_tokens(nc, "second", att, X)
            turn_tokens(nc, "t3", X, tpr, weight="wo", out=A)
            add_to(nc, "a2", H, [A[:, :, 0:D]])
        if upto >= 4:
            token_norm(nc, "n3", H, X, SQ)
            turn_tokens(nc, "t4", X, tpr, XT=XT, weight="gate", out=A)
            route(nc, "r4", A, tpr, coef, 1)
            experts(nc, "ffn", XT, tpr, coef, B, 16, ACT.Relu)
            add_to(nc, "a3", H, [B[:, :, 0:D]], guard=True)
        with nc.semaphore("result_stored") as stored, nc.Block() as block:
            @block.sync
            def _(sp):
                sp.dma_start(result[0:FULL_T * P, :].rearrange("(t p) d -> p t d", p=P), H[:, 0:FULL_T, :]).then_inc(stored, 16)
                sp.dma_start(result[FULL_T * P:TOK, :], H[0:REST, FULL_T, :]).then_inc(stored, 16)
                sp.wait_ge(stored, 32)


def program(nc, din, result):
    spec_ready = nc.dram_tensor("spec_ready", (LAYERS, P, MODES * MODES * 2 * CH), F32, kind="Internal").ap()
    hid = nc.dram_tensor("hid", (TOK, D), F32, kind="Internal").ap()
    att = nc.dram_tensor("att", (TOK, D), F32, kind="Internal").ap()
    with ExitStack() as ctx:
        sb = lambda name, shape: ctx.enter_context(nc.sbuf_tensor(name, shape, F32))
        prm = sb("prm", [P, PRM_W])
        tab = sb("tab", [P, TABLES.shape[1]])
        fc0c = sb("fc0_centered", [3 * TILE_IMG, P])
        operator_setup(nc, din, spec_ready, prm, tab, fc0c)
        operator(nc, din, spec_ready, hid, prm, tab, fc0c)
    token_stages(nc, din, hid, att, result)


def kernel(**inputs):
    import concourse.bacc as bacc
    from concourse.bass_utils import run_bass_kernel_spmd

    i = {k: np.asarray(v) for k, v in inputs.items()}
    host = {**layout_operator(i), **layout_tokens(i), "txt": i["txt"].reshape(BATCH, TXT * D)}
    nc = bacc.Bacc("TRN2", target_bir_lowering=False, num_devices=1)
    arrays = {f"in_{k}": np.ascontiguousarray(v) for k, v in host.items()}
    din = {k: nc.dram_tensor(f"in_{k}", v.shape, F32, kind="ExternalInput").ap() for k, v in host.items()}
    result = nc.dram_tensor("result", (TOK, D), F32, kind="ExternalOutput").ap()
    program(nc, din, result)
    r = run_bass_kernel_spmd(nc, [arrays], core_ids=[0])
    return r.results[0]["result"].reshape(BATCH, SEQ, D)
```

```python
from contextlib import ExitStack

import numpy as np

import concourse.bass as bass
from concourse import mybir

F32 = mybir.dt.float32
BF16 = mybir.dt.bfloat16
ALU = mybir.AluOpType
ACT = mybir.ActivationFunctionType
AX = mybir.AxisListType

P = 128
BATCH, SIDE, CH = 64, 64, 32
LAYERS, MODES = 4, 12
PIX = SIDE * SIDE
OCT = 8
TILE_IMG = P // CH
TILES = OCT // TILE_IMG
N_OCT = BATCH // OCT
NORMS = LAYERS + 1
CHUNK = 512
CHUNKS = PIX // CHUNK
KRI = 2 * MODES
HBLK = 4
N_HBLK = SIDE // HBLK
TXT = 77
SEQ = SIDE + TXT
D = 64
TOK = BATCH * SEQ
NT = 72
FULL_T = TOK // P
REST = TOK - FULL_T * P
LN_EPS = 1e-5


def fourier_tables():
    n = np.arange(SIDE)
    ky = np.arange(MODES)
    kx = np.concatenate([np.arange(MODES), np.arange(SIDE - MODES, SIDE)])
    aw = 2 * np.pi * np.outer(n, ky) / SIDE
    ah = 2 * np.pi * np.outer(n, kx) / SIDE
    fw = np.zeros((2, TILE_IMG, 32, MODES, 2, TILE_IMG))
    for half in range(2):
        a = aw[32 * half:32 * half + 32]
        for b in range(TILE_IMG):
            fw[half, b, :, :, 0, b] = np.cos(a)
            fw[half, b, :, :, 1, b] = -np.sin(a)
    fh = np.zeros((2, TILES, SIDE, TILES, 2, 2, MODES))
    c, s = np.cos(ah).reshape(SIDE, 2, MODES), np.sin(ah).reshape(SIDE, 2, MODES)
    for g in range(TILES):
        fh[0, g, :, g, :, 0], fh[0, g, :, g, :, 1] = c, -s
        fh[1, g, :, g, :, 0], fh[1, g, :, g, :, 1] = s, c
    ih = np.zeros((2, 2, 32, SIDE, 2))
    for st in range(2):
        ih[st, 0, :MODES, :, 0], ih[st, 0, :MODES, :, 1] = c[:, st].T, s[:, st].T
        ih[st, 1, :MODES, :, 0], ih[st, 1, :MODES, :, 1] = -s[:, st].T, c[:, st].T
    iw = np.zeros((HBLK, MODES, 2, HBLK, SIDE))
    weight = np.where(ky == 0, 1.0, 2.0)[:, None] / PIX
    for h in range(HBLK):
        iw[h, :, 0, h] = weight * np.cos(aw).T
        iw[h, :, 1, h] = -weight * np.sin(aw).T
    eye = np.eye(P)
    mean = np.kron(np.eye(TILE_IMG), np.full((CH, CH), 1.0 / CH))
    sign = np.ones((P, 1))
    sign[32:64], sign[96:128] = -1.0, -1.0
    parts = {
        "fw0": fw[0].reshape(P, -1), "fw1": fw[1].reshape(P, -1),
        "fh0": fh[0].reshape(P, -1), "fh1": fh[1].reshape(P, -1),
        "ih": ih.reshape(P, -1), "iw": np.pad(iw.reshape(HBLK * KRI, -1), ((0, P - HBLK * KRI), (0, 0))),
        "eye": eye, "mean": mean, "center": eye - mean, "sign": sign,
    }
    at, n = {}, 0
    for name, a in parts.items():
        at[name] = (n, a.shape[1])
        n += a.shape[1]
    return np.concatenate(list(parts.values()), axis=1).astype(np.float32), at


TABLES, TABLE_AT = fourier_tables()
PRM = {}
_n = 0
for _name, _w in (("bias", NORMS), ("gain", NORMS), ("shift", NORMS), ("fc1b", 1), ("fc2b", 1), ("fc3b", 1),
                  ("fc0", 3 * TILE_IMG), ("conv", LAYERS * P), ("fc1", 128), ("fc2", 64), ("fc3", 2)):
    PRM[_name] = (_n, _w)
    _n += _w
PRM_W = _n


def layout_operator(i):
    p = np.zeros((P, PRM_W), np.float32)

    def put(name, a):
        n, w = PRM[name]
        p[:, n:n + w] = a

    def four(v):
        return np.tile(v, TILE_IMG)

    put("bias", np.stack([four(i["L0_tok_fc0_b"])] + [four(v) for v in i["L0_tok_conv_b"]], 1))
    put("gain", np.stack([four(i["L0_tok_ln0_g"])] + [four(v) for v in i["L0_tok_ln_g"]], 1))
    put("shift", np.stack([four(i["L0_tok_ln0_b"])] + [four(v) for v in i["L0_tok_ln_b"]], 1))
    put("fc1b", i["L0_tok_fc1_b"][:, None])
    put("fc2b", np.tile(i["L0_tok_fc2_b"], 2)[:, None])
    put("fc3b", np.broadcast_to(i["L0_tok_fc3_b"][None, :], (P, 1)))
    fc0 = np.zeros((TILE_IMG, CH, TILE_IMG, 3), np.float32)
    conv = np.zeros((TILE_IMG, CH, LAYERS, TILE_IMG, CH), np.float32)
    for b in range(TILE_IMG):
        fc0[b, :, b, :] = i["L0_tok_fc0_w"].T
        conv[b, :, :, b, :] = i["L0_tok_conv_w"].transpose(1, 0, 2)
    put("fc0", fc0.reshape(P, -1))
    put("conv", conv.reshape(P, -1))
    put("fc1", np.tile(i["L0_tok_fc1_w"], (TILE_IMG, 1)))
    put("fc2", i["L0_tok_fc2_w"])
    fc3 = np.zeros((2, 64, 2), np.float32)
    for s in range(2):
        fc3[s, :, s] = i["L0_tok_fc3_w"][:, 0]
    put("fc3", fc3.reshape(P, 2))
    w = np.empty((LAYERS, 2, 2, CH, MODES, MODES, 2, CH), np.float32)
    for st, (re, im) in enumerate((("L0_tok_w1r", "L0_tok_w1i"), ("L0_tok_w2r", "L0_tok_w2i"))):
        r = i[re].transpose(0, 1, 4, 3, 2)
        m = i[im].transpose(0, 1, 4, 3, 2)
        w[:, st, 0, :, :, :, 0], w[:, st, 0, :, :, :, 1] = r, m
        w[:, st, 1, :, :, :, 0], w[:, st, 1, :, :, :, 1] = m, r
    x = i["x"].transpose(0, 3, 1, 2).reshape(N_OCT, TILES, TILE_IMG * 3, PIX)
    return {"tables": TABLES, "prm": p, "spec": w.reshape(LAYERS, P, MODES * MODES * 2 * CH), "pix": x}


def operator_setup(nc, din, spec_ready, prm, tab, fc0c):
    SPEC_W = MODES * MODES * 2 * CH
    t = lambda name: tab[:, TABLE_AT[name][0]:sum(TABLE_AT[name])]
    q = lambda name: prm[:, PRM[name][0]:sum(PRM[name])]
    with ExitStack() as ctx:
        sb = lambda name, shape: ctx.enter_context(nc.sbuf_tensor(name, shape, F32))
        sem = lambda name: ctx.enter_context(nc.semaphore(name))
        raw = sb("spec_raw", [P, SPEC_W])
        done = sb("spec_done", [P, SPEC_W])
        mean = sb("spec_mean", [P, SPEC_W // CH])
        ps = ctx.enter_context(nc.psum_tensor("setup_ps", [P, 2, CHUNK], F32))
        tables_in, spec_in = sem("tables_in"), sem("spec_in")
        centered, center_kept = sem("centered"), sem("center_kept")
        signed, summed, scaled, finished, stored = (sem(n) for n in ("signed", "summed", "scaled", "finished", "stored"))
        block = ctx.enter_context(nc.Block())

        @block.sync
        def _(sp):
            sp.dma_start(prm[:, :], din["prm"]).then_inc(tables_in, 16)
            sp.dma_start(tab[:, :], din["tables"]).then_inc(tables_in, 16)
            with sp.Fori(0, LAYERS) as layer:
                sp.wait_ge(finished, layer)
                sp.dma_start(raw[:, :], din["spec"][bass.ds(layer, 1), :, :].rearrange("a p n -> (a p) n")).then_inc(spec_in, 16)
            sp.wait_ge(stored, 16 * LAYERS)

        @block.scalar
        def _(act):
            with act.Fori(0, LAYERS) as layer:
                act.wait_ge(finished, layer + 1)
                act.dma_start(spec_ready[bass.ds(layer, 1), :, :].rearrange("a p n -> (a p) n"), done[:, :]).then_inc(stored, 16)

        @block.vector
        def _(dve):
            dve.wait_ge(centered, 1)
            dve.tensor_copy(q("conv"), ps[:, 0, :]).then_inc(center_kept, 1)
            dve.tensor_copy(q("bias"), ps[:, 1, 0:NORMS]).then_inc(center_kept, 1)
            dve.tensor_copy(fc0c[:, :], ps[0:3 * TILE_IMG, 1, P:2 * P]).then_inc(center_kept, 1)
            with dve.Fori(0, LAYERS) as layer:
                dve.wait_ge(spec_in, layer * 16 + 16)
                re_out = raw[:, :].rearrange("p (m r o) -> p m r o", r=2, o=CH)[:, :, 0, :]
                dve.tensor_scalar(re_out, re_out, t("sign"), None, ALU.mult).then_inc(signed, 1)
                dve.wait_ge(signed, layer + 1)
                rows = raw[:, :].rearrange("p (m o) -> p m o", o=CH)
                dve.tensor_reduce(mean[:, :], rows, AX.X, ALU.add).then_inc(summed, 1)
                dve.wait_ge(summed, layer + 1)
                dve.tensor_scalar(mean[:, :], mean[:, :], 1.0 / CH, None, ALU.mult).then_inc(scaled, 1)
                dve.wait_ge(scaled, layer + 1)
                dve.wait_ge(stored, layer * 16)
                dve.tensor_tensor(done[:, :].rearrange("p (m o) -> p m o", o=CH), rows,
                                  mean[:, :].unsqueeze(2).broadcast_to([P, SPEC_W // CH, CH]), ALU.subtract).then_inc(finished, 1)

        @block.tensor
        def _(pe):
            pe.wait_ge(tables_in, 32)
            for layer in range(LAYERS):
                pe.matmul(ps[:, 0, P * layer:P * layer + P], q("conv")[:, P * layer:P * layer + P], t("center"), start=True, stop=True)
            pe.matmul(ps[:, 1, 0:NORMS], t("center"), q("bias"), start=True, stop=True)
            pe.matmul(ps[0:3 * TILE_IMG, 1, P:2 * P], q("fc0"), t("center"), start=True, stop=True).then_inc(centered, 1)


def operator(nc, din, spec_ready, hid, prm, tab, fc0c, n_oct=N_OCT):
    t = lambda name: tab[:, TABLE_AT[name][0]:sum(TABLE_AT[name])]
    q = lambda name, rows=P: prm[0:rows, PRM[name][0]:sum(PRM[name])]
    tok = hid.rearrange("(b s) d -> b (s d)", s=SEQ)
    with ExitStack() as ctx:
        sb = lambda name, shape: ctx.enter_context(nc.sbuf_tensor(name, shape, F32))
        sem = lambda name: ctx.enter_context(nc.semaphore(name))
        Z = sb("Z", [P, TILES, PIX])
        ZW = sb("ZW", [P, TILES, PIX])
        WS = sb("WS", [P, MODES * MODES, 2 * CH])
        MB = sb("MB", [P, MODES * MODES, 2, OCT])
        Y = sb("Y", [P, MODES, OCT, 32])
        YT = sb("YT", [P, MODES, OCT, 32])
        U = sb("U", [P, KRI, TILE_IMG, CH])
        T = sb("T", [P, TILES, SIDE, MODES, 2])
        TT = sb("TT", [HBLK * KRI, TILES, N_HBLK, P])
        SQ = sb("SQ", [P, 4, CHUNK])
        RS = sb("RS", [P, 4, CHUNK])
        conv = sb("conv_now", [P, P])
        vecs = sb("vecs_now", [P, 4])
        epsb = sb("epsb", [P, 1])
        OUT = TT[0:2, :, :, :].rearrange("p t a n -> p (t a n)")
        PS = ctx.enter_context(nc.psum_tensor("PS", [P, 8, CHUNK], F32))
        psf = PS[:, :, :].rearrange("p a n -> p (a n)")
        (pix_in, weights_in, prepared, vecs_ready, conv_ready, y_done, sq_done, var_done, std_done, inv_done, norm_done,
         z_done, turned, u_mm, u_kept, v_mm, v_kept, mix_mm, mix_kept, y_turned, t_mm, t_kept, tt_mm, tt_kept,
         fc1_mm, fc1_act, fc2_mm, fc2_act, fc3_mm, fc3_kept, out_sent, text_sent) = (sem(n) for n in (
             "pix_in weights_in prepared vecs_ready conv_ready y_done sq_done var_done std_done inv_done norm_done z_done "
             "turned u_mm u_kept v_mm v_kept mix_mm mix_kept y_turned t_mm t_kept tt_mm tt_kept fc1_mm fc1_act fc2_mm "
             "fc2_act fc3_mm fc3_kept out_sent text_sent").split())
        NCH = TILES * CHUNKS
        PAIRS = OCT // 2
        NM = PAIRS * CHUNKS
        cols = lambda c: slice((c % CHUNKS) * CHUNK, (c % CHUNKS + 1) * CHUNK)
        H1 = [SQ[:, 0:2, :], SQ[:, 2:4, :]]
        H2 = [RS[:, 0, :], RS[:, 1, :]]

        def keep_modes(copy, y0, y1):
            for img in range(TILE_IMG):
                for st in range(2):
                    for ri in range(2):
                        src = psf[32 * img:32 * img + 32, P * y0:P * y1].rearrange("p (y n) -> p y n", n=P)[:, :, 0:96]
                        src = src.rearrange("p y (g s r x) -> p y g s r x", g=2, s=2, r=2)[:, :, :, st, ri, :]
                        at = 64 * st + 32 * ri
                        dst = MB[at:at + 32, MODES * y0:MODES * y1, st, :].rearrange("p (y x) (g i) -> p y g i x", x=MODES, i=TILE_IMG)[:, :, :, img, :]
                        last = copy(dst, src)
            return last

        def keep_mix(copy, part, st):
            src = psf[0:2 * CH, (3 - 3 * part) * CHUNK:(6 - 3 * part) * CHUNK].rearrange("p (y n) -> p y n", n=256)[:, :, 0:192]
            src = src.rearrange("p y (x s b) -> p y x s b", x=MODES, s=2)[:, :, :, st, :]
            dst = Y[64 * st:64 * st + 64, 6 * part:6 * part + 6, :, 0:MODES].rearrange("p y b x -> p y x b")
            return copy(dst, src)

        def keep_t(copy, g):
            src = psf[:, (3 - 3 * g) * CHUNK:(6 - 3 * g) * CHUNK].rearrange("p (y h r) -> p y h r", h=SIDE, r=2)
            return copy(T[:, g, :, :, :].rearrange("p h y r -> p y h r"), src)

        block = ctx.enter_context(nc.Block())

        @block.sync
        def _(sp):
            for b in range(4):
                sp.dma_start(tok[16 * b:16 * b + 16, SIDE * D:], din["txt"][16 * b:16 * b + 16, :]).then_inc(text_sent, 16)
            with sp.Fori(0, n_oct) as octet:
                sp.wait_ge(fc3_kept, octet * NM)
                sp.dma_start(ZW[0:3 * TILE_IMG, :, :], din["pix"][bass.ds(octet, 1), :, :, :].rearrange("a t p n -> p (a t) n")).then_inc(pix_in, 16)
                with sp.Fori(0, LAYERS) as layer:
                    sp.wait_ge(mix_mm, (octet * LAYERS + layer) * 2)
                    sp.dma_start(WS[:, :, :], spec_ready[bass.ds(layer, 1), :, :].rearrange("a p (m n) -> p (a m) n", n=2 * CH)).then_inc(weights_in, 16)
                for pair in range(PAIRS):
                    sp.wait_ge(fc3_kept, octet * NM + (pair + 1) * CHUNKS)
                    sp.dma_start(tok[bass.ds(octet * OCT + 2 * pair, 2), 0:PIX], OUT).then_inc(out_sent, 16)
            sp.wait_ge(out_sent, 16 * PAIRS * n_oct)
            sp.wait_ge(text_sent, 64)

        @block.tensor
        def _(pe):
            def norm(n, make):
                for c in range(NCH + 1):
                    if c < NCH:
                        if c >= 4:
                            pe.wait_ge(norm_done, n * NCH + c - 3)
                        make(c).then_inc(y_done, 1)
                    if c >= 1:
                        v = c - 1
                        if v >= 4:
                            pe.wait_ge(std_done, n * NCH + v - 3)
                        pe.wait_ge(sq_done, n * NCH + v + 1)
                        pe.matmul(PS[:, 4 + v % 4, :], t("mean"), SQ[:, v % 4, :], start=True, stop=True).then_inc(var_done, 1)

            def first(c):
                return pe.matmul(PS[:, c % 4, :], fc0c[:, :], ZW[0:3 * TILE_IMG, c // CHUNKS, cols(c)], start=True, stop=True)

            def layer_step(it, n):
                pe.wait_ge(turned, (it + 1) * TILES)
                for c in range(CH):
                    for half in range(2):
                        z = ZW[:, :, :].rearrange("p t (h v c) -> p t h v c", v=2, c=CH)[:, :, :, half, c]
                        mm = pe.matmul(PS[:, c // 4, 96 * (c % 4):96 * (c % 4) + 96], z, t(f"fw{half}"), start=(half == 0), stop=(half == 1))
                    if c % 4 == 3:
                        mm.then_inc(u_mm, 1)
                pe.wait_ge(u_kept, (it + 1) * 8)
                for ky in range(MODES):
                    for ri in range(2):
                        mm = pe.matmul(psf[:, P * ky:P * ky + 96], U[:, 2 * ky + ri, :, :], t(f"fh{ri}"), start=(ri == 0), stop=(ri == 1))
                    if ky % 4 == 3:
                        mm.then_inc(v_mm, 1)
                pe.wait_ge(weights_in, it * 16 + 16)
                pe.wait_ge(v_kept, (it + 1) * 2)
                for part in range(2):
                    for m in range(72 * part, 72 * part + 72):
                        at = (3 - 3 * part) * CHUNK + 256 * (m // 12 - 6 * part) + 16 * (m % 12)
                        mm = pe.matmul(psf[0:2 * CH, at:at + 16], WS[:, m, :], MB[:, m, :, :], start=True, stop=True)
                    mm.then_inc(mix_mm, 1)
                pe.wait_ge(y_turned, it + 1)
                for g in range(TILES):
                    for ky in range(MODES):
                        at = (3 - 3 * g) * CHUNK + P * ky
                        mm = pe.matmul(psf[:, at:at + P], YT[:, ky, TILE_IMG * g:TILE_IMG * (g + 1), :], t("ih"), start=True, stop=True)
                    mm.then_inc(t_mm, 1)
                pe.wait_ge(t_kept, (it + 1) * 2)
                for u in range(TILES * N_HBLK // 4):
                    g = u // 4
                    for k in range(4):
                        hb = 4 * (u % 4) + k
                        src = T[:, g, HBLK * hb:HBLK * (hb + 1), :, :].rearrange("p h k r -> p (h k r)")
                        mm = pe.transpose(PS[0:HBLK * KRI, u, P * k:P * k + P], src, t("eye"))
                    mm.then_inc(tt_mm, 1)
                pe.wait_ge(tt_kept, (it + 1) * 8)
                pe.wait_ge(conv_ready, it + 1)

                def both(c):
                    g, j = c // CHUNKS, c % CHUNKS
                    for k in range(2):
                        half = PS[:, c % 4, 256 * k:256 * k + 256]
                        pe.matmul(half, conv[:, :], Z[:, g, CHUNK * j + 256 * k:CHUNK * j + 256 * k + 256], start=True, stop=False)
                        mm = pe.matmul(half, TT[:, g, 2 * j + k, :], t("iw")[0:HBLK * KRI, :], start=False, stop=True)
                    return mm

                norm(n, both)

            def mlp(octet):
                b = octet * NM
                for i in range(NM + 2):
                    pair, j = i // CHUNKS, i % CHUNKS
                    if i < NM:
                        if i >= 2:
                            pe.wait_ge(fc1_act, b + i - 1)
                        for s in range(2):
                            im = 2 * pair + s
                            k = 32 * (im % TILE_IMG)
                            mm = pe.matmul(PS[:, 2 * (i % 2) + s, :], q("fc1")[k:k + 32, :], Z[k:k + 32, im // TILE_IMG, CHUNK * j:CHUNK * (j + 1)],
                                           start=True, stop=True)
                        mm.then_inc(fc1_mm, 1)
                    if 1 <= i <= NM:
                        pe.wait_ge(fc1_act, b + i)
                        if i >= 3:
                            pe.wait_ge(fc2_act, b + i - 2)
                        for s in range(2):
                            mm = pe.matmul(PS[64 * s:64 * s + 64, 4 + (i - 1) % 2, :], q("fc2"), H1[(i - 1) % 2][:, s, :], start=True, stop=True)
                        mm.then_inc(fc2_mm, 1)
                    if i >= 2:
                        pe.wait_ge(fc2_act, b + i - 1)
                        if i >= 4:
                            pe.wait_ge(fc3_kept, b + i - 3)
                        pe.matmul(PS[0:2, 6 + i % 2, :], q("fc3"), H2[i % 2], start=True, stop=True).then_inc(fc3_mm, 1)

            pe.wait_ge(prepared, 1)
            with pe.Fori(0, n_oct) as octet:
                pe.wait_ge(pix_in, octet * 16 + 16)
                pe.wait_ge(fc3_kept, octet * NM)
                norm(octet * NORMS, first)
                with pe.Fori(0, LAYERS) as layer:
                    layer_step(octet * LAYERS + layer, octet * NORMS + 1 + layer)
                pe.wait_ge(z_done, (octet + 1) * NORMS * TILES)
                mlp(octet)

        @block.scalar
        def _(act):
            def norm(n, last, gelu):
                act.wait_ge(vecs_ready, n + 1)
                for c in range(NCH + 1):
                    if c < NCH:
                        act.wait_ge(y_done, n * NCH + c + 1)
                        act.activation(SQ[:, c % 4, :], PS[:, c % 4, :], ACT.Square, bias=vecs[:, 0:1]).then_inc(sq_done, 1)
                    if c >= 1:
                        v = c - 1
                        act.wait_ge(var_done, n * NCH + v + 1)
                        if v >= 4:
                            act.wait_ge(norm_done, n * NCH + v - 3)
                        act.activation(RS[:, v % 4, :], PS[:, 4 + v % 4, :], ACT.Sqrt, bias=epsb[:, :]).then_inc(std_done, 1)
                for g in range(TILES):
                    act.wait_ge(norm_done, n * NCH + (g + 1) * CHUNKS)
                    act.activation(Z[:, g, :], Z[:, g, :], ACT.Gelu if gelu else ACT.Identity,
                                   bias=vecs[:, 2:3], scale=vecs[:, 1:2]).then_inc(z_done, 1)

            def layer_step(it, n, gelu):
                for u in range(1, 8, 2):
                    act.wait_ge(u_mm, it * 8 + u + 1)
                    act.copy(U[:, :, :, 4 * u:4 * u + 4].rearrange("p k b c -> p c (k b)"),
                             PS[:, u, 0:384].rearrange("p (c k) -> p c k", c=4)).then_inc(u_kept, 1)
                act.wait_ge(v_mm, it * 3 + 1)
                keep_modes(act.copy, 0, 4).then_inc(v_kept, 1)
                act.wait_ge(mix_mm, it * 2 + 1)
                for st in range(2):
                    last = keep_mix(act.copy, 0, st)
                last.then_inc(mix_kept, 1)
                act.wait_ge(t_mm, it * 2 + 2)
                keep_t(act.copy, 1).then_inc(t_kept, 1)
                for u in range(1, 8, 2):
                    act.wait_ge(tt_mm, it * 8 + u + 1)
                    act.copy(TT[:, u // 4, 4 * (u % 4):4 * (u % 4) + 4, :], PS[0:HBLK * KRI, u, :].rearrange("p (a n) -> p a n", a=4)).then_inc(tt_kept, 1)
                norm(n, None, gelu)

            def mlp(octet):
                b = octet * NM
                for i in range(NM + 1):
                    if i < NM:
                        act.wait_ge(fc1_mm, b + i + 1)
                        if i >= 2:
                            act.wait_ge(fc2_mm, b + i - 1)
                        act.activation(H1[i % 2], PS[:, 2 * (i % 2):2 * (i % 2) + 2, :], ACT.Gelu, bias=q("fc1b")).then_inc(fc1_act, 1)
                    if i >= 1:
                        act.wait_ge(fc2_mm, b + i)
                        if i >= 3:
                            act.wait_ge(fc3_mm, b + i - 2)
                        act.activation(H2[(i - 1) % 2], PS[:, 4 + (i - 1) % 2, :], ACT.Gelu, bias=q("fc2b")).then_inc(fc2_act, 1)

            act.wait_ge(prepared, 1)
            with act.Fori(0, n_oct) as octet:
                act.wait_ge(out_sent, octet * (16 * PAIRS))
                norm(octet * NORMS, None, False)
                with act.Fori(0, LAYERS - 1) as layer:
                    layer_step(octet * LAYERS + layer, octet * NORMS + 1 + layer, True)
                layer_step(octet * LAYERS + LAYERS - 1, octet * NORMS + LAYERS, False)
                mlp(octet)

        @block.vector
        def _(dve):
            def norm(n):
                for c in range(NCH):
                    dve.wait_ge(std_done, n * NCH + c + 1)
                    dve.reciprocal(RS[:, c % 4, :], RS[:, c % 4, :]).then_inc(inv_done, 1)
                    dve.wait_ge(inv_done, n * NCH + c + 1)
                    dve.scalar_tensor_tensor(out=Z[:, c // CHUNKS, cols(c)], in0=PS[:, c % 4, :], scalar=vecs[:, 0:1],
                                             in1=RS[:, c % 4, :], op0=ALU.add, op1=ALU.mult).then_inc(norm_done, 1)

            def take_vecs(n, layer1):
                if layer1 is not None:
                    dve.wait_ge(z_done, n * TILES)
                v = prm[:, 0:3 * NORMS].rearrange("p (k n) -> p k n", n=NORMS)
                v = v[:, :, 0:1] if layer1 is None else v[:, :, bass.ds(layer1, 1)]
                dve.tensor_copy(vecs[:, 0:3].unsqueeze(2), v).then_inc(vecs_ready, 1)

            def layer_step(it, n, layer):
                for g in range(TILES):
                    dve.wait_ge(z_done, n * TILES - TILES + g + 1)
                    dve.transpose(ZW[:, g, :], Z[:, g, :]).then_inc(turned, 1)
                take_vecs(n, layer + 1)
                dve.tensor_copy(conv[:, :].unsqueeze(1), q("conv").rearrange("p (l n) -> p l n", n=P)[:, bass.ds(layer, 1), :]).then_inc(conv_ready, 1)
                for u in range(0, 8, 2):
                    dve.wait_ge(u_mm, it * 8 + u + 1)
                    dve.tensor_copy(U[:, :, :, 4 * u:4 * u + 4].rearrange("p k b c -> p c (k b)"),
                                    PS[:, u, 0:384].rearrange("p (c k) -> p c k", c=4)).then_inc(u_kept, 1)
                dve.wait_ge(v_mm, it * 3 + 3)
                keep_modes(dve.tensor_copy, 4, 12).then_inc(v_kept, 1)
                dve.wait_ge(mix_mm, it * 2 + 2)
                for st in range(2):
                    last = keep_mix(dve.tensor_copy, 1, st)
                last.then_inc(mix_kept, 1)
                dve.wait_ge(mix_kept, (it + 1) * 2)
                dve.transpose(YT[:, :, :, :].rearrange("p y b x -> p (y b x)"), Y[:, :, :, :].rearrange("p y b x -> p (y b x)")).then_inc(y_turned, 1)
                dve.wait_ge(t_mm, it * 2 + 1)
                keep_t(dve.tensor_copy, 0).then_inc(t_kept, 1)
                for u in range(0, 8, 2):
                    dve.wait_ge(tt_mm, it * 8 + u + 1)
                    dve.tensor_copy(TT[:, u // 4, 4 * (u % 4):4 * (u % 4) + 4, :], PS[0:HBLK * KRI, u, :].rearrange("p (a n) -> p a n", a=4)).then_inc(tt_kept, 1)
                norm(n)

            dve.memset(epsb[:, :], LN_EPS)
            dve.memset(MB[:, :, :, :], 0.0)
            dve.memset(Y[:, :, :, :], 0.0).then_inc(prepared, 1)
            dve.wait_ge(prepared, 1)
            with dve.Fori(0, n_oct) as octet:
                dve.wait_ge(out_sent, octet * (16 * PAIRS))
                dve.wait_ge(z_done, octet * NORMS * TILES)
                take_vecs(octet * NORMS, None)
                dve.wait_ge(fc1_mm, octet * NM)
                norm(octet * NORMS)
                with dve.Fori(0, LAYERS) as layer:
                    layer_step(octet * LAYERS + layer, octet * NORMS + 1 + layer, layer)
                for i in range(NM):
                    dve.wait_ge(fc3_mm, octet * NM + i + 1)
                    if i % CHUNKS == 0:
                        dve.wait_ge(out_sent, octet * (16 * PAIRS) + 16 * (i // CHUNKS))
                    dve.tensor_scalar(OUT[:, CHUNK * (i % CHUNKS):CHUNK * (i % CHUNKS + 1)], PS[0:2, 6 + i % 2, :], q("fc3b", 2), None, ALU.add).then_inc(fc3_kept, 1)


HEADS, HD = 4, 16
EXPERTS = 8
CAP = int(np.ceil(1.25 * TOK / EXPERTS))
Q_ROWS = (SEQ + 1) // 2
M_ROWS = (Q_ROWS, SEQ - Q_ROWS)
TC = NT // 4

TPR = {}
_n = 0
for _name, _w in (("router", EXPERTS), ("gate", EXPERTS), ("wq", P), ("wk", P), ("wv", D), ("wo", D), ("m_w1", 4 * P), ("f_w1", 16 * P),
                  ("m_w2", 4 * P), ("f_w2", 16 * D), ("m_b2", EXPERTS * D), ("f_b2", EXPERTS * D),
                  ("m_b1", 4), ("f_b1", 16), ("eye", P), ("tri", P), ("ones", P), ("rank", EXPERTS),
                  ("gate_b", EXPERTS), ("wo_b", D), ("wv_b", D), ("wq_b", 1), ("wk_b", 1)):
    TPR[_name] = (_n, _w)
    _n += _w
STACKED = sum(TPR["f_w1"])
SPLIT_W = sum(TPR["f_b2"])
TPR_W = _n - SPLIT_W
SPLIT_NAMES = [name for name, (at, _) in TPR.items() if at < SPLIT_W]
TPR = {name: (at if at < SPLIT_W else at - SPLIT_W, width) for name, (at, width) in TPR.items()}


def layout_tokens(i):
    split, rest = np.zeros((P, SPLIT_W), np.float32), np.zeros((P, TPR_W), np.float32)

    def put(name, a, rows=0):
        n, w = TPR[name]
        a = np.asarray(a).reshape(-1, w)
        (split if name in SPLIT_NAMES else rest)[rows:rows + a.shape[0], n:n + w] = a

    def twice(name, a):
        put(name, a)
        put(name, a, D)

    twice("router", i["L0_ffn_router_w"].T)
    twice("gate", i["L1_ffn_gate_w"])
    for name, w, b in (("wq", "L1_attn_Wq", "L1_attn_bq"), ("wk", "L1_attn_Wk", "L1_attn_bk")):
        a = np.zeros((D, HEADS, 32), np.float32)
        a[:, :, :HD] = i[w].T.reshape(D, HEADS, HD)
        twice(name, a)
        v = np.zeros((HEADS, 32), np.float32)
        v[:, :HD] = i[b].reshape(HEADS, HD)
        put(name + "_b", v)
    twice("wv", i["L1_attn_Wv"].T)
    twice("wo", i["L1_attn_Wo"].T)
    twice("m_w1", i["L0_ffn_w1"].transpose(1, 0, 2))
    twice("f_w1", i["L1_ffn_w1"].transpose(1, 0, 2))
    w2 = np.zeros((2, D, 4, 2, D), np.float32)
    for e in range(2):
        w2[e, :, :, e] = i["L0_ffn_w2"][e::2].transpose(1, 0, 2)
    put("m_w2", w2)
    put("f_w2", i["L1_ffn_w2"].reshape(16, P, D).transpose(1, 0, 2))
    put("m_b2", i["L0_ffn_b2"])
    put("f_b2", i["L1_ffn_b2"])
    for k in (32, 64):
        put("m_b2", i["L0_ffn_b2"], k)
        put("f_b2", i["L1_ffn_b2"], k)
    put("m_b1", i["L0_ffn_b1"].reshape(4, P).T)
    put("f_b1", i["L1_ffn_b1"].reshape(16, P).T)
    put("eye", np.eye(P))
    put("tri", np.triu(np.ones((P, P))))
    put("ones", np.ones((P, P)))
    put("rank", np.broadcast_to(np.arange(EXPERTS, 0, -1.0), (P, EXPERTS)))
    put("gate_b", np.broadcast_to(i["L1_ffn_gate_b"], (P, EXPERTS)))
    put("wo_b", np.broadcast_to(i["L1_attn_bo"], (P, D)))
    put("wv_b", np.broadcast_to(i["L1_attn_bv"], (P, D)))
    return {"weights": split, "tokprm": rest}


def bc(ap, n):
    return ap.unsqueeze(2).broadcast_to([ap.shape[0], ap.shape[1], n])


def chain_of(eng, step):
    count = [0]

    def link(ins):
        count[0] += 1
        ins.then_inc(step, 1)
        eng.wait_ge(step, count[0])
        return count[0]
    return link


def load_tokens(nc, name, src, X, more=()):
    with nc.semaphore(name + "_loaded") as loaded, nc.Block() as block:
        @block.sync
        def _(sp):
            sp.dma_start(X[:, 0:FULL_T, :], src[0:FULL_T * P, :].rearrange("(t p) d -> p t d", p=P)).then_inc(loaded, 16)
            sp.dma_start(X[0:REST, FULL_T, :], src[FULL_T * P:TOK, :]).then_inc(loaded, 16)
            for to, frm in more:
                sp.dma_start(to, frm).then_inc(loaded, 16)
            sp.wait_ge(loaded, 32 + 16 * len(more))

        @block.vector
        def _(dve):
            dve.memset(X[REST:P, FULL_T, :], 0.0)
            dve.memset(X[:, FULL_T + 1:NT, :], 0.0)


def split_weights(nc, raw, REM, tpr, WH, WM, WC, eyeb):
    with ExitStack() as ctx:
        step = ctx.enter_context(nc.semaphore("weights_step"))
        block = ctx.enter_context(nc.Block())

        @block.vector
        def _(dve):
            link = chain_of(dve, step)
            link(dve.tensor_copy(WH[:, :], raw))
            link(dve.tensor_tensor(REM, raw, WH[:, :], ALU.subtract))
            link(dve.tensor_copy(WM[:, :], REM))
            link(dve.tensor_tensor(WC[0:D, :], REM[0:D, :], WM[0:D, :], ALU.subtract))
            link(dve.tensor_tensor(WC[D:P, STACKED:SPLIT_W], REM[D:P, STACKED:SPLIT_W], WM[D:P, STACKED:SPLIT_W], ALU.subtract))
            link(dve.tensor_copy(WC[D:P, 0:STACKED], WH[D:P, 0:STACKED]))
            b = slice(TPR["m_b2"][0], SPLIT_W)
            link(dve.tensor_copy(WH[32:33, b], WM[32:33, b]))
            link(dve.tensor_copy(WH[64:65, b], WC[64:65, b]))
            o = slice(*(TPR["wo"][0], sum(TPR["wo"])))
            link(dve.tensor_copy(WH[D:P, o], WM[D:P, o]))
            link(dve.memset(WC[D:P, o], 0.0))
            dve.tensor_copy(eyeb[:, 0, :], tpr[:, TPR["eye"][0]:sum(TPR["eye"])])
            dve.tensor_copy(eyeb[:, 1, :], tpr[:, TPR["ones"][0]:sum(TPR["ones"])])


def token_norm(nc, name, H, X, SQ, HML, clip=None, unit=None):
    with ExitStack() as ctx:
        sb = lambda n, shape: ctx.enter_context(nc.sbuf_tensor(name + n, shape, F32))
        sem = lambda n: ctx.enter_context(nc.semaphore(name + n))
        st = sb("_stat", [P, 4, NT])
        cst = sb("_const", [P, 2])
        step, rooted, squared = sem("_step"), sem("_rooted"), sem("_squared")
        block = ctx.enter_context(nc.Block())
        sq = SQ[:, 0:NT * D].rearrange("p (t d) -> p t d", d=D)
        marks = {}

        @block.vector
        def _(dve):
            link = chain_of(dve, step)
            dve.memset(cst[:, 0:1], LN_EPS)
            dve.memset(cst[:, 1:2], 0.0)
            link(dve.tensor_reduce(st[:, 0, :], H[:, :, :], AX.X, ALU.add))
            link(dve.tensor_scalar(st[:, 0, :], st[:, 0, :], 1.0 / D, None, ALU.mult))
            marks["centered"] = link(dve.tensor_tensor(X[:, :, :], H[:, :, :], bc(st[:, 0, :], D), ALU.subtract))
            dve.wait_ge(squared, 1)
            marks["variance"] = link(dve.tensor_reduce(st[:, 1, :], sq, AX.X, ALU.add))
            dve.wait_ge(rooted, 1)
            link(dve.reciprocal(st[:, 2, :], st[:, 1, :]))
            marks["normed"] = link(dve.tensor_tensor(X[:, :, :], X[:, :, :], bc(st[:, 2, :], D), ALU.mult))
            if clip is not None:
                link(dve.tensor_scalar(X[:, :, :], X[:, :, :], clip, -clip, ALU.min, ALU.max))
            if unit is not None:
                dve.wait_ge(squared, 2)
                marks["length"] = link(dve.tensor_reduce(st[:, 1, :], sq, AX.X, ALU.add))
                dve.wait_ge(rooted, 2)
                link(dve.tensor_scalar(st[:, 1, :], st[:, 1, :], 1e-12, None, ALU.max))
                link(dve.reciprocal(st[:, 2, :], st[:, 1, :]))
                link(dve.tensor_tensor(unit[:, :, 0:D], X[:, :, :], bc(st[:, 2, :], D), ALU.mult))
            split_tokens(dve, link, X[:, :, :] if unit is None else unit[:, :, 0:D], sq, HML, marks)

        @block.scalar
        def _(act):
            act.wait_ge(step, marks["centered"])
            act.activation(sq, X[:, :, :], ACT.Square).then_inc(squared, 1)
            act.wait_ge(step, marks["variance"])
            act.activation(st[:, 1, :], st[:, 1, :], ACT.Sqrt, bias=cst[:, 0:1], scale=1.0 / D).then_inc(rooted, 1)
            if unit is not None:
                act.wait_ge(step, marks["normed"])
                act.activation(sq, X[:, :, :], ACT.Square).then_inc(squared, 1)
                act.wait_ge(step, marks["length"])
                act.activation(st[:, 1, :], st[:, 1, :], ACT.Sqrt, bias=cst[:, 1:2]).then_inc(rooted, 1)
            act.wait_ge(step, marks["high"])
            act.copy(HML[:, 1, :, 0:D], HML[:, 0, :, 0:D])


def split_tokens(dve, link, x, rest, HML, marks):
    marks["high"] = link(dve.tensor_copy(HML[:, 0, :, 0:D], x))
    link(dve.tensor_tensor(rest, x, HML[:, 0, :, 0:D], ALU.subtract))
    link(dve.tensor_copy(HML[:, 0, :, D:P], rest))
    link(dve.tensor_tensor(HML[:, 1, :, D:P], rest, HML[:, 0, :, D:P], ALU.subtract))


def turn_tokens(nc, name, HML, eyeb, XP, w=None, weight=None, out=None, parts=2):
    width = TPR[weight][1] if weight else 0
    c0 = TPR[weight][0] if weight else 0
    with ExitStack() as ctx:
        sem = lambda n: ctx.enter_context(nc.semaphore(name + n))
        ps = ctx.enter_context(nc.psum_tensor(name + "_ps", [P, 6, CHUNK], F32))
        turned, spread, spread_low, formed, kept = (sem("_" + n) for n in ("turned", "spread", "spread_low", "formed", "kept"))
        block = ctx.enter_context(nc.Block())

        @block.tensor
        def _(pe):
            with pe.Fori(0, TC // 2) as i:
                for s in range(2):
                    c = 2 * i + s
                    pe.wait_ge(spread, c - s)
                    if parts == 2:
                        pe.wait_ge(spread_low, c - s)
                    for part in range(parts):
                        for k in range(4):
                            mm = pe.matmul(ps[:, 2 * s + part, P * k:P * k + P], HML[:, part, bass.ds(c * 4 + k, 1), :].rearrange("p a n -> p (a n)"),
                                           eyeb[:, 0, :], start=True, stop=True)
                    mm.then_inc(turned, 1)
                if out is not None:
                    for s in range(2):
                        c = 2 * i + s
                        pe.wait_ge(kept, c - s)
                        pe.wait_ge(spread, c + 1)
                        if parts == 2:
                            pe.wait_ge(spread_low, c + 1)
                        terms = [(0, w[0]), (0, w[1]), (1, w[2])] if parts == 2 else [(0, w[0]), (0, w[2])]
                        for k in range(4):
                            for n, (part, wt) in enumerate(terms):
                                mm = pe.matmul(ps[:, 4 + s, width * k:width * k + width], XP[:, part, bass.ds(c * CHUNK + P * k, P)], wt[:, c0:c0 + width],
                                               start=(n == 0), stop=(n == len(terms) - 1))
                        mm.then_inc(formed, 1)

        @block.scalar
        def _(act):
            with act.Fori(0, TC // 2) as i:
                for s in range(2):
                    c = 2 * i + s
                    act.wait_ge(turned, c + 1)
                    act.copy(XP[:, 0, bass.ds(c * CHUNK, CHUNK)], ps[:, 2 * s, :]).then_inc(spread, 1)

        @block.vector
        def _(dve):
            with dve.Fori(0, TC // 2) as i:
                for s in range(2):
                    c = 2 * i + s
                    if parts == 2:
                        dve.wait_ge(turned, c + 1)
                        dve.tensor_copy(XP[:, 1, bass.ds(c * CHUNK, CHUNK)], ps[:, 2 * s + 1, :]).then_inc(spread_low, 1)
                if out is not None:
                    for s in range(2):
                        c = 2 * i + s
                        dve.wait_ge(formed, c + 1)
                        dve.tensor_copy(out[:, bass.ds(c * 4, 4), 0:width], ps[:, 4 + s, 0:4 * width].rearrange("p (a n) -> p a n", a=4)).then_inc(kept, 1)


def global_attention(nc, HML, XP, OA, tpr, SUM):
    NJ = FULL_T + 1
    NS = 4
    LAG = 3
    with ExitStack() as ctx:
        sb = lambda n, shape, dt=F32: ctx.enter_context(nc.sbuf_tensor(n, shape, dt))
        sem = lambda n: ctx.enter_context(nc.semaphore(n))
        E = sb("E", [P, NS, CHUNK])
        EH = sb("E_high", [P, NS, CHUNK], BF16)
        EL = sb("E_low", [P, NS, CHUNK], BF16)
        Q = sb("queries", [P, 2, 3, CHUNK], BF16)
        OT = sb("sums_feature", [P, 2, CHUNK])
        ps = ctx.enter_context(nc.psum_tensor("att_ps", [P, 8, CHUNK], F32))
        q_ready, scored, weighed, high, split, used, sums_kept, turned, placed = (sem("att_" + n) for n in (
            "q_ready", "scored", "weighed", "high", "split", "used", "sums_kept", "turned", "placed"))
        placed_low = sem("att_placed_low")
        block = ctx.enter_context(nc.Block())

        @block.tensor
        def _(pe):
            def turn_back(n, half):
                pe.wait_ge(sums_kept, n + 1)
                pe.wait_ge(placed, n - half)
                for k in range(4):
                    mm = pe.transpose(ps[:, 6 + half, P * k:P * k + P], OT[:, half, P * k:P * k + P], tpr[:, TPR["eye"][0]:sum(TPR["eye"])])
                mm.then_inc(turned, 1)

            with pe.Fori(0, TC // 2) as i:
                for half in range(2):
                    n = 2 * i + half
                    pe.wait_ge(q_ready, n + 1)
                    for j in range(NJ + LAG):
                        if j < NJ:
                            if j >= NS:
                                pe.wait_ge(weighed, n * NJ + j - NS + 1)
                            for k, part in enumerate((0, 0, 1)):
                                mm = pe.matmul(ps[:, j % NS, :], XP[:, part, P * j:P * j + P], Q[:, half, k, :], start=(k == 0), stop=(k == 2))
                            mm.then_inc(scored, 1)
                        if j >= LAG:
                            m = j - LAG
                            if m == 0:
                                pe.wait_ge(sums_kept, n - half)
                            pe.wait_ge(split, n * NJ + m + 1)
                            for k, e in enumerate((EH, EL)):
                                mm = pe.matmul(ps[:, 4 + half, :], HML[:, 0, m, :], e[:, m % NS, :], start=(m == 0 and k == 0), stop=(m == NJ - 1 and k == 1))
                            mm.then_inc(used, 1)
                    turn_back(n, half)

        @block.scalar
        def _(act):
            with act.Fori(0, TC // 2) as i:
                for half in range(2):
                    n = 2 * i + half
                    for j in range(NJ):
                        act.wait_ge(scored, n * NJ + j + 1)
                        if j >= NS:
                            act.wait_ge(split, n * NJ + j - NS + 1)
                        act.activation(E[:, j % NS, :], ps[:, j % NS, :], ACT.Exp,
                                       accum_out=SUM[:, j, bass.ds(n, 1)]).then_inc(weighed, 1)

        @block.vector
        def _(dve):
            def queries(c, slot):
                cols = bass.ds(c * CHUNK, CHUNK)
                for k, (lower, upper) in enumerate((((0, 0), (0, 0)), ((D, 0), (D, 0)), ((D, 1), (0, 1)))):
                    for to, (frm, part) in ((0, lower), (D, upper)):
                        last = dve.tensor_copy(Q[to:to + D, slot, k, :], XP[frm:frm + D, part, cols])
                last.then_inc(q_ready, 1)

            def place(n, half):
                dve.wait_ge(turned, n + 1)
                src = ps[:, 6 + half, :].rearrange("p (a k d) -> p a k d", a=4, k=2)
                dve.tensor_copy(OA[:, bass.ds(n * 4, 4), 0:D], src[:, :, 0, :]).then_inc(placed_low, 1)
                dve.wait_ge(placed_low, n + 1)
                dve.tensor_tensor(OA[:, bass.ds(n * 4, 4), 0:D], OA[:, bass.ds(n * 4, 4), 0:D], src[:, :, 1, :], ALU.add).then_inc(placed, 1)

            with dve.Fori(0, TC // 2) as i:
                for half in range(2):
                    n = 2 * i + half
                    dve.wait_ge(used, (n - half) * NJ)
                    queries(n, half)
                    for j in range(NJ):
                        dve.wait_ge(weighed, n * NJ + j + 1)
                        if j >= NS:
                            dve.wait_ge(used, n * NJ + j - NS + 1)
                        dve.tensor_copy(EH[:, j % NS, :], E[:, j % NS, :]).then_inc(high, 1)
                        dve.wait_ge(high, n * NJ + j + 1)
                        dve.tensor_tensor(EL[:, j % NS, :], E[:, j % NS, :], EH[:, j % NS, :], ALU.subtract).then_inc(split, 1)
                    dve.wait_ge(used, (n + 1) * NJ)
                    dve.tensor_copy(OT[:, half, :], ps[:, 4 + half, :]).then_inc(sums_kept, 1)
                    place(n, half)


def blend(nc, H, FA, OA, SQ, SUM):
    with ExitStack() as ctx:
        st = ctx.enter_context(nc.sbuf_tensor("blend_stat", [P, 2, NT], F32))
        NJ = FULL_T + 1
        zero = ctx.enter_context(nc.sbuf_tensor("blend_zero", [P, 2], F32))
        weighed = ctx.enter_context(nc.semaphore("blend_weighed"))
        step, squared, rooted = (ctx.enter_context(nc.semaphore("blend_" + n)) for n in ("step", "squared", "rooted"))
        sq = SQ[:, 0:NT * D].rearrange("p (t d) -> p t d", d=D)
        block = ctx.enter_context(nc.Block())
        marks = {}

        @block.vector
        def _(dve):
            link = chain_of(dve, step)
            att = OA[:, :, 0:D]
            link(dve.memset(zero[:, 0:1], 0.0))
            marks["zero"] = 1
            link(dve.memset(st[:, 0, :], float(NT * P)))
            link(dve.tensor_reduce(st[:, 0, 0:NJ], SUM[:, :, :], AX.X, ALU.add))
            dve.wait_ge(weighed, 1)
            link(dve.tensor_scalar(zero[:, 1:2], zero[:, 1:2], float(NT * P - TOK), None, ALU.mult))
            link(dve.tensor_scalar(st[:, 0, :], st[:, 0, :], zero[:, 1:2], None, ALU.subtract))
            link(dve.reciprocal(st[:, 0, :], st[:, 0, :]))
            link(dve.tensor_scalar(st[:, 0, :], st[:, 0, :], 1.0 - 0.8, None, ALU.mult))
            link(dve.tensor_tensor(att, att, bc(st[:, 0, :], D), ALU.mult))
            marks["mixed"] = link(dve.scalar_tensor_tensor(out=att, in0=FA[:, :, 0:D], scalar=0.8, in1=att, op0=ALU.mult, op1=ALU.add))
            dve.wait_ge(squared, 1)
            marks["length"] = link(dve.tensor_reduce(st[:, 0, :], sq, AX.X, ALU.add))
            dve.wait_ge(rooted, 1)
            link(dve.tensor_scalar(st[:, 1, :], st[:, 0, :], 1e-12, None, ALU.max))
            link(dve.reciprocal(st[:, 0, :], st[:, 1, :]))
            link(dve.tensor_tensor(att, att, bc(st[:, 0, :], D), ALU.mult))
            link(dve.tensor_tensor(H[:, :, :], H[:, :, :], att, ALU.add))

        @block.scalar
        def _(act):
            act.wait_ge(step, marks["zero"])
            act.activation(zero[:, 1:2], zero[:, 0:1], ACT.Exp).then_inc(weighed, 1)
            act.wait_ge(step, marks["mixed"])
            act.activation(sq, OA[:, :, 0:D], ACT.Square).then_inc(squared, 1)
            act.wait_ge(step, marks["length"])
            act.activation(st[:, 0, :], st[:, 0, :], ACT.Sqrt, bias=zero[:, 0:1]).then_inc(rooted, 1)


def route(nc, name, LG, tpr, coef, top, bias=None):
    t = lambda n: tpr[:, TPR[n][0]:sum(TPR[n])]
    with ExitStack() as ctx:
        sb = lambda n, shape: ctx.enter_context(nc.sbuf_tensor(name + n, shape, F32))
        sem = lambda n: ctx.enter_context(nc.semaphore(name + n))
        PR, A, S1, S2 = (sb(n, [P, NT, EXPERTS]) for n in ("_prob", "_a", "_first", "_second"))
        st = sb("_stat", [P, NT])
        step, powered, counted = sem("_step"), sem("_powered"), sem("_counted")
        ps = ctx.enter_context(nc.psum_tensor(name + "_ps", [P, 4, CHUNK], F32))
        block = ctx.enter_context(nc.Block())
        marks = {}
        HALF = NT // 2 * EXPERTS
        rank = t("rank").unsqueeze(1).broadcast_to([P, NT, EXPERTS])

        @block.vector
        def _(dve):
            link = chain_of(dve, step)
            tt = lambda out, a, b, op: link(dve.tensor_tensor(out, a, b, op))
            lg = LG[:, :, 0:EXPERTS]
            pr, a, s1, s2 = (x[:, :, :] for x in (PR, A, S1, S2))
            if bias is not None:
                tt(lg, lg, t(bias).unsqueeze(1).broadcast_to([P, NT, EXPERTS]), ALU.add)
            link(dve.tensor_reduce(st[:, :], lg, AX.X, ALU.max))
            marks["shifted"] = tt(pr, lg, bc(st[:, :], EXPERTS), ALU.subtract)
            dve.wait_ge(powered, 1)
            link(dve.tensor_reduce(st[:, :], pr, AX.X, ALU.add))
            link(dve.reciprocal(st[:, :], st[:, :]))
            tt(pr, pr, bc(st[:, :], EXPERTS), ALU.mult)

            def pick(src, one_hot):
                link(dve.tensor_reduce(st[:, :], src, AX.X, ALU.max))
                tt(a, src, bc(st[:, :], EXPERTS), ALU.is_equal)
                tt(a, a, rank, ALU.mult)
                link(dve.tensor_reduce(st[:, :], a, AX.X, ALU.max))
                tt(one_hot, a, bc(st[:, :], EXPERTS), ALU.is_equal)

            pick(pr, s1)
            c = coef[:, :, :]
            if top == 2:
                link(dve.scalar_tensor_tensor(out=s2, in0=s1, scalar=-2.0, in1=pr, op0=ALU.mult, op1=ALU.add))
                pick(s2, c)
                tt(s1, s1, c, ALU.add)
                tt(c, s1, pr, ALU.mult)
                link(dve.tensor_reduce(st[:, :], c, AX.X, ALU.add))
                link(dve.tensor_scalar(st[:, :], st[:, :], 1e-12, None, ALU.max))
                link(dve.reciprocal(st[:, :], st[:, :]))
                tt(c, c, bc(st[:, :], EXPERTS), ALU.mult)
            else:
                marks["picked"] = step_now = tt(c, s1, pr, ALU.mult)
                dve.wait_ge(counted, 1)
                halves = lambda x: x.rearrange("p (h t) e -> p h (t e)", h=2)
                link(dve.tensor_copy(halves(s2), ps[:, 2:4, 0:HALF]))
                for e in range(EXPERTS):
                    last = dve.tensor_tensor_scan(a[:, :, e], s2[:, :, e], s2[:, :, e], 0.0, ALU.add, ALU.bypass)
                link(last)
                tt(a, a, s2, ALU.subtract)
                link(dve.tensor_tensor(halves(s2), ps[:, 0:2, 0:HALF], halves(a), ALU.add))
                link(dve.tensor_scalar(s2, s2, CAP + 0.5, None, ALU.is_lt))
                tt(c, c, s2, ALU.mult)

        @block.scalar
        def _(act):
            act.wait_ge(step, marks["shifted"])
            act.activation(PR[:, :, :], PR[:, :, :], ACT.Exp).then_inc(powered, 1)

        @block.tensor
        def _(pe):
            if top == 1:
                pe.wait_ge(step, marks["picked"])
                for h in range(2):
                    rows = S1[:, NT // 2 * h:NT // 2 * (h + 1), :].rearrange("p t e -> p (t e)")
                    pe.matmul(ps[:, h, 0:HALF], t("tri"), rows, start=True, stop=True)
                    mm = pe.matmul(ps[:, 2 + h, 0:HALF], t("ones"), rows, start=True, stop=True)
                mm.then_inc(counted, 1)


def experts(nc, name, XP, tpr, w, onesb, coef, YO, kt, func):
    pre = name[0]
    at = lambda n: TPR[pre + "_" + n][0]
    b1 = tpr[:, at("b1"):at("b1") + kt]
    wide = TPR[pre + "_w2"][1] // kt
    per = max(1, kt * wide // (EXPERTS * D))
    WH, WM, WC = w
    with ExitStack() as ctx:
        sb = lambda n, shape, dt=F32: ctx.enter_context(nc.sbuf_tensor(name + n, shape, dt))
        sem = lambda n: ctx.enter_context(nc.semaphore(name + n))
        G = 4
        AHEAD = 3
        HF = sb("_hidden", [P, G, CHUNK])
        HB = sb("_hidden_parts", [P, G, 2, CHUNK], BF16)
        prod = sb("_prod", [P, 2, EXPERTS * D])
        ps = ctx.enter_context(nc.psum_tensor(name + "_ps", [P, 8, CHUNK], F32))
        hidden_mm, hidden, high, split, used, y_mm, scaled, reduced = (sem("_" + n) for n in (
            "hidden_mm", "hidden", "high", "split", "used", "y_mm", "scaled", "reduced"))
        block = ctx.enter_context(nc.Block())

        @block.tensor
        def _(pe):
            def first_layer(c, k):
                if not (isinstance(c, int) and c * kt + k < G):
                    pe.wait_ge(hidden, c * kt + k - G + 1)
                cols = slice(at("w1") + P * k, at("w1") + P * k + P)
                for n, (wt, part) in enumerate(((WH, 0), (WM, 0), (WC, 1))):
                    mm = pe.matmul(ps[:, k % G, :], wt[:, cols], XP[:, part, bass.ds(c * CHUNK, CHUNK)], start=(n == 0), stop=(n == 2))
                mm.then_inc(hidden_mm, 1)

            def second_layer(c, k):
                if k == 0:
                    pe.wait_ge(scaled, c * 4)
                pe.wait_ge(split, c * kt + k + 1)
                g = k // per
                for j in range(4):
                    out = ps[:, 4 + j, wide * g:wide * g + wide]
                    if k % per == 0:
                        pe.matmul(out, onesb, WH[:, at("b2") + wide * g:at("b2") + wide * g + wide], start=True, stop=False)
                    w2 = slice(at("w2") + wide * k, at("w2") + wide * k + wide)
                    for part in range(2):
                        for wt in (WH, WM):
                            mm = pe.matmul(out, HB[:, k % G, part, P * j:P * j + P], wt[:, w2], start=False,
                                           stop=(k % per == per - 1 and part == 1 and wt is WM))
                mm.then_inc(used, 1)

            def chunk(c, last):
                for k in range(kt):
                    if k + AHEAD < kt:
                        first_layer(c, k + AHEAD)
                    elif not last:
                        first_layer(c + 1, k + AHEAD - kt)
                    second_layer(c, k)

            for k in range(AHEAD):
                first_layer(0, k)
            with pe.Fori(0, TC - 1) as c:
                chunk(c, False)
            chunk(TC - 1, True)

        @block.scalar
        def _(act):
            with act.Fori(0, TC) as c:
                for k in range(kt):
                    act.wait_ge(hidden_mm, c * kt + k + 1)
                    if k >= G:
                        act.wait_ge(split, c * kt + k - G + 1)
                    else:
                        act.wait_ge(split, c * kt)
                    act.activation(HF[:, k % G, :], ps[:, k % G, :], func, bias=b1[:, k:k + 1]).then_inc(hidden, 1)

        @block.vector
        def _(dve):
            def parts(c, k):
                dve.wait_ge(hidden, c * kt + k + 1)
                if not (isinstance(c, int) and c * kt + k < G):
                    dve.wait_ge(used, c * kt + k - G + 1)
                dve.tensor_copy(HB[:, k % G, 0, :], HF[:, k % G, :]).then_inc(high, 1)
                dve.wait_ge(high, c * kt + k + 1)
                dve.tensor_tensor(HB[:, k % G, 1, :], HF[:, k % G, :], HB[:, k % G, 0, :], ALU.subtract).then_inc(split, 1)

            def combine(c, j):
                n = c * 4 + j
                if j == 0:
                    dve.wait_ge(used, (c + 1) * kt)
                dve.tensor_tensor(prod[:, j % 2, :].rearrange("p (e d) -> p e d", d=D), ps[:, 4 + j, :].rearrange("p (e d) -> p e d", d=D),
                                  coef[:, bass.ds(n, 1), :].rearrange("p a e -> p (a e)").unsqueeze(2).broadcast_to([P, EXPERTS, D]), ALU.mult).then_inc(scaled, 1)
                dve.wait_ge(scaled, n + 1)
                dve.tensor_reduce(YO[:, bass.ds(n, 1), 0:D].rearrange("p a d -> p (a d)"),
                                  prod[:, j % 2, :].rearrange("p (e d) -> p d e", d=D), AX.X, ALU.add).then_inc(reduced, 1)

            def chunk(c, last):
                for k in range(2, kt):
                    parts(c, k)
                if not last:
                    for k in range(2):
                        parts(c + 1, k)
                for j in range(4):
                    combine(c, j)

            for k in range(2):
                parts(0, k)
            chunk(0, False)
            with dve.Fori(1, TC - 1) as c:
                chunk(c, False)
            chunk(TC - 1, True)


def add_to(nc, name, H, parts, guard=False, bias=None):
    with ExitStack() as ctx:
        step = ctx.enter_context(nc.semaphore(name + "_step"))
        mask = ctx.enter_context(nc.sbuf_tensor(name + "_mask", [P, NT, D], mybir.dt.uint8)) if guard else None
        fill = ctx.enter_context(nc.sbuf_tensor(name + "_fill", [P, 3], F32)) if guard else None
        block = ctx.enter_context(nc.Block())

        @block.vector
        def _(dve):
            link = chain_of(dve, step)
            if guard:
                y = parts[0]
                top = float(np.finfo(np.float32).max)
                for n, (value, test) in enumerate(((0.0, None), (10000.0, ALU.is_gt), (-10000.0, ALU.is_lt))):
                    link(dve.memset(fill[:, n:n + 1], value))
                    if test is None:
                        link(dve.tensor_tensor(mask[:, :, :], y, y, ALU.not_equal))
                    else:
                        link(dve.tensor_scalar(mask[:, :, :], y, top if value > 0 else -top, None, test))
                    link(dve.copy_predicated(y, mask[:, :, :], fill[:, n:n + 1].unsqueeze(2).broadcast_to([P, NT, D])))
            if bias is not None:
                link(dve.tensor_tensor(H[:, :, :], H[:, :, :], bias.unsqueeze(1).broadcast_to([P, NT, D]), ALU.add))
            for part in parts:
                link(dve.tensor_tensor(H[:, :, :], H[:, :, :], part, ALU.add))


def head_attention(nc, XP, tpr, w, att):
    t = lambda n: tpr[:, TPR[n][0]:sum(TPR[n])]
    with ExitStack() as ctx:
        sb = lambda n, shape, dt=F32: ctx.enter_context(nc.sbuf_tensor("mha_" + n, shape, dt))
        sem = lambda n: ctx.enter_context(nc.semaphore("mha_" + n))
        QK = sb("qk", [P, 2, SEQ])
        V = sb("v", [Q_ROWS, 2, HEADS, HD + 1])
        S = sb("s", [Q_ROWS, 2 * HEADS, SEQ])
        PT = sb("pt", [Q_ROWS, 2, 2, HEADS * Q_ROWS])
        mx = sb("mx", [Q_ROWS, 2 * HEADS])
        rc = sb("rc", [Q_ROWS, 2 * HEADS])
        OB = sb("ob", [Q_ROWS, 2 * HEADS, HD], BF16)
        OF = sb("of", [Q_ROWS, 2, 2, D])
        ps = ctx.enter_context(nc.psum_tensor("mha_ps", [P, 8, CHUNK], F32))
        (ones_set, qkv, qk_kept, v_kept, scored, maxed, shifted, weighed, turned, pt_kept, mixed, inverted,
         rounded, widened, sent) = (sem(n) for n in (
             "ones_set qkv qk_kept v_kept scored maxed shifted weighed turned pt_kept mixed inverted rounded widened sent").split())
        block = ctx.enter_context(nc.Block())
        PAIRS = BATCH // 2
        rows = att.rearrange("(b s) d -> b s d", s=SEQ)
        sv = ps[0:Q_ROWS, 0:4, 0:2 * SEQ].rearrange("p h (n m) -> p h n m", n=2)
        ov = ps[0:Q_ROWS, 0, 0:2 * HEADS * (HD + 1)].rearrange("p (n f) -> p n f", f=HD + 1)

        @block.tensor
        def _(pe):
            pe.wait_ge(ones_set, 1)
            with pe.Fori(0, PAIRS) as i:
                for s in range(2):
                    b = 2 * i + s
                    pe.wait_ge(pt_kept, b * 2)
                    terms = [(w[0], 0), (w[1], 0), (w[2], 1)]
                    for a, name in enumerate(("wq", "wk")):
                        cols = slice(TPR[name][0], sum(TPR[name]))
                        for n, (wt, part) in enumerate(terms):
                            pe.matmul(ps[:, 4, 256 * a:256 * a + SEQ], wt[:, cols], XP[:, part, bass.ds(b * SEQ, SEQ)], start=(n == 0), stop=(n == 2))
                    cols = slice(TPR["wv"][0], sum(TPR["wv"]))
                    for m in range(2):
                        for n, (wt, part) in enumerate(terms):
                            mm = pe.matmul(ps[0:M_ROWS[m], 5, D * m:D * m + D], XP[:, part, bass.ds(b * SEQ + Q_ROWS * m, M_ROWS[m])], wt[:, cols], start=(n == 0), stop=(n == 2))
                    mm.then_inc(qkv, 1)
                    pe.wait_ge(qk_kept, b + 1)
                    pe.wait_ge(inverted, b)
                    pe.wait_ge(rounded, b)
                    for n in range(2):
                        q0 = (SEQ - Q_ROWS) * n
                        for h in range(HEADS):
                            mm = pe.matmul(ps[0:Q_ROWS, h, SEQ * n:SEQ * n + SEQ],
                                           QK[32 * h:32 * h + 32, 0, q0:q0 + Q_ROWS], QK[32 * h:32 * h + 32, 1, :], start=True, stop=True)
                    mm.then_inc(scored, 1)
                    pe.wait_ge(weighed, b + 1)
                    pe.wait_ge(v_kept, b + 1)
                    for m in range(2):
                        for n in range(2):
                            for h in range(HEADS):
                                mm = pe.transpose(ps[0:M_ROWS[m], 4 + 2 * m + n, Q_ROWS * h:Q_ROWS * h + Q_ROWS],
                                                  S[:, 2 * h + n, Q_ROWS * m:Q_ROWS * m + M_ROWS[m]], t("eye")[0:Q_ROWS, 0:Q_ROWS])
                        mm.then_inc(turned, 1)
                    pe.wait_ge(pt_kept, b * 2 + 2)
                    for n in range(2):
                        for h in range(HEADS):
                            for m in range(2):
                                mm = pe.matmul(ov[:, HEADS * n + h, :], PT[0:M_ROWS[m], m, n, Q_ROWS * h:Q_ROWS * h + Q_ROWS], V[0:M_ROWS[m], m, h, :],
                                               start=(m == 0), stop=(m == 1))
                    mm.then_inc(mixed, 1)

        @block.scalar
        def _(act):
            with act.Fori(0, PAIRS) as i:
                for s in range(2):
                    b = 2 * i + s
                    act.wait_ge(qkv, b + 1)
                    act.wait_ge(scored, b)
                    for a, name in enumerate(("wq_b", "wk_b")):
                        last = act.activation(QK[:, a, :], ps[:, 4, 256 * a:256 * a + SEQ], ACT.Identity, bias=t(name))
                    last.then_inc(qk_kept, 1)
                    act.wait_ge(shifted, b + 1)
                    act.activation(S[:, :, :], S[:, :, :], ACT.Exp, scale=HD ** -0.5).then_inc(weighed, 1)
                    act.wait_ge(turned, b * 2 + 1)
                    act.copy(PT[0:M_ROWS[0], 0, :, :], ps[0:M_ROWS[0], 4:6, 0:HEADS * Q_ROWS]).then_inc(pt_kept, 1)

        @block.vector
        def _(dve):
            dve.memset(V[:, :, :, :], 1.0).then_inc(ones_set, 1)
            dve.wait_ge(ones_set, 1)
            with dve.Fori(0, PAIRS) as i:
                for s in range(2):
                    b = 2 * i + s
                    dve.wait_ge(qkv, b + 1)
                    for m in range(2):
                        last = dve.tensor_tensor(V[0:M_ROWS[m], m, :, 0:HD], ps[0:M_ROWS[m], 5, D * m:D * m + D].rearrange("p (h f) -> p h f", f=HD),
                                                 t("wv_b")[0:M_ROWS[m], :].rearrange("p (h f) -> p h f", f=HD), ALU.add)
                    last.then_inc(v_kept, 1)
                    dve.wait_ge(scored, b + 1)
                    dve.tensor_reduce(mx[:, :].rearrange("p (h n) -> p h n", n=2), sv, AX.X, ALU.max).then_inc(maxed, 1)
                    dve.wait_ge(maxed, b + 1)
                    dve.tensor_tensor(S[:, :, :].rearrange("p (h n) m -> p h n m", n=2), sv,
                                      mx[:, :].rearrange("p (h n) -> p h n", n=2).unsqueeze(3).broadcast_to([Q_ROWS, 4, 2, SEQ]), ALU.subtract).then_inc(shifted, 1)
                    dve.wait_ge(turned, b * 2 + 2)
                    dve.tensor_copy(PT[0:M_ROWS[1], 1, :, :], ps[0:M_ROWS[1], 6:8, 0:HEADS * Q_ROWS]).then_inc(pt_kept, 1)
                    dve.wait_ge(mixed, b + 1)
                    dve.reciprocal(rc[:, :].unsqueeze(2), ov[:, :, HD:HD + 1]).then_inc(inverted, 1)
                    dve.wait_ge(inverted, b + 1)
                    dve.tensor_tensor(OB[:, :, :], ov[:, :, 0:HD], bc(rc[:, :], HD), ALU.mult).then_inc(rounded, 1)
                    dve.wait_ge(rounded, b + 1)
                    dve.wait_ge(sent, i * 64)
                    dve.tensor_copy(OF[:, s, :, :].rearrange("p n d -> p (n d)"), OB[:, :, :].rearrange("p n f -> p (n f)")).then_inc(widened, 1)

        @block.sync
        def _(sp):
            with sp.Fori(0, PAIRS) as i:
                for s in range(2):
                    b = 2 * i + s
                    sp.wait_ge(widened, b + 1)
                    row = rows[bass.ds(b, 1), :, :].rearrange("a s d -> (a s) d")
                    sp.dma_start(row[0:Q_ROWS, :], OF[:, s, 0, :]).then_inc(sent, 16)
                    sp.dma_start(row[Q_ROWS:SEQ, :], OF[1:Q_ROWS, s, 1, :]).then_inc(sent, 16)
            sp.wait_ge(sent, 32 * BATCH)


def pair_tokens(nc, X, HML):
    with nc.Block() as block:
        @block.vector
        def _(dve):
            for half in range(2):
                dve.tensor_copy(HML[:, 0, :, D * half:D * half + D], X[:, :, :])


def token_stages(nc, din, hid, att, result, upto=9):
    with ExitStack() as ctx:
        sb = lambda n, shape, dt=F32: ctx.enter_context(nc.sbuf_tensor(n, shape, dt))
        tpr = sb("tpr", [P, TPR_W])
        w = [sb(n, [P, SPLIT_W], BF16) for n in ("w_high", "w_middle", "w_stack")]
        eyeb = sb("eye_ones", [P, 2, P], BF16)
        H = sb("H", [P, NT, D])
        X = sb("X", [P, NT, D])
        B = sb("B", [P, NT, D])
        HML = sb("HML", [P, 2, NT, P], BF16)
        XP = sb("XP", [P, 2, NT * P], BF16)
        LG = sb("logits", [P, NT, EXPERTS])
        coef = sb("coef", [P, NT, EXPERTS])
        SQ = B[:, :, :].rearrange("p t d -> p (t d)")
        ones = eyeb[:, 1, :]
        raw = HML[:, :, :, :].rearrange("p a t d -> p (a t d)").bitcast(F32)[:, 0:SPLIT_W]
        rest = XP[:, :, :].rearrange("p a n -> p (a n)").bitcast(F32)[:, 0:SPLIT_W]
        load_tokens(nc, "first", hid, H, [(tpr[:, :], din["tokprm"]), (raw, din["weights"])])
        split_weights(nc, raw, rest, tpr, *w, eyeb)
        if upto >= 1:
            with nc.sbuf_tensor("row_sums", [P, FULL_T + 1, TC], F32) as SUM:
                token_norm(nc, "n0", H, X, SQ, HML, unit=X)
                turn_tokens(nc, "t0", HML, eyeb, XP)
                global_attention(nc, HML, XP, B, tpr, SUM)
                blend(nc, H, X, B, HML[:, :, :, :].rearrange("p a t d -> p (a t d)").bitcast(F32)[:, 0:NT * D], SUM)
        if upto >= 2:
            token_norm(nc, "n1", H, X, SQ, HML)
            turn_tokens(nc, "t1", HML, eyeb, XP, w, "router", LG)
            route(nc, "r1", LG, tpr, coef, 2)
            experts(nc, "moe", XP, tpr, w, ones, coef, B, 4, ACT.Gelu)
            add_to(nc, "a1", H, [X[:, :, :], B[:, :, :]])
        if upto >= 3:
            token_norm(nc, "n2", H, X, SQ, HML, clip=10000.0)
            turn_tokens(nc, "t2", HML, eyeb, XP)
            head_attention(nc, XP, tpr, w, att)
            load_tokens(nc, "second", att, X)
            pair_tokens(nc, X, HML)
            turn_tokens(nc, "t3", HML, eyeb, XP, w, "wo", B, parts=1)
            add_to(nc, "a2", H, [B[:, :, :]], bias=tpr[:, TPR["wo_b"][0]:sum(TPR["wo_b"])])
        if upto >= 4:
            token_norm(nc, "n3", H, X, SQ, HML)
            turn_tokens(nc, "t4", HML, eyeb, XP, w, "gate", LG)
            route(nc, "r4", LG, tpr, coef, 1, "gate_b")
            experts(nc, "ffn", XP, tpr, w, ones, coef, B, 16, ACT.Relu)
            add_to(nc, "a3", H, [B[:, :, :]], guard=True)
        with nc.semaphore("result_stored") as stored, nc.Block() as block:
            @block.sync
            def _(sp):
                sp.dma_start(result[0:FULL_T * P, :].rearrange("(t p) d -> p t d", p=P), H[:, 0:FULL_T, :]).then_inc(stored, 16)
                sp.dma_start(result[FULL_T * P:TOK, :], H[0:REST, FULL_T, :]).then_inc(stored, 16)
                sp.wait_ge(stored, 32)


def program(nc, din, result):
    spec_ready = nc.dram_tensor("spec_ready", (LAYERS, P, MODES * MODES * 2 * CH), F32, kind="Internal").ap()
    hid = nc.dram_tensor("hid", (TOK, D), F32, kind="Internal").ap()
    att = nc.dram_tensor("att", (TOK, D), F32, kind="Internal").ap()
    with ExitStack() as ctx:
        sb = lambda name, shape: ctx.enter_context(nc.sbuf_tensor(name, shape, F32))
        prm = sb("prm", [P, PRM_W])
        tab = sb("tab", [P, TABLES.shape[1]])
        fc0c = sb("fc0_centered", [3 * TILE_IMG, P])
        operator_setup(nc, din, spec_ready, prm, tab, fc0c)
        operator(nc, din, spec_ready, hid, prm, tab, fc0c)
    token_stages(nc, din, hid, att, result)


def kernel(**inputs):
    import concourse.bacc as bacc
    from concourse.bass_utils import run_bass_kernel_spmd

    i = {k: np.asarray(v) for k, v in inputs.items()}
    host = {**layout_operator(i), **layout_tokens(i), "txt": i["txt"].reshape(BATCH, TXT * D)}
    nc = bacc.Bacc("TRN2", target_bir_lowering=False, num_devices=1)
    arrays = {f"in_{k}": np.ascontiguousarray(v) for k, v in host.items()}
    din = {k: nc.dram_tensor(f"in_{k}", v.shape, F32, kind="ExternalInput").ap() for k, v in host.items()}
    result = nc.dram_tensor("result", (TOK, D), F32, kind="ExternalOutput").ap()
    program(nc, din, result)
    r = run_bass_kernel_spmd(nc, [arrays], core_ids=[0])
    return r.results[0]["result"].reshape(BATCH, SEQ, D)
```

```python
from contextlib import ExitStack

import numpy as np

import concourse.bass as bass
from concourse import mybir

F32 = mybir.dt.float32
BF16 = mybir.dt.bfloat16
ALU = mybir.AluOpType
ACT = mybir.ActivationFunctionType
AX = mybir.AxisListType

P = 128
BATCH, SIDE, CH = 64, 64, 32
LAYERS, MODES = 4, 12
PIX = SIDE * SIDE
OCT = 8
TILE_IMG = P // CH
TILES = OCT // TILE_IMG
N_OCT = BATCH // OCT
NORMS = LAYERS + 1
CHUNK = 512
CHUNKS = PIX // CHUNK
KRI = 2 * MODES
HBLK = 4
N_HBLK = SIDE // HBLK
TXT = 77
SEQ = SIDE + TXT
D = 64
TOK = BATCH * SEQ
NT = 72
FULL_T = TOK // P
REST = TOK - FULL_T * P
LN_EPS = 1e-5


PIX_STACK = ((0, 0, 0), (12, 0, 1), (32, 0, 2), (64, 1, 0), (76, 1, 1), (96, 2, 0))


def fourier_tables():
    n = np.arange(SIDE)
    ky = np.arange(MODES)
    kx = np.concatenate([np.arange(MODES), np.arange(SIDE - MODES, SIDE)])
    aw = 2 * np.pi * np.outer(n, ky) / SIDE
    ah = 2 * np.pi * np.outer(n, kx) / SIDE
    fw = np.zeros((2, TILE_IMG, 32, MODES, 2, TILE_IMG))
    for half in range(2):
        a = aw[32 * half:32 * half + 32]
        for b in range(TILE_IMG):
            fw[half, b, :, :, 0, b] = np.cos(a)
            fw[half, b, :, :, 1, b] = -np.sin(a)
    fh = np.zeros((2, TILES, SIDE, TILES, 2, 2, MODES))
    c, s = np.cos(ah).reshape(SIDE, 2, MODES), np.sin(ah).reshape(SIDE, 2, MODES)
    for g in range(TILES):
        fh[0, g, :, g, :, 0], fh[0, g, :, g, :, 1] = c, -s
        fh[1, g, :, g, :, 0], fh[1, g, :, g, :, 1] = s, c
    ih = np.zeros((2, 2, 32, SIDE, 2))
    for st in range(2):
        ih[st, 0, :MODES, :, 0], ih[st, 0, :MODES, :, 1] = c[:, st].T, s[:, st].T
        ih[st, 1, :MODES, :, 0], ih[st, 1, :MODES, :, 1] = -s[:, st].T, c[:, st].T
    iw = np.zeros((HBLK, MODES, 2, HBLK, SIDE))
    weight = np.where(ky == 0, 1.0, 2.0)[:, None] / PIX
    for h in range(HBLK):
        iw[h, :, 0, h] = weight * np.cos(aw).T
        iw[h, :, 1, h] = -weight * np.sin(aw).T
    eye = np.eye(P)
    mean = np.kron(np.eye(TILE_IMG), np.full((CH, CH), 1.0 / CH))
    sign = np.ones((P, 1))
    sign[32:64], sign[96:128] = -1.0, -1.0
    part = np.zeros((P, 3))
    for row, _, n in PIX_STACK:
        part[row:row + 3 * TILE_IMG, n] = 1
    parts = {
        "fw0": fw[0].reshape(P, -1), "fw1": fw[1].reshape(P, -1),
        "fh0": fh[0].reshape(P, -1), "fh1": fh[1].reshape(P, -1),
        "ih": ih.reshape(P, -1), "iw": np.pad(iw.reshape(HBLK * KRI, -1), ((0, P - HBLK * KRI), (0, 0))),
        "mean": mean, "center": eye - mean, "sign": sign, "part": part,
    }
    at, n = {}, 0
    for name, a in parts.items():
        at[name] = (n, a.shape[1])
        n += a.shape[1]
    return np.concatenate(list(parts.values()), axis=1).astype(np.float32), at


TABLES, TABLE_AT = fourier_tables()
PRM = {}
_n = 0
for _name, _w in (("bias", NORMS), ("gain", NORMS), ("shift", NORMS), ("fc1b", 1), ("fc2b", 1), ("fc3b", 1),
                  ("fc0", P), ("conv", LAYERS * P), ("fc1", 128), ("fc2", 64), ("fc3", 2)):
    PRM[_name] = (_n, _w)
    _n += _w
PRM_W = _n


def layout_operator(i):
    p = np.zeros((P, PRM_W), np.float32)

    def put(name, a):
        n, w = PRM[name]
        p[:, n:n + w] = a

    def four(v):
        return np.tile(v, TILE_IMG)

    put("bias", np.stack([four(i["L0_tok_fc0_b"])] + [four(v) for v in i["L0_tok_conv_b"]], 1))
    put("gain", np.stack([four(i["L0_tok_ln0_g"])] + [four(v) for v in i["L0_tok_ln_g"]], 1))
    put("shift", np.stack([four(i["L0_tok_ln0_b"])] + [four(v) for v in i["L0_tok_ln_b"]], 1))
    put("fc1b", i["L0_tok_fc1_b"][:, None])
    put("fc2b", np.tile(i["L0_tok_fc2_b"], 2)[:, None])
    put("fc3b", np.broadcast_to(i["L0_tok_fc3_b"][None, :], (P, 1)))
    fc0 = np.zeros((TILE_IMG, CH, TILE_IMG, 3), np.float32)
    conv = np.zeros((TILE_IMG, CH, LAYERS, TILE_IMG, CH), np.float32)
    for b in range(TILE_IMG):
        fc0[b, :, b, :] = i["L0_tok_fc0_w"].T
        conv[b, :, :, b, :] = i["L0_tok_conv_w"].transpose(1, 0, 2)
    stack = np.zeros((P, P), np.float32)
    for row, _, _ in PIX_STACK:
        stack[:, row:row + 3 * TILE_IMG] = fc0.reshape(P, -1)
    put("fc0", stack)
    put("conv", conv.reshape(P, -1))
    put("fc1", np.tile(i["L0_tok_fc1_w"], (TILE_IMG, 1)))
    put("fc2", i["L0_tok_fc2_w"])
    fc3 = np.zeros((2, 64, 2), np.float32)
    for s in range(2):
        fc3[s, :, s] = i["L0_tok_fc3_w"][:, 0]
    put("fc3", fc3.reshape(P, 2))
    w = np.empty((LAYERS, 2, 2, CH, MODES, MODES, 2, CH), np.float32)
    for st, (re, im) in enumerate((("L0_tok_w1r", "L0_tok_w1i"), ("L0_tok_w2r", "L0_tok_w2i"))):
        r = i[re].transpose(0, 1, 4, 3, 2)
        m = i[im].transpose(0, 1, 4, 3, 2)
        w[:, st, 0, :, :, :, 0], w[:, st, 0, :, :, :, 1] = r, m
        w[:, st, 1, :, :, :, 0], w[:, st, 1, :, :, :, 1] = m, r
    x = i["x"].transpose(0, 3, 1, 2).reshape(N_OCT, TILES, TILE_IMG * 3, PIX)
    pix = np.zeros((N_OCT, P, TILES, PIX), np.float32)
    for row, _, _ in PIX_STACK:
        pix[:, row:row + 3 * TILE_IMG] = x.transpose(0, 2, 1, 3)
    return {"tables": TABLES, "prm": p, "spec": w.reshape(LAYERS, P, MODES * MODES * 2 * CH), "pix": pix}


def operator_setup(nc, din, prm, tab, fc0c, fc1p):
    t = lambda name: tab[:, TABLE_AT[name][0]:sum(TABLE_AT[name])]
    q = lambda name: prm[:, PRM[name][0]:sum(PRM[name])]
    with ExitStack() as ctx:
        sem = lambda name: ctx.enter_context(nc.semaphore(name))
        ps = ctx.enter_context(nc.psum_tensor("setup_ps", [P, 2, CHUNK], F32))
        tables_in, centered, negated, step = sem("tables_in"), sem("centered"), sem("negated"), sem("fc0_step")
        rest = ctx.enter_context(nc.sbuf_tensor("fc0_rest", [P, P], F32))
        high = ctx.enter_context(nc.sbuf_tensor("fc0_part", [P, P], BF16))
        chosen = ctx.enter_context(nc.sbuf_tensor("fc0_chosen", [P, P], F32))
        block = ctx.enter_context(nc.Block())

        @block.sync
        def _(sp):
            sp.dma_start(prm[:, :], din["prm"]).then_inc(tables_in, 16)
            sp.dma_start(tab[:, :], din["tables"]).then_inc(tables_in, 16)
            sp.wait_ge(tables_in, 32)

        @block.vector
        def _(dve):
            dve.wait_ge(tables_in, 32)
            dve.memset(fc1p[:, :, :], 0.0)
            dve.tensor_scalar(q("gain"), q("gain"), -1.0, None, ALU.mult).then_inc(negated, 1)
            dve.wait_ge(negated, 1)
            last = q("gain")[:, LAYERS:NORMS]
            for b in range(TILE_IMG):
                rows = slice(CH * b, CH * b + CH)
                dve.tensor_scalar(fc1p[rows, b, :], q("fc1")[rows, :], last[rows, :], None, ALU.mult)
            dve.wait_ge(centered, 1)
            dve.tensor_copy(q("conv"), ps[:, 0, :])
            dve.tensor_copy(q("bias"), ps[:, 1, 0:NORMS])
            dve.tensor_tensor(q("fc1b"), q("fc1b"), ps[:, 1, NORMS:NORMS + 1], ALU.add)
            count = 0

            def link(ins):
                nonlocal count
                count += 1
                ins.then_inc(step, 1)
                dve.wait_ge(step, count)

            part = t("part")
            link(dve.tensor_copy(rest[:, :], ps[:, 1, P:2 * P]))
            for n in range(3):
                link(dve.tensor_copy(high[:, :], rest[:, :]))
                if n == 0:
                    link(dve.tensor_scalar(chosen[:, :], high[:, :], part[:, 0:1], None, ALU.mult))
                else:
                    link(dve.scalar_tensor_tensor(out=chosen[:, :], in0=high[:, :], scalar=part[:, n:n + 1], in1=chosen[:, :], op0=ALU.mult, op1=ALU.add))
                if n < 2:
                    link(dve.tensor_tensor(rest[:, :], rest[:, :], high[:, :], ALU.subtract))
            dve.tensor_copy(fc0c[:, :], chosen[:, :])

        @block.tensor
        def _(pe):
            pe.wait_ge(tables_in, 32)
            for layer in range(LAYERS):
                pe.matmul(ps[:, 0, P * layer:P * layer + P], q("conv")[:, P * layer:P * layer + P], t("center"), start=True, stop=True)
            pe.matmul(ps[:, 1, 0:NORMS], t("center"), q("bias"), start=True, stop=True)
            pe.matmul(ps[:, 1, NORMS:NORMS + 1], q("fc1")[0:CH, :], q("shift")[0:CH, LAYERS:NORMS], start=True, stop=True)
            pe.matmul(ps[:, 1, P:2 * P], q("fc0"), t("center"), start=True, stop=True).then_inc(centered, 1)


def operator(nc, din, hid, prm, tab, fc0c, fc1p, n_oct=N_OCT):
    t = lambda name: tab[:, TABLE_AT[name][0]:sum(TABLE_AT[name])]
    q = lambda name, rows=P: prm[0:rows, PRM[name][0]:sum(PRM[name])]
    tok = hid.rearrange("(b s) d -> b (s d)", s=SEQ)
    with ExitStack() as ctx:
        sb = lambda name, shape: ctx.enter_context(nc.sbuf_tensor(name, shape, F32))
        sem = lambda name: ctx.enter_context(nc.semaphore(name))
        YB, VB = 5, 3
        LAG = 2
        Z = sb("Z", [P, TILES, PIX])
        ZW = sb("ZW", [P, TILES, PIX])
        WS = sb("WS", [P, MODES * MODES, 2 * CH])
        MB = sb("MB", [P, MODES * MODES, 2, OCT])
        Y = sb("Y", [P, MODES, OCT, 32])
        YT = sb("YT", [P, MODES, OCT, 32])
        U = sb("U", [P, KRI, TILE_IMG, CH])
        T = sb("T", [P, TILES, SIDE, MODES, 2])
        TT = sb("TT", [HBLK * KRI, TILES, N_HBLK, P])
        SQ = sb("SQ", [P, YB, CHUNK])
        RS = sb("RS", [P, YB, CHUNK])
        conv = sb("conv_now", [P, P])
        vecs = sb("vecs_now", [P, 4])
        epsb = sb("epsb", [P, 2])
        PIXELS = [A.bitcast(BF16)[:, 0:PIX] for A in (U[:, :, :, :].rearrange("p k b c -> p (k b c)"), T[:, :, :, :, :].rearrange("p t h k r -> p (t h k r)"))]
        zero = ctx.enter_context(nc.sbuf_tensor("zero", [P, 4 * 96], BF16))
        OUT = TT[0:2, :, :, :].rearrange("p t a n -> p (t a n)")
        PS = ctx.enter_context(nc.psum_tensor("PS", [P, 8, CHUNK], F32))
        psf = PS[:, :, :].rearrange("p a n -> p (a n)")
        (pix_in, pix_step, pix_split, weights_in, weights_signed, prepared, octet_free, out_free, vecs_ready, conv_ready, y_done, sq_done, var_done, root_done,
         half_square_done, scaled, corrected, norm_done, z_done, turned, u_mm, u_kept_even, u_kept_odd, v_mm, v_kept_low, v_kept, mix_mm,
         mix_kept, mix_kept_other, y_turned, t_mm, t_kept, t_kept_other, tt_mm, tt_kept_even, tt_kept_odd,
         fc1_mm, fc1_act, fc2_mm, fc2_act, fc3_mm, fc3_kept, out_sent, text_sent) = (sem(n) for n in (
             "pix_in pix_step pix_split weights_in weights_signed prepared octet_free out_free vecs_ready conv_ready y_done sq_done var_done root_done "
             "half_square_done scaled corrected norm_done z_done turned u_mm u_kept_even u_kept_odd v_mm v_kept_low v_kept mix_mm "
             "mix_kept mix_kept_other y_turned t_mm t_kept t_kept_other tt_mm tt_kept_even tt_kept_odd "
             "fc1_mm fc1_act fc2_mm fc2_act fc3_mm fc3_kept out_sent text_sent").split())
        NCH = TILES * CHUNKS
        PAIRS = OCT // 2
        NM = PAIRS * CHUNKS
        WIDE = SIDE // 2
        JN = CHUNKS // 2
        rows_of = lambda a: a.rearrange("p (h w) -> p h w", w=SIDE)
        of_bank = lambda a: a.rearrange("p (h w) -> p h w", w=WIDE)

        def pixels(A, c):
            v, g, j = c // (TILES * JN), c // JN % TILES, c % JN
            return rows_of(A[g])[:, 16 * j:16 * j + 16, WIDE * v:WIDE * v + WIDE]

        FINISH_AT = (12, 12, NCH + LAG - 1, NCH + LAG - 1)
        TURN_AT = (10, 10, NCH, NCH)
        half_of = lambda A, k: rows_of(A[k % TILES])[:, :, WIDE * (k // TILES):WIDE * (k // TILES) + WIDE]
        HALVES = len(TURN_AT)
        ZT, ZWT = [Z[:, g, :] for g in range(TILES)], [ZW[:, g, :] for g in range(TILES)]
        LEFT = sorted([(c % YB, c, True) for c in range(NCH - YB, NCH)] + [(YB + c % VB, c, False) for c in range(NCH - VB, NCH)], key=lambda b: b[1])
        H1 = [SQ[:, 0:2, :], SQ[:, 2:4, :]]
        H2 = [RS[:, 0, :], RS[:, 1, :]]

        def keep_modes(copy, y0, y1):
            for img in range(TILE_IMG):
                for st in range(2):
                    for ri in range(2):
                        src = psf[32 * img:32 * img + 32, P * y0:P * y1].rearrange("p (y n) -> p y n", n=P)[:, :, 0:96]
                        src = src.rearrange("p y (g s r x) -> p y g s r x", g=2, s=2, r=2)[:, :, :, st, ri, :]
                        at = 64 * st + 32 * ri
                        dst = MB[at:at + 32, MODES * y0:MODES * y1, st, :].rearrange("p (y x) (g i) -> p y g i x", x=MODES, i=TILE_IMG)[:, :, :, img, :]
                        last = copy(dst, src)
            return last

        def keep_mix(copy, part, st):
            src = psf[0:2 * CH, (3 - 3 * part) * CHUNK:(6 - 3 * part) * CHUNK].rearrange("p (y n) -> p y n", n=256)[:, :, 0:192]
            src = src.rearrange("p y (x s b) -> p y x s b", x=MODES, s=2)[:, :, :, st, :]
            dst = Y[64 * st:64 * st + 64, 6 * part:6 * part + 6, :, 0:MODES].rearrange("p y b x -> p y x b")
            return copy(dst, src)

        def t_at(half, g, ky):
            return (3 * CHUNK + 768 * g if half == 0 else 6 * CHUNK * g) + P * (ky - 6 * half)

        def keep_t(copy, half, g):
            at = t_at(half, g, 6 * half)
            src = psf[:, at:at + 768].rearrange("p (y h r) -> p y h r", h=SIDE, r=2)
            return copy(T[:, g, :, 6 * half:6 * half + 6, :].rearrange("p h y r -> p y h r"), src)

        block = ctx.enter_context(nc.Block())

        @block.sync
        def _(sp):
            for b in range(4):
                sp.dma_start(tok[16 * b:16 * b + 16, SIDE * D:], din["txt"][16 * b:16 * b + 16, :]).then_inc(text_sent, 16)
            sp.sem_inc(out_free, 1)

            def load_pixels(octet):
                sp.dma_start(ZW[:, :, :], din["pix"][bass.ds(octet, 1), :, :, :].rearrange("a p t n -> (a p) t n")).then_inc(pix_in, 16)

            def transfers(octet, after):
                with sp.Fori(0, LAYERS) as layer:
                    sp.wait_ge(mix_mm, (octet * LAYERS + layer) * 2 + 1)
                    sp.dma_start(WS[:, :, :], din["spec"][bass.ds(layer, 1), :, :].rearrange("a p (m n) -> p (a m) n", n=2 * CH)).then_inc(weights_in, 16)
                sp.wait_ge(u_mm, (octet + 1) * (LAYERS * 8))
                load_pixels(after)
                for pair in range(PAIRS):
                    sp.wait_ge(fc3_kept, octet * NM + (pair + 1) * CHUNKS)
                    sp.dma_start(tok[bass.ds(octet * OCT + 2 * pair, 2), 0:PIX], OUT).then_inc(out_sent, 16)
                sp.wait_ge(out_sent, (octet + 1) * (16 * PAIRS))
                sp.sem_inc(out_free, 1)

            load_pixels(0)
            if n_oct > 1:
                with sp.Fori(0, n_oct - 1) as octet:
                    transfers(octet, octet + 1)
            transfers(n_oct - 1, n_oct - 1)
            sp.wait_ge(text_sent, 64)

        @block.gpsimd
        def _(pool):
            with pool.Fori(0, n_oct * LAYERS) as it:
                pool.wait_ge(weights_in, it * 16 + 16)
                pool.tensor_tensor(WS[:, :, 0:CH], WS[:, :, 0:CH], t("sign").unsqueeze(2).broadcast_to([P, MODES * MODES, CH]), ALU.mult).then_inc(weights_signed, 1)

        @block.tensor
        def _(pe):
            def norm(n, make):
                for c in range(NCH + LAG):
                    if c < NCH:
                        if c >= YB:
                            pe.wait_ge(scaled, n * NCH + c - YB + 1)
                        make(c).then_inc(y_done, 1)
                    if c >= LAG:
                        v = c - LAG
                        if v >= VB:
                            pe.wait_ge(corrected, n * NCH + v - VB + 1)
                        pe.wait_ge(sq_done, n * NCH + v + 1)
                        pe.matmul(PS[:, YB + v % VB, :], t("mean"), SQ[:, v % YB, :], start=True, stop=True).then_inc(var_done, 1)

            def first(octet):
                def make(c):
                    pe.wait_ge(pix_split, octet * NCH + c + 1)
                    return pe.matmul(PS[:, c % YB, :], fc0c[:, :], pixels(PIXELS, c), start=True, stop=True)
                return make

            def layer_step(it, n):
                columns = lambda half, c: ZW[:, :, :].rearrange("p t (h v c) -> p t h v c", v=2, c=CH)[:, :, :, half, c]
                pe.wait_ge(turned, it * HALVES + TILES)
                for bank, last, of_y in LEFT:
                    if of_y:
                        pe.wait_ge(scaled, (n - 1) * NCH + last + 1)
                    else:
                        pe.wait_ge(corrected, (n - 1) * NCH + last + 1)
                    pe.matmul(PS[:, bank, 0:4 * 96], zero[:, 0:P], zero[:, :], start=True, stop=False)
                    for k in range(4):
                        pe.matmul(PS[:, bank, 96 * k:96 * k + 96], columns(0, 4 * bank + k), t("fw0"), start=False, stop=False)
                pe.wait_ge(turned, (it + 1) * HALVES)
                for bank in range(8):
                    for k in range(4):
                        mm = pe.matmul(PS[:, bank, 96 * k:96 * k + 96], columns(1, 4 * bank + k), t("fw1"), start=False, stop=(k == 3))
                    mm.then_inc(u_mm, 1)
                pe.wait_ge(u_kept_even, (it + 1) * 4)
                pe.wait_ge(u_kept_odd, (it + 1) * 4)
                for ky in range(MODES):
                    for ri in range(2):
                        mm = pe.matmul(psf[:, P * ky:P * ky + 96], U[:, 2 * ky + ri, :, :], t(f"fh{ri}"), start=(ri == 0), stop=(ri == 1))
                    if ky % 4 == 3:
                        mm.then_inc(v_mm, 1)
                pe.wait_ge(weights_signed, it + 1)
                pe.wait_ge(v_kept_low, it + 1)
                for part in range(2):
                    for m in range(72 * part, 72 * part + 72):
                        if m == 48:
                            pe.wait_ge(v_kept, it + 1)
                        at = (3 - 3 * part) * CHUNK + 256 * (m // 12 - 6 * part) + 16 * (m % 12)
                        mm = pe.matmul(psf[0:2 * CH, at:at + 16], WS[:, m, :], MB[:, m, :, :], start=True, stop=True)
                    mm.then_inc(mix_mm, 1)
                for half in range(2):
                    pe.wait_ge(y_turned, it * 2 + half + 1)
                    for g in range(TILES):
                        for ky in range(6 * half, 6 * half + 6):
                            at = t_at(half, g, ky)
                            mm = pe.matmul(psf[:, at:at + P], YT[:, ky, TILE_IMG * g:TILE_IMG * (g + 1), :], t("ih"), start=True, stop=True)
                    mm.then_inc(t_mm, 1)
                pe.wait_ge(t_kept, (it + 1) * 2)
                pe.wait_ge(t_kept_other, it + 1)
                for u in range(TILES * N_HBLK // 4):
                    g = u // 4
                    for k in range(4):
                        hb = 4 * (u % 4) + k
                        src = T[:, g, HBLK * hb:HBLK * (hb + 1), :, :].rearrange("p h k r -> p (h k r)")
                        mm = pe.matmul(PS[0:HBLK * KRI, u, P * k:P * k + P], src, t("center"), start=True, stop=True)
                    mm.then_inc(tt_mm, 1)
                pe.wait_ge(conv_ready, it + 1)

                def bank_kept(u):
                    if u % 2 == 0:
                        pe.wait_ge(tt_kept_even, it * 4 + u // 2 + 1)
                    else:
                        pe.wait_ge(tt_kept_odd, it * 4 + u // 2 + 1)

                def both(c):
                    if c < YB:
                        bank_kept(c)
                    if LAG <= c < LAG + VB:
                        bank_kept(YB + c - LAG)
                    v, g, j = c // (TILES * JN), c // JN % TILES, c % JN
                    table = t("iw")[0:HBLK * KRI, :].rearrange("p (h w) -> p h w", w=SIDE)[:, :, WIDE * v:WIDE * v + WIDE]
                    for k in range(4):
                        block = PS[:, c % YB, P * k:P * k + P]
                        pe.matmul(block, conv[:, :], pixels(ZT, c)[:, HBLK * k:HBLK * k + HBLK, :], start=True, stop=False)
                        mm = pe.matmul(block, TT[:, g, 4 * j + k, :], table, start=False, stop=True)
                    return mm

                norm(n, both)

            def mlp(octet):
                b = octet * NM
                for i in range(NM + 2):
                    pair, j = i // CHUNKS, i % CHUNKS
                    if i < NM:
                        if i >= 2:
                            pe.wait_ge(fc1_act, b + i - 1)
                        for s in range(2):
                            im = 2 * pair + s
                            mm = pe.matmul(PS[:, 2 * (i % 2) + s, :], fc1p[:, im % TILE_IMG, :], Z[:, im // TILE_IMG, CHUNK * j:CHUNK * (j + 1)],
                                           start=True, stop=True)
                        mm.then_inc(fc1_mm, 1)
                    if 1 <= i <= NM:
                        pe.wait_ge(fc1_act, b + i)
                        if i >= 3:
                            pe.wait_ge(fc2_act, b + i - 2)
                        for s in range(2):
                            mm = pe.matmul(PS[64 * s:64 * s + 64, 4 + (i - 1) % 2, :], q("fc2"), H1[(i - 1) % 2][:, s, :], start=True, stop=True)
                        mm.then_inc(fc2_mm, 1)
                    if i >= 2:
                        pe.wait_ge(fc2_act, b + i - 1)
                        if i >= 4:
                            pe.wait_ge(fc3_kept, b + i - 3)
                        pe.matmul(PS[0:2, 6 + i % 2, :], q("fc3"), H2[i % 2], start=True, stop=True).then_inc(fc3_mm, 1)

            pe.sem_inc(mix_mm, 1)
            with pe.Fori(0, n_oct) as octet:
                pe.wait_ge(octet_free, octet + 1)
                norm(octet * NORMS, first(octet))
                with pe.Fori(0, LAYERS) as layer:
                    layer_step(octet * LAYERS + layer, octet * NORMS + 1 + layer)
                pe.wait_ge(norm_done, (octet + 1) * (NORMS * NCH))
                mlp(octet)

        @block.scalar
        def _(act):
            def norm(n, func):
                def finish(k):
                    act.wait_ge(norm_done, n * NCH + JN * (k + 1))
                    act.activation(half_of(ZT, k), half_of(ZT, k), func, bias=vecs[:, 2:3], scale=vecs[:, 1:2]).then_inc(z_done, 1)

                act.wait_ge(vecs_ready, n + 1)
                for c in range(NCH + LAG):
                    if c < NCH:
                        act.wait_ge(y_done, n * NCH + c + 1)
                        if c >= YB:
                            act.wait_ge(norm_done, n * NCH + c - YB + 1)
                        act.activation(SQ[:, c % YB, :], PS[:, c % YB, :], ACT.Square, bias=vecs[:, 0:1]).then_inc(sq_done, 1)
                    if c >= LAG:
                        v = c - LAG
                        act.wait_ge(var_done, n * NCH + v + 1)
                        act.activation(RS[:, v % YB, :], PS[:, YB + v % VB, :], ACT.Abs_reciprocal_sqrt, bias=epsb[:, 0:1]).then_inc(root_done, 1)
                        act.wait_ge(root_done, n * NCH + v + 1)
                        act.activation(SQ[:, v % YB, :], RS[:, v % YB, :], ACT.Square, bias=epsb[:, 1:2], scale=0.5 ** 0.5).then_inc(half_square_done, 1)
                    for k in range(HALVES):
                        if FINISH_AT[k] == c and func is not None:
                            finish(k)

            def layer_step(it, n, func):
                for u in range(1, 8, 2):
                    act.wait_ge(u_mm, it * 8 + u + 1)
                    act.copy(U[:, :, :, 4 * u:4 * u + 4].rearrange("p k b c -> p c (k b)"),
                             PS[:, u, 0:384].rearrange("p (c k) -> p c k", c=4)).then_inc(u_kept_odd, 1)
                act.wait_ge(v_mm, it * 3 + 1)
                keep_modes(act.copy, 0, 4).then_inc(v_kept_low, 1)
                act.wait_ge(mix_mm, it * 2 + 2)
                keep_mix(act.copy, 0, 0).then_inc(mix_kept, 1)
                keep_mix(act.copy, 0, 1).then_inc(mix_kept, 1)
                act.wait_ge(t_mm, it * 2 + 1)
                for g in range(TILES):
                    last = keep_t(act.copy, 0, g)
                last.then_inc(t_kept, 1)
                act.wait_ge(t_mm, it * 2 + 2)
                keep_t(act.copy, 1, 1).then_inc(t_kept, 1)
                for u in range(1, 8, 2):
                    act.wait_ge(tt_mm, it * 8 + u + 1)
                    act.copy(TT[:, u // 4, 4 * (u % 4):4 * (u % 4) + 4, :], PS[0:HBLK * KRI, u, :].rearrange("p (a n) -> p a n", a=4)).then_inc(tt_kept_odd, 1)
                norm(n, func)

            def mlp(octet):
                b = octet * NM
                for i in range(NM + 1):
                    if i < NM:
                        act.wait_ge(fc1_mm, b + i + 1)
                        if i >= 2:
                            act.wait_ge(fc2_mm, b + i - 1)
                        act.activation(H1[i % 2], PS[:, 2 * (i % 2):2 * (i % 2) + 2, :], ACT.Gelu, bias=q("fc1b")).then_inc(fc1_act, 1)
                    if i >= 1:
                        act.wait_ge(fc2_mm, b + i)
                        if i >= 3:
                            act.wait_ge(fc3_mm, b + i - 2)
                        act.activation(H2[(i - 1) % 2], PS[:, 4 + (i - 1) % 2, :], ACT.Gelu, bias=q("fc2b")).then_inc(fc2_act, 1)

            act.wait_ge(prepared, 1)
            with act.Fori(0, n_oct) as octet:
                norm(octet * NORMS, ACT.Identity)
                act.wait_ge(out_free, octet + 1)
                with act.Fori(0, LAYERS - 1) as layer:
                    layer_step(octet * LAYERS + layer, octet * NORMS + 1 + layer, ACT.Gelu)
                layer_step(octet * LAYERS + LAYERS - 1, octet * NORMS + LAYERS, None)
                mlp(octet)

        @block.vector
        def _(dve):
            def norm(n, it=None):
                def turn(k):
                    dve.wait_ge(z_done, it * HALVES + k + 1)
                    dve.transpose(half_of(ZWT, k), half_of(ZT, k)).then_inc(turned, 1)

                for c in range(NCH + 1):
                    if c < NCH:
                        dve.wait_ge(root_done, n * NCH + c + 1)
                        dve.scalar_tensor_tensor(out=pixels(ZT, c), in0=of_bank(PS[:, c % YB, :]), scalar=vecs[:, 0:1],
                                                 in1=of_bank(RS[:, c % YB, :]), op0=ALU.add, op1=ALU.mult).then_inc(scaled, 1)
                        dve.wait_ge(half_square_done, n * NCH + c + 1)
                        dve.scalar_tensor_tensor(out=SQ[:, c % YB, :], in0=PS[:, YB + c % VB, :], scalar=LN_EPS,
                                                 in1=SQ[:, c % YB, :], op0=ALU.add, op1=ALU.mult).then_inc(corrected, 1)
                    if c >= 1:
                        v = c - 1
                        dve.wait_ge(corrected, n * NCH + v + 1)
                        z = pixels(ZT, v)
                        dve.scalar_tensor_tensor(out=z, in0=of_bank(SQ[:, v % YB, :]), scalar=1.5, in1=z, op0=ALU.subtract, op1=ALU.mult).then_inc(norm_done, 1)
                    for k in range(HALVES):
                        if TURN_AT[k] == c and it is not None:
                            turn(k)

            def split_pixels(octet, c):
                raw, to = pixels(ZWT, c), pixels(PIXELS, c)
                for k in range(5):
                    r = slice((0, 64, 64, 96, 96)[k], P)
                    if k % 2 == 0:
                        part = dve.tensor_copy(to[r, :, :], raw[r, :, :])
                    else:
                        part = dve.tensor_tensor(raw[r, :, :], raw[r, :, :], to[r, :, :], ALU.subtract)
                    if k < 4:
                        part.then_inc(pix_step, 1)
                        dve.wait_ge(pix_step, (octet * NCH + c) * 4 + k + 1)
                    else:
                        part.then_inc(pix_split, 1)

            def take_vecs(n, layer1):
                v = prm[:, 0:3 * NORMS].rearrange("p (k n) -> p k n", n=NORMS)
                v = v[:, :, 0:1] if layer1 is None else v[:, :, bass.ds(layer1, 1)]
                dve.tensor_copy(vecs[:, 0:3].unsqueeze(2), v).then_inc(vecs_ready, 1)

            def layer_step(it, n, layer, last):
                take_vecs(n, layer + 1)
                dve.tensor_copy(conv[:, :].unsqueeze(1), q("conv").rearrange("p (l n) -> p l n", n=P)[:, bass.ds(layer, 1), :]).then_inc(conv_ready, 1)
                for u in range(0, 8, 2):
                    dve.wait_ge(u_mm, it * 8 + u + 1)
                    dve.tensor_copy(U[:, :, :, 4 * u:4 * u + 4].rearrange("p k b c -> p c (k b)"),
                                    PS[:, u, 0:384].rearrange("p (c k) -> p c k", c=4)).then_inc(u_kept_even, 1)
                dve.wait_ge(v_mm, it * 3 + 3)
                keep_modes(dve.tensor_copy, 4, 12).then_inc(v_kept, 1)

                def turn_y(half):
                    dve.transpose(YT[:, 6 * half:6 * half + 6, :, :].rearrange("p y b x -> p (y b x)"),
                                  Y[:, 6 * half:6 * half + 6, :, :].rearrange("p y b x -> p (y b x)")).then_inc(y_turned, 1)

                dve.wait_ge(mix_kept, (it + 1) * 2)
                turn_y(0)
                dve.wait_ge(mix_mm, it * 2 + 3)
                for st in range(2):
                    kept = keep_mix(dve.tensor_copy, 1, st)
                kept.then_inc(mix_kept_other, 1)
                dve.wait_ge(mix_kept_other, it + 1)
                turn_y(1)
                dve.wait_ge(t_mm, it * 2 + 2)
                keep_t(dve.tensor_copy, 1, 0).then_inc(t_kept_other, 1)
                for u in range(0, 8, 2):
                    dve.wait_ge(tt_mm, it * 8 + u + 1)
                    dve.tensor_copy(TT[:, u // 4, 4 * (u % 4):4 * (u % 4) + 4, :], PS[0:HBLK * KRI, u, :].rearrange("p (a n) -> p a n", a=4)).then_inc(tt_kept_even, 1)
                norm(n, None if last else it + 1)

            dve.sem_inc(octet_free, 1)
            dve.memset(zero[:, :], 0.0)
            dve.memset(epsb[:, 0:1], LN_EPS)
            dve.memset(epsb[:, 1:2], 0.0)
            dve.memset(MB[:, :, :, :], 0.0)
            dve.memset(Y[:, :, :, :], 0.0).then_inc(prepared, 1)
            dve.wait_ge(prepared, 1)
            dve.wait_ge(pix_in, 16)
            for c in range(NCH):
                split_pixels(0, c)
            with dve.Fori(0, n_oct) as octet:
                take_vecs(octet * NORMS, None)
                norm(octet * NORMS, octet * LAYERS)
                with dve.Fori(0, LAYERS - 1) as layer:
                    layer_step(octet * LAYERS + layer, octet * NORMS + 1 + layer, layer, False)
                layer_step(octet * LAYERS + LAYERS - 1, octet * NORMS + LAYERS, LAYERS - 1, True)
                dve.wait_ge(out_free, octet + 1)
                for i in range(NM):
                    dve.wait_ge(fc3_mm, octet * NM + i + 1)
                    if i % CHUNKS == 0 and i > 0:
                        dve.wait_ge(out_sent, octet * (16 * PAIRS) + 16 * (i // CHUNKS))
                    dve.tensor_scalar(OUT[:, CHUNK * (i % CHUNKS):CHUNK * (i % CHUNKS + 1)], PS[0:2, 6 + i % 2, :], q("fc3b", 2), None, ALU.add).then_inc(fc3_kept, 1)
                    if i == 0:
                        dve.wait_ge(pix_in, octet * 16 + 32)
                    if i % 2 == 0:
                        split_pixels(octet + 1, i // 2)
                dve.sem_inc(octet_free, 1)


HEADS, HD = 4, 16
EXPERTS = 8
CAP = int(np.ceil(1.25 * TOK / EXPERTS))
Q_ROWS = (SEQ + 1) // 2
M_ROWS = (Q_ROWS, SEQ - Q_ROWS)
TC = NT // 4

TPR = {}
_n = 0
for _name, _w in (("router", EXPERTS), ("gate", EXPERTS), ("wq", P), ("wk", P), ("wv", D), ("wo", D), ("m_w1", 4 * P), ("f_w1", 16 * P),
                  ("m_w2", 4 * P), ("f_w2", 16 * D), ("m_b2", EXPERTS * D), ("f_b2", EXPERTS * D),
                  ("m_b1", 4), ("f_b1", 16), ("eye", P), ("tri", P), ("ones", P), ("rank", EXPERTS),
                  ("gate_b", EXPERTS), ("wo_b", D), ("wv_b", D), ("wq_b", 1), ("wk_b", 1)):
    TPR[_name] = (_n, _w)
    _n += _w
STACKED = sum(TPR["f_w1"])
SPLIT_W = sum(TPR["f_b2"])
TPR_W = _n - SPLIT_W
SPLIT_NAMES = [name for name, (at, _) in TPR.items() if at < SPLIT_W]
TPR = {name: (at if at < SPLIT_W else at - SPLIT_W, width) for name, (at, width) in TPR.items()}


def layout_tokens(i):
    split, rest = np.zeros((P, SPLIT_W), np.float32), np.zeros((P, TPR_W), np.float32)

    def put(name, a, rows=0):
        n, w = TPR[name]
        a = np.asarray(a).reshape(-1, w)
        (split if name in SPLIT_NAMES else rest)[rows:rows + a.shape[0], n:n + w] = a

    def twice(name, a):
        put(name, a)
        put(name, a, D)

    twice("router", i["L0_ffn_router_w"].T)
    twice("gate", i["L1_ffn_gate_w"])
    for name, w, b in (("wq", "L1_attn_Wq", "L1_attn_bq"), ("wk", "L1_attn_Wk", "L1_attn_bk")):
        a = np.zeros((D, HEADS, 32), np.float32)
        a[:, :, :HD] = i[w].T.reshape(D, HEADS, HD)
        twice(name, a)
        v = np.zeros((HEADS, 32), np.float32)
        v[:, :HD] = i[b].reshape(HEADS, HD)
        put(name + "_b", v)
    twice("wv", i["L1_attn_Wv"].T)
    twice("wo", i["L1_attn_Wo"].T)
    twice("m_w1", i["L0_ffn_w1"].transpose(1, 0, 2))
    twice("f_w1", i["L1_ffn_w1"].transpose(1, 0, 2))
    w2 = np.zeros((2, D, 4, 2, D), np.float32)
    for e in range(2):
        w2[e, :, :, e] = i["L0_ffn_w2"][e::2].transpose(1, 0, 2)
    put("m_w2", w2)
    put("f_w2", i["L1_ffn_w2"].reshape(16, P, D).transpose(1, 0, 2))
    put("m_b2", i["L0_ffn_b2"])
    put("f_b2", i["L1_ffn_b2"])
    for k in (32, 64):
        put("m_b2", i["L0_ffn_b2"], k)
        put("f_b2", i["L1_ffn_b2"], k)
    put("m_b1", i["L0_ffn_b1"].reshape(4, P).T)
    put("f_b1", i["L1_ffn_b1"].reshape(16, P).T)
    put("eye", np.eye(P))
    put("tri", np.triu(np.ones((P, P))))
    put("ones", np.ones((P, P)))
    put("rank", np.broadcast_to(np.arange(EXPERTS, 0, -1.0), (P, EXPERTS)))
    put("gate_b", np.broadcast_to(i["L1_ffn_gate_b"], (P, EXPERTS)))
    put("wo_b", np.broadcast_to(i["L1_attn_bo"], (P, D)))
    put("wv_b", np.broadcast_to(i["L1_attn_bv"], (P, D)))
    return {"weights": split, "tokprm": rest}


def bc(ap, n):
    return ap.unsqueeze(2).broadcast_to([ap.shape[0], ap.shape[1], n])


def chain_of(eng, step):
    count = [0]

    def link(ins):
        count[0] += 1
        ins.then_inc(step, 1)
        eng.wait_ge(step, count[0])
        return count[0]
    return link


def load_tokens(nc, name, src, X, more=()):
    with nc.semaphore(name + "_loaded") as loaded, nc.Block() as block:
        @block.sync
        def _(sp):
            sp.dma_start(X[:, 0:FULL_T, :], src[0:FULL_T * P, :].rearrange("(t p) d -> p t d", p=P)).then_inc(loaded, 16)
            sp.dma_start(X[0:REST, FULL_T, :], src[FULL_T * P:TOK, :]).then_inc(loaded, 16)
            for to, frm in more:
                sp.dma_start(to, frm).then_inc(loaded, 16)
            sp.wait_ge(loaded, 32 + 16 * len(more))

        @block.vector
        def _(dve):
            dve.memset(X[REST:P, FULL_T, :], 0.0)
            dve.memset(X[:, FULL_T + 1:NT, :], 0.0)


def split_weights(nc, raw, REM, tpr, WH, WM, WC, eyeb):
    with ExitStack() as ctx:
        step = ctx.enter_context(nc.semaphore("weights_step"))
        block = ctx.enter_context(nc.Block())

        @block.vector
        def _(dve):
            link = chain_of(dve, step)
            link(dve.tensor_copy(WH[:, :], raw))
            link(dve.tensor_tensor(REM, raw, WH[:, :], ALU.subtract))
            link(dve.tensor_copy(WM[:, :], REM))
            link(dve.tensor_tensor(WC[0:D, :], REM[0:D, :], WM[0:D, :], ALU.subtract))
            link(dve.tensor_tensor(WC[D:P, STACKED:SPLIT_W], REM[D:P, STACKED:SPLIT_W], WM[D:P, STACKED:SPLIT_W], ALU.subtract))
            link(dve.tensor_copy(WC[D:P, 0:STACKED], WH[D:P, 0:STACKED]))
            b = slice(TPR["m_b2"][0], SPLIT_W)
            link(dve.tensor_copy(WH[32:33, b], WM[32:33, b]))
            link(dve.tensor_copy(WH[64:65, b], WC[64:65, b]))
            o = slice(*(TPR["wo"][0], sum(TPR["wo"])))
            link(dve.tensor_copy(WH[D:P, o], WM[D:P, o]))
            link(dve.memset(WC[D:P, o], 0.0))
            dve.tensor_copy(eyeb[:, 0, :], tpr[:, TPR["eye"][0]:sum(TPR["eye"])])
            dve.tensor_copy(eyeb[:, 1, :], tpr[:, TPR["ones"][0]:sum(TPR["ones"])])


def token_norm(nc, name, H, X, SQ, HML, clip=None, unit=None):
    with ExitStack() as ctx:
        sb = lambda n, shape: ctx.enter_context(nc.sbuf_tensor(name + n, shape, F32))
        sem = lambda n: ctx.enter_context(nc.semaphore(name + n))
        st = sb("_stat", [P, 3, NT])
        cst = sb("_const", [P, 2])
        step, rooted, squared, high_made, middle_made = (sem("_" + n) for n in ("step", "rooted", "squared", "high_made", "middle_made"))
        block = ctx.enter_context(nc.Block())
        sq = SQ[:, 0:NT * D].rearrange("p (t d) -> p t d", d=D)
        HALVES = (slice(0, NT // 2), slice(NT // 2, NT))
        result = X if unit is None else unit
        marks = {}

        @block.vector
        def _(dve):
            link = chain_of(dve, step)
            dve.memset(cst[:, 0:1], LN_EPS)
            dve.memset(cst[:, 1:2], 0.0)
            for h in HALVES:
                link(dve.tensor_reduce(st[:, 0, h], H[:, h, :], AX.X, ALU.add))
                link(dve.tensor_scalar(st[:, 0, h], st[:, 0, h], 1.0 / D, None, ALU.mult))
                marks["centered", h.start] = link(dve.tensor_tensor(X[:, h, :], H[:, h, :], bc(st[:, 0, h], D), ALU.subtract))
            for n, h in enumerate(HALVES):
                dve.wait_ge(squared, n + 1)
                marks["variance", h.start] = link(dve.tensor_reduce(st[:, 1, h], sq[:, h, :], AX.X, ALU.add))
            for n, h in enumerate(HALVES):
                dve.wait_ge(rooted, n + 1)
                link(dve.reciprocal(st[:, 2, h], st[:, 1, h]))
                marks["normed", h.start] = link(dve.tensor_tensor(X[:, h, :], X[:, h, :], bc(st[:, 2, h], D), ALU.mult))
                if clip is not None:
                    marks["normed", h.start] = link(dve.tensor_scalar(X[:, h, :], X[:, h, :], clip, -clip, ALU.min, ALU.max))
            if unit is not None:
                for n, h in enumerate(HALVES):
                    dve.wait_ge(squared, len(HALVES) + n + 1)
                    marks["length", h.start] = link(dve.tensor_reduce(st[:, 1, h], sq[:, h, :], AX.X, ALU.add))
                for n, h in enumerate(HALVES):
                    dve.wait_ge(rooted, len(HALVES) + n + 1)
                    link(dve.tensor_scalar(st[:, 1, h], st[:, 1, h], 1e-12, None, ALU.max))
                    link(dve.reciprocal(st[:, 2, h], st[:, 1, h]))
                    marks["scaled", h.start] = link(dve.tensor_tensor(unit[:, h, :], X[:, h, :], bc(st[:, 2, h], D), ALU.mult))
            for n, h in enumerate(HALVES):
                dve.wait_ge(high_made, n + 1)
                marks["rest", h.start] = link(dve.tensor_tensor(sq[:, h, :], result[:, h, :], HML[:, 0, h, 0:D], ALU.subtract))
            for n, h in enumerate(HALVES):
                dve.wait_ge(middle_made, n + 1)
                link(dve.tensor_tensor(HML[:, 1, h, D:P], sq[:, h, :], HML[:, 0, h, D:P], ALU.subtract))

        @block.scalar
        def _(act):
            def squares_and_roots(before, after, bias, scale):
                for h in HALVES:
                    act.wait_ge(step, marks[before, h.start])
                    act.activation(sq[:, h, :], X[:, h, :], ACT.Square, bias=cst[:, 1:2]).then_inc(squared, 1)
                for h in HALVES:
                    act.wait_ge(step, marks[after, h.start])
                    act.activation(st[:, 1, h], st[:, 1, h], ACT.Sqrt, bias=bias, scale=scale).then_inc(rooted, 1)

            squares_and_roots("centered", "variance", cst[:, 0:1], 1.0 / D)
            if unit is not None:
                squares_and_roots("normed", "length", cst[:, 1:2], 1.0)
            for h in HALVES:
                act.wait_ge(step, marks["normed" if unit is None else "scaled", h.start])
                act.copy(HML[:, 0, h, 0:D], result[:, h, :]).then_inc(high_made, 1)
            for h in HALVES:
                act.wait_ge(step, marks["rest", h.start])
                act.copy(HML[:, 0, h, D:P], sq[:, h, :]).then_inc(middle_made, 1)
            for h in HALVES:
                act.copy(HML[:, 1, h, 0:D], result[:, h, :])


def start_at_one(eng, *sems, count=1):
    for s in sems:
        eng.sem_inc(s, count)


def turn_tokens(nc, name, HML, eyeb, XP, w=None, weight=None, out=None, parts=2):
    width = TPR[weight][1] if weight else 0
    c0 = TPR[weight][0] if weight else 0
    with ExitStack() as ctx:
        sem = lambda n: ctx.enter_context(nc.semaphore(name + n))
        ps = ctx.enter_context(nc.psum_tensor(name + "_ps", [P, 6, CHUNK], F32))
        turned, spread, spread_low, formed, kept = (sem("_" + n) for n in ("turned", "spread", "spread_low", "formed", "kept"))
        block = ctx.enter_context(nc.Block())

        @block.tensor
        def _(pe):
            with pe.Fori(0, TC // 2) as i:
                for s in range(2):
                    c = 2 * i + s
                    pe.wait_ge(spread, 1 + c - s)
                    if parts == 2:
                        pe.wait_ge(spread_low, 1 + c - s)
                    for part in range(parts):
                        for k in range(4):
                            mm = pe.matmul(ps[:, 2 * s + part, P * k:P * k + P], HML[:, part, bass.ds(c * 4 + k, 1), :].rearrange("p a n -> p (a n)"),
                                           eyeb[:, 0, :], start=True, stop=True)
                    mm.then_inc(turned, 1)
                if out is not None:
                    for s in range(2):
                        c = 2 * i + s
                        pe.wait_ge(kept, 1 + c - s)
                        pe.wait_ge(spread, 1 + c + 1)
                        if parts == 2:
                            pe.wait_ge(spread_low, 1 + c + 1)
                        terms = [(0, w[0]), (0, w[1]), (1, w[2])] if parts == 2 else [(0, w[0]), (0, w[2])]
                        for k in range(4):
                            for n, (part, wt) in enumerate(terms):
                                mm = pe.matmul(ps[:, 4 + s, width * k:width * k + width], XP[:, part, bass.ds(c * CHUNK + P * k, P)], wt[:, c0:c0 + width],
                                               start=(n == 0), stop=(n == len(terms) - 1))
                        mm.then_inc(formed, 1)

        @block.scalar
        def _(act):
            start_at_one(act, spread)
            with act.Fori(0, TC // 2) as i:
                for s in range(2):
                    c = 2 * i + s
                    act.wait_ge(turned, c + 1)
                    act.copy(XP[:, 0, bass.ds(c * CHUNK, CHUNK)], ps[:, 2 * s, :]).then_inc(spread, 1)

        @block.vector
        def _(dve):
            start_at_one(dve, spread_low, kept)
            with dve.Fori(0, TC // 2) as i:
                for s in range(2):
                    c = 2 * i + s
                    if parts == 2:
                        dve.wait_ge(turned, c + 1)
                        dve.tensor_copy(XP[:, 1, bass.ds(c * CHUNK, CHUNK)], ps[:, 2 * s + 1, :]).then_inc(spread_low, 1)
                if out is not None:
                    for s in range(2):
                        c = 2 * i + s
                        dve.wait_ge(formed, c + 1)
                        dve.tensor_copy(out[:, bass.ds(c * 4, 4), 0:width], ps[:, 4 + s, 0:4 * width].rearrange("p (a n) -> p a n", a=4)).then_inc(kept, 1)


def global_attention(nc, HML, XP, OA, tpr, SUM):
    NJ = FULL_T + 1
    NS = 4
    LAG = 3
    with ExitStack() as ctx:
        sb = lambda n, shape, dt=F32: ctx.enter_context(nc.sbuf_tensor(n, shape, dt))
        sem = lambda n: ctx.enter_context(nc.semaphore(n))
        E = sb("E", [P, NS, CHUNK])
        EH = sb("E_high", [P, NS, CHUNK], BF16)
        EL = sb("E_low", [P, NS, CHUNK], BF16)
        Q = sb("queries", [P, 2, 3, CHUNK], BF16)
        OT = sb("sums_feature", [P, 2, CHUNK])
        ps = ctx.enter_context(nc.psum_tensor("att_ps", [P, 8, CHUNK], F32))
        q_ready, scored, weighed, high, split, used, sums_kept, turned, placed = (sem("att_" + n) for n in (
            "q_ready", "scored", "weighed", "high", "split", "used", "sums_kept", "turned", "placed"))
        placed_low = sem("att_placed_low")
        block = ctx.enter_context(nc.Block())

        KEEP, TURN, PLACE, QUERIES = 3, 8, 12, 16

        def free(n, j):
            return NS + n * NJ + (j - NS + 1 if j >= NS else -((NJ - 1 - j) % NS))

        @block.tensor
        def _(pe):
            def score(n, half, j):
                if j == 0:
                    pe.wait_ge(q_ready, n + 1)
                pe.wait_ge(weighed, free(n, j))
                for k, part in enumerate((0, 0, 1)):
                    mm = pe.matmul(ps[:, j % NS, :], XP[:, part, P * j:P * j + P], Q[:, half, k, :], start=(k == 0), stop=(k == 2))
                mm.then_inc(scored, 1)

            def weigh(n, half, j):
                if j == 0:
                    pe.wait_ge(sums_kept, 2 + n - 1)
                pe.wait_ge(split, NS + n * NJ + j + 1)
                for k, e in enumerate((EH, EL)):
                    mm = pe.matmul(ps[:, 4 + half, :], HML[:, 0, j, :], e[:, j % NS, :], start=(j == 0 and k == 0), stop=(j == NJ - 1 and k == 1))
                mm.then_inc(used, 1)

            def turn_back(n, half):
                pe.wait_ge(sums_kept, 2 + n + 1)
                pe.wait_ge(placed, 2 + n - 1)
                for k in range(4):
                    mm = pe.transpose(ps[:, 6 + half, P * k:P * k + P], OT[:, half, P * k:P * k + P], tpr[:, TPR["eye"][0]:sum(TPR["eye"])])
                mm.then_inc(turned, 1)

            def chunk(n, half, first=False, last=False):
                for j in range(NJ):
                    if j + LAG < NJ:
                        score(n, half, j + LAG)
                    elif not last:
                        score(n + 1, 1 - half, j + LAG - NJ)
                    weigh(n, half, j)
                    if j == TURN and not first:
                        turn_back(n - 1, 1 - half)

            start_at_one(pe, used, count=NS)
            for j in range(LAG):
                score(0, 0, j)
            chunk(0, 0, first=True)
            with pe.Fori(0, TC // 2 - 1) as i:
                chunk(2 * i + 1, 1)
                chunk(2 * i + 2, 0)
            chunk(TC - 1, 1, last=True)
            turn_back(TC - 1, 1)

        @block.scalar
        def _(act):
            start_at_one(act, weighed, count=NS)
            with act.Fori(0, TC) as n:
                for j in range(NJ):
                    act.wait_ge(scored, n * NJ + j + 1)
                    act.wait_ge(split, free(n, j))
                    act.activation(E[:, j % NS, :], ps[:, j % NS, :], ACT.Exp, accum_out=SUM[:, j, bass.ds(n, 1)]).then_inc(weighed, 1)

        @block.vector
        def _(dve):
            STACKS = [(k, to, frm, part) for k, halves in enumerate((((0, 0), (0, 0)), ((D, 0), (D, 0)), ((D, 1), (0, 1))))
                      for to, (frm, part) in zip((0, D), halves)]

            def queries(n, slot, step):
                k, to, frm, part = STACKS[step]
                copy = dve.tensor_copy(Q[to:to + D, slot, k, :], XP[frm:frm + D, part, bass.ds(n * CHUNK, CHUNK)])
                if step == len(STACKS) - 1:
                    copy.then_inc(q_ready, 1)

            def keep(n, half):
                dve.wait_ge(used, NS + (n + 1) * NJ)
                dve.tensor_copy(OT[:, half, :], ps[:, 4 + half, :]).then_inc(sums_kept, 1)

            def place(n, half):
                dve.wait_ge(turned, n + 1)
                src = ps[:, 6 + half, :].rearrange("p (a k d) -> p a k d", a=4, k=2)
                dve.tensor_copy(OA[:, bass.ds(n * 4, 4), 0:D], src[:, :, 0, :]).then_inc(placed_low, 1)
                dve.wait_ge(placed_low, n + 1)
                dve.tensor_tensor(OA[:, bass.ds(n * 4, 4), 0:D], OA[:, bass.ds(n * 4, 4), 0:D], src[:, :, 1, :], ALU.add).then_inc(placed, 1)

            def chunk(n, half, first=False, last=False):
                for j in range(NJ):
                    dve.wait_ge(weighed, NS + n * NJ + j + 1)
                    dve.wait_ge(used, free(n, j))
                    dve.tensor_copy(EH[:, j % NS, :], E[:, j % NS, :]).then_inc(high, 1)
                    dve.wait_ge(high, n * NJ + j + 1)
                    dve.tensor_tensor(EL[:, j % NS, :], E[:, j % NS, :], EH[:, j % NS, :], ALU.subtract).then_inc(split, 1)
                    if j == KEEP and not first:
                        keep(n - 1, 1 - half)
                    if j == PLACE and not first:
                        place(n - 1, 1 - half)
                    if QUERIES <= j < QUERIES + len(STACKS) and not last:
                        if j == QUERIES:
                            dve.wait_ge(used, NS + n * NJ)
                        queries(n + 1, 1 - half, j - QUERIES)

            start_at_one(dve, split, count=NS)
            start_at_one(dve, sums_kept, placed, count=2)
            for step in range(len(STACKS)):
                queries(0, 0, step)
            chunk(0, 0, first=True)
            with dve.Fori(0, TC // 2 - 1) as i:
                chunk(2 * i + 1, 1)
                chunk(2 * i + 2, 0)
            chunk(TC - 1, 1, last=True)
            keep(TC - 1, 1)
            place(TC - 1, 1)


def blend(nc, H, FA, OA, SQ, SUM):
    with ExitStack() as ctx:
        st = ctx.enter_context(nc.sbuf_tensor("blend_stat", [P, 2, NT], F32))
        NJ = FULL_T + 1
        zero = ctx.enter_context(nc.sbuf_tensor("blend_zero", [P, 2], F32))
        weighed = ctx.enter_context(nc.semaphore("blend_weighed"))
        step, squared, rooted = (ctx.enter_context(nc.semaphore("blend_" + n)) for n in ("step", "squared", "rooted"))
        sq = SQ[:, 0:NT * D].rearrange("p (t d) -> p t d", d=D)
        block = ctx.enter_context(nc.Block())
        marks = {}

        @block.vector
        def _(dve):
            link = chain_of(dve, step)
            att = OA[:, :, 0:D]
            link(dve.memset(zero[:, 0:1], 0.0))
            marks["zero"] = 1
            link(dve.memset(st[:, 0, :], float(NT * P)))
            link(dve.tensor_reduce(st[:, 0, 0:NJ], SUM[:, :, :], AX.X, ALU.add))
            dve.wait_ge(weighed, 1)
            link(dve.tensor_scalar(zero[:, 1:2], zero[:, 1:2], float(NT * P - TOK), None, ALU.mult))
            link(dve.tensor_scalar(st[:, 0, :], st[:, 0, :], zero[:, 1:2], None, ALU.subtract))
            link(dve.reciprocal(st[:, 0, :], st[:, 0, :]))
            link(dve.tensor_scalar(st[:, 0, :], st[:, 0, :], 1.0 - 0.8, None, ALU.mult))
            link(dve.tensor_tensor(att, att, bc(st[:, 0, :], D), ALU.mult))
            marks["mixed"] = link(dve.scalar_tensor_tensor(out=att, in0=FA[:, :, 0:D], scalar=0.8, in1=att, op0=ALU.mult, op1=ALU.add))
            dve.wait_ge(squared, 1)
            marks["length"] = link(dve.tensor_reduce(st[:, 0, :], sq, AX.X, ALU.add))
            dve.wait_ge(rooted, 1)
            link(dve.tensor_scalar(st[:, 1, :], st[:, 0, :], 1e-12, None, ALU.max))
            link(dve.reciprocal(st[:, 0, :], st[:, 1, :]))
            link(dve.tensor_tensor(att, att, bc(st[:, 0, :], D), ALU.mult))
            link(dve.tensor_tensor(H[:, :, :], H[:, :, :], att, ALU.add))

        @block.scalar
        def _(act):
            act.wait_ge(step, marks["zero"])
            act.activation(zero[:, 1:2], zero[:, 0:1], ACT.Exp).then_inc(weighed, 1)
            act.wait_ge(step, marks["mixed"])
            act.activation(sq, OA[:, :, 0:D], ACT.Square).then_inc(squared, 1)
            act.wait_ge(step, marks["length"])
            act.activation(st[:, 0, :], st[:, 0, :], ACT.Sqrt, bias=zero[:, 0:1]).then_inc(rooted, 1)


def route(nc, name, LG, tpr, coef, top, bias=None):
    t = lambda n: tpr[:, TPR[n][0]:sum(TPR[n])]
    with ExitStack() as ctx:
        sb = lambda n, shape: ctx.enter_context(nc.sbuf_tensor(name + n, shape, F32))
        sem = lambda n: ctx.enter_context(nc.semaphore(name + n))
        PR, A, S1, S2 = (sb(n, [P, NT, EXPERTS]) for n in ("_prob", "_a", "_first", "_second"))
        st = sb("_stat", [P, NT])
        step, powered, counted = sem("_step"), sem("_powered"), sem("_counted")
        ps = ctx.enter_context(nc.psum_tensor(name + "_ps", [P, 4, CHUNK], F32))
        block = ctx.enter_context(nc.Block())
        marks = {}
        HALF = NT // 2 * EXPERTS
        rank = t("rank").unsqueeze(1).broadcast_to([P, NT, EXPERTS])

        @block.vector
        def _(dve):
            link = chain_of(dve, step)
            tt = lambda out, a, b, op: link(dve.tensor_tensor(out, a, b, op))
            lg = LG[:, :, 0:EXPERTS]
            pr, a, s1, s2 = (x[:, :, :] for x in (PR, A, S1, S2))
            if bias is not None:
                tt(lg, lg, t(bias).unsqueeze(1).broadcast_to([P, NT, EXPERTS]), ALU.add)
            link(dve.tensor_reduce(st[:, :], lg, AX.X, ALU.max))
            marks["shifted"] = tt(pr, lg, bc(st[:, :], EXPERTS), ALU.subtract)
            dve.wait_ge(powered, 1)
            link(dve.tensor_reduce(st[:, :], pr, AX.X, ALU.add))
            link(dve.reciprocal(st[:, :], st[:, :]))
            tt(pr, pr, bc(st[:, :], EXPERTS), ALU.mult)

            def pick(src, one_hot):
                link(dve.tensor_reduce(st[:, :], src, AX.X, ALU.max))
                tt(a, src, bc(st[:, :], EXPERTS), ALU.is_equal)
                tt(a, a, rank, ALU.mult)
                link(dve.tensor_reduce(st[:, :], a, AX.X, ALU.max))
                tt(one_hot, a, bc(st[:, :], EXPERTS), ALU.is_equal)

            pick(pr, s1)
            c = coef[:, :, :]
            if top == 2:
                link(dve.scalar_tensor_tensor(out=s2, in0=s1, scalar=-2.0, in1=pr, op0=ALU.mult, op1=ALU.add))
                pick(s2, c)
                tt(s1, s1, c, ALU.add)
                tt(c, s1, pr, ALU.mult)
                link(dve.tensor_reduce(st[:, :], c, AX.X, ALU.add))
                link(dve.tensor_scalar(st[:, :], st[:, :], 1e-12, None, ALU.max))
                link(dve.reciprocal(st[:, :], st[:, :]))
                tt(c, c, bc(st[:, :], EXPERTS), ALU.mult)
            else:
                marks["picked"] = tt(c, s1, pr, ALU.mult)
                dve.wait_ge(counted, 1)
                halves = lambda x: x.rearrange("p (h t) e -> p h (t e)", h=2)
                link(dve.tensor_copy(halves(s2), ps[:, 2:4, 0:HALF]))
                for e in range(EXPERTS):
                    last = dve.tensor_tensor_scan(a[:, :, e], s2[:, :, e], s2[:, :, e], 0.0, ALU.add, ALU.bypass)
                link(last)
                tt(a, a, s2, ALU.subtract)
                link(dve.tensor_tensor(halves(s2), ps[:, 0:2, 0:HALF], halves(a), ALU.add))
                link(dve.tensor_scalar(s2, s2, CAP + 0.5, None, ALU.is_lt))
                tt(c, c, s2, ALU.mult)

        @block.scalar
        def _(act):
            act.wait_ge(step, marks["shifted"])
            act.activation(PR[:, :, :], PR[:, :, :], ACT.Exp).then_inc(powered, 1)

        @block.tensor
        def _(pe):
            if top == 1:
                pe.wait_ge(step, marks["picked"])
                for h in range(2):
                    rows = S1[:, NT // 2 * h:NT // 2 * (h + 1), :].rearrange("p t e -> p (t e)")
                    pe.matmul(ps[:, h, 0:HALF], t("tri"), rows, start=True, stop=True)
                    mm = pe.matmul(ps[:, 2 + h, 0:HALF], t("ones"), rows, start=True, stop=True)
                mm.then_inc(counted, 1)


def experts(nc, name, XP, tpr, w, onesb, coef, YO, kt, func):
    pre = name[0]
    at = lambda n: TPR[pre + "_" + n][0]
    b1 = tpr[:, at("b1"):at("b1") + kt]
    wide = TPR[pre + "_w2"][1] // kt
    per = max(1, kt * wide // (EXPERTS * D))
    WH, WM, WC = w
    with ExitStack() as ctx:
        sb = lambda n, shape, dt=F32: ctx.enter_context(nc.sbuf_tensor(name + n, shape, dt))
        sem = lambda n: ctx.enter_context(nc.semaphore(name + n))
        G = 4
        AHEAD = 3
        HF = sb("_hidden", [P, G, CHUNK])
        HB = sb("_hidden_parts", [P, G, 2, CHUNK], BF16)
        prod = sb("_prod", [P, 2, EXPERTS * D])
        ps = ctx.enter_context(nc.psum_tensor(name + "_ps", [P, 8, CHUNK], F32))
        hidden_mm, hidden, high, split, used, scaled, reduced = (sem("_" + n) for n in (
            "hidden_mm", "hidden", "high", "split", "used", "scaled", "reduced"))
        block = ctx.enter_context(nc.Block())

        @block.tensor
        def _(pe):
            def first_layer(c, k):
                if not (isinstance(c, int) and c * kt + k < G):
                    pe.wait_ge(hidden, 1 + c * kt + k - G + 1)
                cols = slice(at("w1") + P * k, at("w1") + P * k + P)
                for n, (wt, part) in enumerate(((WH, 0), (WM, 0), (WC, 1))):
                    mm = pe.matmul(ps[:, k % G, :], wt[:, cols], XP[:, part, bass.ds(c * CHUNK, CHUNK)], start=(n == 0), stop=(n == 2))
                mm.then_inc(hidden_mm, 1)

            def second_layer(c, k):
                if k == 0:
                    pe.wait_ge(scaled, 1 + c * 4)
                pe.wait_ge(split, 1 + c * kt + k + 1)
                g = k // per
                for j in range(4):
                    out = ps[:, 4 + j, wide * g:wide * g + wide]
                    if k % per == 0:
                        pe.matmul(out, onesb, WH[:, at("b2") + wide * g:at("b2") + wide * g + wide], start=True, stop=False)
                    w2 = slice(at("w2") + wide * k, at("w2") + wide * k + wide)
                    for part in range(2):
                        for wt in (WH, WM):
                            mm = pe.matmul(out, HB[:, k % G, part, P * j:P * j + P], wt[:, w2], start=False,
                                           stop=(k % per == per - 1 and part == 1 and wt is WM))
                mm.then_inc(used, 1)

            def chunk(c, last):
                for k in range(kt):
                    if k + AHEAD < kt:
                        first_layer(c, k + AHEAD)
                    elif not last:
                        first_layer(c + 1, k + AHEAD - kt)
                    second_layer(c, k)

            for k in range(AHEAD):
                first_layer(0, k)
            with pe.Fori(0, TC - 1) as c:
                chunk(c, False)
            chunk(TC - 1, True)

        @block.scalar
        def _(act):
            start_at_one(act, hidden)
            with act.Fori(0, TC) as c:
                for k in range(kt):
                    act.wait_ge(hidden_mm, c * kt + k + 1)
                    if k >= G:
                        act.wait_ge(split, 1 + c * kt + k - G + 1)
                    else:
                        act.wait_ge(split, 1 + c * kt)
                    act.activation(HF[:, k % G, :], ps[:, k % G, :], func, bias=b1[:, k:k + 1]).then_inc(hidden, 1)

        @block.vector
        def _(dve):
            start_at_one(dve, scaled, split)
            def parts(c, k):
                dve.wait_ge(hidden, 1 + c * kt + k + 1)
                if not (isinstance(c, int) and c * kt + k < G):
                    dve.wait_ge(used, c * kt + k - G + 1)
                dve.tensor_copy(HB[:, k % G, 0, :], HF[:, k % G, :]).then_inc(high, 1)
                dve.wait_ge(high, c * kt + k + 1)
                dve.tensor_tensor(HB[:, k % G, 1, :], HF[:, k % G, :], HB[:, k % G, 0, :], ALU.subtract).then_inc(split, 1)

            def combine(c, j):
                n = c * 4 + j
                if j == 0:
                    dve.wait_ge(used, (c + 1) * kt)
                dve.tensor_tensor(prod[:, j % 2, :].rearrange("p (e d) -> p e d", d=D), ps[:, 4 + j, :].rearrange("p (e d) -> p e d", d=D),
                                  coef[:, bass.ds(n, 1), :].rearrange("p a e -> p (a e)").unsqueeze(2).broadcast_to([P, EXPERTS, D]), ALU.mult).then_inc(scaled, 1)
                dve.wait_ge(scaled, 1 + n + 1)
                dve.tensor_reduce(YO[:, bass.ds(n, 1), 0:D].rearrange("p a d -> p (a d)"),
                                  prod[:, j % 2, :].rearrange("p (e d) -> p d e", d=D), AX.X, ALU.add).then_inc(reduced, 1)

            def chunk(c, last):
                for k in range(2, kt):
                    parts(c, k)
                if not last:
                    for k in range(2):
                        parts(c + 1, k)
                for j in range(4):
                    combine(c, j)

            for k in range(2):
                parts(0, k)
            chunk(0, False)
            with dve.Fori(1, TC - 1) as c:
                chunk(c, False)
            chunk(TC - 1, True)


def add_to(nc, name, H, parts, guard=False, bias=None):
    with ExitStack() as ctx:
        step = ctx.enter_context(nc.semaphore(name + "_step"))
        mask = ctx.enter_context(nc.sbuf_tensor(name + "_mask", [P, NT, D], mybir.dt.uint8)) if guard else None
        fill = ctx.enter_context(nc.sbuf_tensor(name + "_fill", [P, 3], F32)) if guard else None
        block = ctx.enter_context(nc.Block())

        @block.vector
        def _(dve):
            link = chain_of(dve, step)
            if guard:
                y = parts[0]
                top = float(np.finfo(np.float32).max)
                for n, (value, test) in enumerate(((0.0, None), (10000.0, ALU.is_gt), (-10000.0, ALU.is_lt))):
                    link(dve.memset(fill[:, n:n + 1], value))
                    if test is None:
                        link(dve.tensor_tensor(mask[:, :, :], y, y, ALU.not_equal))
                    else:
                        link(dve.tensor_scalar(mask[:, :, :], y, top if value > 0 else -top, None, test))
                    link(dve.copy_predicated(y, mask[:, :, :], fill[:, n:n + 1].unsqueeze(2).broadcast_to([P, NT, D])))
            if bias is not None:
                link(dve.tensor_tensor(H[:, :, :], H[:, :, :], bias.unsqueeze(1).broadcast_to([P, NT, D]), ALU.add))
            for part in parts:
                link(dve.tensor_tensor(H[:, :, :], H[:, :, :], part, ALU.add))


def head_attention(nc, XP, tpr, w, att):
    t = lambda n: tpr[:, TPR[n][0]:sum(TPR[n])]
    with ExitStack() as ctx:
        sb = lambda n, shape, dt=F32: ctx.enter_context(nc.sbuf_tensor("mha_" + n, shape, dt))
        sem = lambda n: ctx.enter_context(nc.semaphore("mha_" + n))
        QZ = sb("q", [P, 2, HEADS, SEQ])
        K = sb("k", [P, 2, SEQ])
        V = sb("v", [Q_ROWS, 2, 2, HEADS, HD + 1])
        VR = sb("v_raw", [Q_ROWS, 2, 2, D])
        S = sb("s", [Q_ROWS, 2, 2 * HEADS, SEQ])
        PT = sb("pt", [Q_ROWS, 2, 2, HEADS * Q_ROWS])
        mx = sb("mx", [Q_ROWS, 2 * HEADS])
        rc = sb("rc", [Q_ROWS, 2 * HEADS])
        OB = sb("ob", [Q_ROWS, 2 * HEADS, HD], BF16)
        OF = sb("of", [Q_ROWS, 2, 2, D])
        ps = ctx.enter_context(nc.psum_tensor("mha_ps", [P, 8, CHUNK], F32))
        (set_up, qkv_mm, qk_kept, qkv_kept, v_kept, scored_0, scored_1, maxed, shifted_0, shifted_1, weighed, turned_0, turned_1, pt_kept_0, pt_kept_1, mixed, inverted,
         rounded, widened, sent_even, sent_odd) = (sem(n) for n in (
             "set_up qkv_mm qk_kept qkv_kept v_kept scored_0 scored_1 maxed shifted_0 shifted_1 weighed turned_0 turned_1 pt_kept_0 pt_kept_1 mixed inverted "
             "rounded widened sent_even sent_odd").split())
        scored, shifted, sent = (scored_0, scored_1), (shifted_0, shifted_1), (sent_even, sent_odd)
        block = ctx.enter_context(nc.Block())
        rows = att.rearrange("(b s) d -> b s d", s=SEQ)
        V_AT = CHUNK - 2 * D
        sv = ps[0:Q_ROWS, 0:4, 0:2 * SEQ].rearrange("p h (n m) -> p h n m", n=2)
        ov = ps[0:Q_ROWS, 7, 0:2 * HEADS * (HD + 1)].rearrange("p (n f) -> p n f", f=HD + 1)
        late = lambda b, n: not isinstance(b, int) or b >= n
        FIRST = 4

        @block.tensor
        def _(pe):
            terms = [(w[0], 0), (w[1], 0), (w[2], 1)]

            def project(b):
                if late(b, 1):
                    pe.wait_ge(qkv_kept, b)
                for name, at in (("wq", 0), ("wk", SEQ)):
                    cols = slice(TPR[name][0], sum(TPR[name]))
                    for n, (wt, part) in enumerate(terms):
                        pe.matmul(ps[:, 6, at:at + SEQ], wt[:, cols], XP[:, part, bass.ds(b * SEQ, SEQ)], start=(n == 0), stop=(n == 2))
                cols = slice(TPR["wv"][0], sum(TPR["wv"]))
                for m in range(2):
                    at = V_AT + D * m
                    for n, (wt, part) in enumerate(terms):
                        mm = pe.matmul(ps[0:M_ROWS[m], 6, at:at + D], XP[:, part, bass.ds(b * SEQ + Q_ROWS * m, M_ROWS[m])], wt[:, cols], start=(n == 0), stop=(n == 2))
                mm.then_inc(qkv_mm, 1)

            def score(b, slot, part):
                if part == 0:
                    pe.wait_ge(qk_kept, b + 1)
                if late(b, 1):
                    pe.wait_ge(shifted[part], b)
                for h in range(2 * part, 2 * part + 2):
                    for n in range(2):
                        q0 = (SEQ - Q_ROWS) * n
                        mm = pe.matmul(ps[0:Q_ROWS, h, SEQ * n:SEQ * n + SEQ], QZ[:, slot, h, q0:q0 + Q_ROWS], K[:, slot, :], start=True, stop=True)
                mm.then_inc(scored[part], 1)

            def turn(b, slot, m):
                if m == 0:
                    pe.wait_ge(weighed, b + 1)
                    if late(b, 1):
                        pe.wait_ge(pt_kept_1, b)
                else:
                    pe.wait_ge(pt_kept_0, b + 1)
                for n in range(2):
                    for h in range(HEADS):
                        mm = pe.transpose(ps[0:M_ROWS[m], 4 + n, Q_ROWS * h:Q_ROWS * h + Q_ROWS],
                                          S[:, slot, 2 * h + n, Q_ROWS * m:Q_ROWS * m + M_ROWS[m]], t("eye")[0:Q_ROWS, 0:Q_ROWS])
                mm.then_inc(turned_1 if m else turned_0, 1)

            def mix(b, slot):
                pe.wait_ge(pt_kept_1, b + 1)
                pe.wait_ge(v_kept, b + 1)
                if late(b, 1):
                    pe.wait_ge(rounded, b)
                for n in range(2):
                    for h in range(HEADS):
                        for m in range(2):
                            mm = pe.matmul(ov[:, HEADS * n + h, :], PT[0:M_ROWS[m], m, n, Q_ROWS * h:Q_ROWS * h + Q_ROWS], V[0:M_ROWS[m], slot, m, h, :],
                                           start=(m == 0), stop=(m == 1))
                mm.then_inc(mixed, 1)

            def step(b, slot, more=True):
                score(b, slot, 0)
                turn(b - 1, 1 - slot, 0)
                score(b, slot, 1)
                turn(b - 1, 1 - slot, 1)
                if more:
                    project(b + 2)
                mix(b - 1, 1 - slot)

            pe.wait_ge(set_up, 1)
            project(0)
            project(1)
            score(0, 0, 0)
            score(0, 0, 1)
            project(2)
            for b in range(1, FIRST):
                step(b, b % 2)
            with pe.Fori(0, (BATCH - 2 - FIRST) // 2) as i:
                for s in range(2):
                    step(2 * i + FIRST + s, (FIRST + s) % 2)
            for b in range(BATCH - 2, BATCH):
                step(b, b % 2, False)
            last = BATCH - 1
            turn(last, last % 2, 0)
            turn(last, last % 2, 1)
            mix(last, last % 2)

        @block.scalar
        def _(act):
            def keep_qkv(b, slot):
                act.wait_ge(qkv_mm, b + 1)
                if late(b, 2):
                    act.wait_ge(scored_1, b - 1)
                for h in range(HEADS):
                    r = slice(32 * h, 32 * h + 32)
                    act.activation(QZ[r, slot, h, :], ps[r, 6, 0:SEQ], ACT.Identity, bias=t("wq_b")[r, :])
                act.activation(K[:, slot, :], ps[:, 6, SEQ:2 * SEQ], ACT.Identity, bias=t("wk_b")).then_inc(qk_kept, 1)
                if late(b, 2):
                    act.wait_ge(v_kept, b - 1)
                for m in range(2):
                    kept = act.copy(VR[0:M_ROWS[m], slot, m, :], ps[0:M_ROWS[m], 6, V_AT + D * m:V_AT + D * m + D])
                kept.then_inc(qkv_kept, 1)

            def keep_turned(b):
                act.wait_ge(turned_0, b + 1)
                act.copy(PT[0:M_ROWS[0], 0, :, :], ps[0:M_ROWS[0], 4:6, 0:HEADS * Q_ROWS]).then_inc(pt_kept_0, 1)

            def weigh(b, slot):
                act.wait_ge(shifted_0, b + 1)
                act.wait_ge(shifted_1, b + 1)
                act.activation(S[:, slot, :, :], S[:, slot, :, :], ACT.Exp, scale=HD ** -0.5).then_inc(weighed, 1)

            def step(b, slot, more=True):
                keep_turned(b - 1)
                weigh(b, slot)
                if more:
                    keep_qkv(b + 2, slot)

            act.wait_ge(set_up, 1)
            keep_qkv(0, 0)
            keep_qkv(1, 1)
            weigh(0, 0)
            keep_qkv(2, 0)
            for b in range(1, FIRST):
                step(b, b % 2)
            with act.Fori(0, (BATCH - 2 - FIRST) // 2) as i:
                for s in range(2):
                    step(2 * i + FIRST + s, (FIRST + s) % 2)
            for b in range(BATCH - 2, BATCH):
                step(b, b % 2, False)
            keep_turned(BATCH - 1)

        @block.vector
        def _(dve):
            def keep_v(b, slot):
                dve.wait_ge(qkv_kept, b + 1)
                if late(b, 2):
                    dve.wait_ge(mixed, b - 1)
                for m in range(2):
                    kept = dve.tensor_tensor(V[0:M_ROWS[m], slot, m, :, 0:HD], VR[0:M_ROWS[m], slot, m, :].rearrange("p (h f) -> p h f", f=HD),
                                             t("wv_b")[0:M_ROWS[m], :].rearrange("p (h f) -> p h f", f=HD), ALU.add)
                kept.then_inc(v_kept, 1)

            def shift(b, slot, part):
                heads = slice(2 * part, 2 * part + 2)
                top = mx[:, :].rearrange("p (h n) -> p h n", n=2)[:, heads, :]
                dve.wait_ge(scored[part], b + 1)
                dve.tensor_reduce(top, sv[:, heads, :, :], AX.X, ALU.max).then_inc(maxed, 1)
                dve.wait_ge(maxed, 2 * b + part + 1)
                dve.tensor_tensor(S[:, slot, :, :].rearrange("p (h n) m -> p h n m", n=2)[:, heads, :, :], sv[:, heads, :, :],
                                  top.unsqueeze(3).broadcast_to([Q_ROWS, 2, 2, SEQ]), ALU.subtract).then_inc(shifted[part], 1)

            def keep_turned(b):
                dve.wait_ge(turned_1, b + 1)
                dve.tensor_copy(PT[0:M_ROWS[1], 1, :, :], ps[0:M_ROWS[1], 4:6, 0:HEADS * Q_ROWS]).then_inc(pt_kept_1, 1)

            def results(b, slot, pair):
                dve.wait_ge(mixed, b + 1)
                dve.reciprocal(rc[:, :].unsqueeze(2), ov[:, :, HD:HD + 1]).then_inc(inverted, 1)
                dve.wait_ge(inverted, b + 1)
                dve.tensor_tensor(OB[:, :, :], ov[:, :, 0:HD], bc(rc[:, :], HD), ALU.mult).then_inc(rounded, 1)
                dve.wait_ge(rounded, b + 1)
                if late(b, 2):
                    dve.wait_ge(sent[slot], pair * 32)
                dve.tensor_copy(OF[:, slot, :, :].rearrange("p n d -> p (n d)"), OB[:, :, :].rearrange("p n f -> p (n f)")).then_inc(widened, 1)

            def step(b, slot, pair_before, more=True):
                shift(b, slot, 0)
                keep_turned(b - 1)
                shift(b, slot, 1)
                results(b - 1, 1 - slot, pair_before)
                if more:
                    keep_v(b + 1, 1 - slot)

            dve.memset(QZ[:, :, :, :], 0.0)
            dve.memset(V[:, :, :, :, :], 1.0).then_inc(set_up, 1)
            dve.wait_ge(set_up, 1)
            keep_v(0, 0)
            shift(0, 0, 0)
            shift(0, 0, 1)
            keep_v(1, 1)
            for b in range(1, FIRST):
                step(b, b % 2, (b - 1) // 2)
            with dve.Fori(0, (BATCH - 2 - FIRST) // 2) as i:
                for s in range(2):
                    step(2 * i + FIRST + s, (FIRST + s) % 2, i + (FIRST - 1 + s) // 2)
            for b in range(BATCH - 2, BATCH):
                step(b, b % 2, (b - 1) // 2, b + 1 < BATCH)
            last = BATCH - 1
            keep_turned(last)
            results(last, last % 2, last // 2)

        @block.sync
        def _(sp):
            with sp.Fori(0, BATCH // 2) as i:
                for s in range(2):
                    b = 2 * i + s
                    sp.wait_ge(widened, b + 1)
                    row = rows[bass.ds(b, 1), :, :].rearrange("a s d -> (a s) d")
                    sp.dma_start(row[0:Q_ROWS, :], OF[:, s, 0, :]).then_inc(sent[s], 16)
                    sp.dma_start(row[Q_ROWS:SEQ, :], OF[1:Q_ROWS, s, 1, :]).then_inc(sent[s], 16)
            for s in range(2):
                sp.wait_ge(sent[s], 16 * BATCH)


def pair_tokens(nc, X, HML):
    with nc.Block() as block:
        @block.vector
        def _(dve):
            for half in range(2):
                dve.tensor_copy(HML[:, 0, :, D * half:D * half + D], X[:, :, :])


def token_stages(nc, din, hid, att, result, upto=9):
    with ExitStack() as ctx:
        sb = lambda n, shape, dt=F32: ctx.enter_context(nc.sbuf_tensor(n, shape, dt))
        tpr = sb("tpr", [P, TPR_W])
        w = [sb(n, [P, SPLIT_W], BF16) for n in ("w_high", "w_middle", "w_stack")]
        eyeb = sb("eye_ones", [P, 2, P], BF16)
        H = sb("H", [P, NT, D])
        X = sb("X", [P, NT, D])
        B = sb("B", [P, NT, D])
        HML = sb("HML", [P, 2, NT, P], BF16)
        XP = sb("XP", [P, 2, NT * P], BF16)
        LG = sb("logits", [P, NT, EXPERTS])
        coef = sb("coef", [P, NT, EXPERTS])
        SQ = B[:, :, :].rearrange("p t d -> p (t d)")
        ones = eyeb[:, 1, :]
        raw = HML[:, :, :, :].rearrange("p a t d -> p (a t d)").bitcast(F32)[:, 0:SPLIT_W]
        rest = XP[:, :, :].rearrange("p a n -> p (a n)").bitcast(F32)[:, 0:SPLIT_W]
        load_tokens(nc, "first", hid, H, [(tpr[:, :], din["tokprm"]), (raw, din["weights"])])
        split_weights(nc, raw, rest, tpr, *w, eyeb)
        if upto >= 1:
            with nc.sbuf_tensor("row_sums", [P, FULL_T + 1, TC], F32) as SUM:
                token_norm(nc, "n0", H, X, SQ, HML, unit=X)
                turn_tokens(nc, "t0", HML, eyeb, XP)
                global_attention(nc, HML, XP, B, tpr, SUM)
                blend(nc, H, X, B, HML[:, :, :, :].rearrange("p a t d -> p (a t d)").bitcast(F32)[:, 0:NT * D], SUM)
        if upto >= 2:
            token_norm(nc, "n1", H, X, SQ, HML)
            turn_tokens(nc, "t1", HML, eyeb, XP, w, "router", LG)
            route(nc, "r1", LG, tpr, coef, 2)
            experts(nc, "moe", XP, tpr, w, ones, coef, B, 4, ACT.Gelu)
            add_to(nc, "a1", H, [X[:, :, :], B[:, :, :]])
        if upto >= 3:
            token_norm(nc, "n2", H, X, SQ, HML, clip=10000.0)
            turn_tokens(nc, "t2", HML, eyeb, XP)
            head_attention(nc, XP, tpr, w, att)
            load_tokens(nc, "second", att, X)
            pair_tokens(nc, X, HML)
            turn_tokens(nc, "t3", HML, eyeb, XP, w, "wo", B, parts=1)
            add_to(nc, "a2", H, [B[:, :, :]], bias=tpr[:, TPR["wo_b"][0]:sum(TPR["wo_b"])])
        if upto >= 4:
            token_norm(nc, "n3", H, X, SQ, HML)
            turn_tokens(nc, "t4", HML, eyeb, XP, w, "gate", LG)
            route(nc, "r4", LG, tpr, coef, 1, "gate_b")
            experts(nc, "ffn", XP, tpr, w, ones, coef, B, 16, ACT.Relu)
            add_to(nc, "a3", H, [B[:, :, :]], guard=True)
        with nc.semaphore("result_stored") as stored, nc.Block() as block:
            @block.sync
            def _(sp):
                sp.dma_start(result[0:FULL_T * P, :].rearrange("(t p) d -> p t d", p=P), H[:, 0:FULL_T, :]).then_inc(stored, 16)
                sp.dma_start(result[FULL_T * P:TOK, :], H[0:REST, FULL_T, :]).then_inc(stored, 16)
                sp.wait_ge(stored, 32)


def program(nc, din, result):
    hid = nc.dram_tensor("hid", (TOK, D), F32, kind="Internal").ap()
    att = nc.dram_tensor("att", (TOK, D), F32, kind="Internal").ap()
    with ExitStack() as ctx:
        sb = lambda name, shape: ctx.enter_context(nc.sbuf_tensor(name, shape, F32))
        prm = sb("prm", [P, PRM_W])
        tab = sb("tab", [P, TABLES.shape[1]])
        fc0c = ctx.enter_context(nc.sbuf_tensor("fc0_parts", [P, P], BF16))
        fc1p = sb("fc1_padded", [P, TILE_IMG, P])
        operator_setup(nc, din, prm, tab, fc0c, fc1p)
        operator(nc, din, hid, prm, tab, fc0c, fc1p)
    token_stages(nc, din, hid, att, result)


def kernel(**inputs):
    import concourse.bacc as bacc
    from concourse.bass_utils import run_bass_kernel_spmd

    i = {k: np.asarray(v) for k, v in inputs.items()}
    host = {**layout_operator(i), **layout_tokens(i), "txt": i["txt"].reshape(BATCH, TXT * D)}
    nc = bacc.Bacc("TRN2", target_bir_lowering=False, num_devices=1)
    arrays = {f"in_{k}": np.ascontiguousarray(v) for k, v in host.items()}
    din = {k: nc.dram_tensor(f"in_{k}", v.shape, F32, kind="ExternalInput").ap() for k, v in host.items()}
    result = nc.dram_tensor("result", (TOK, D), F32, kind="ExternalOutput").ap()
    program(nc, din, result)
    r = run_bass_kernel_spmd(nc, [arrays], core_ids=[0])
    return r.results[0]["result"].reshape(BATCH, SEQ, D)
```
